# Optimizing a Trainium2 kernel written in Bass

```python
import numpy as np
import jax
import jax.numpy as jnp

def _softmax(x, axis=-1):
    return jax.nn.softmax(x, axis=axis)

def _gelu(x):
    return jax.nn.gelu(x, approximate=True)

def _silu(x):
    return jax.nn.silu(x)

def _sigmoid(x):
    return jax.nn.sigmoid(x)

def _layernorm(x, axis=-1, eps=1e-05):
    m = jnp.mean(x, axis=axis, keepdims=True)
    v = jnp.var(x, axis=axis, keepdims=True)
    return (x - m) / jnp.sqrt(v + eps)

def _scatter_add(tgt, idx, src, axis=0):
    return tgt.at[idx].add(src)

def _segment_sum(src, seg, n):
    return jax.ops.segment_sum(src, seg, n)
kernel_name = 'mk_audio_tower_d1_tok_audfeat1024_r4_69e794'

def setup_inputs(seed: int=0):
    np.random.seed(seed)
    _w = jnp.asarray

    def _rec_inputs():
        import jax
        import jax.numpy as jnp
        _rk = jax.random.key(seed)
        x = 0.00021031 + 1.00007 * jax.random.normal(jax.random.fold_in(_rk, 1), (32, 750, 256), jnp.float32)
        return x
    x = _rec_inputs()

    def _L0_tok_setup():
        import jax, jax.numpy as jnp
        import numpy as np
        DB4_DEC_LO = np.array([-0.010597401784997278, 0.032883011666982945, 0.030841381835986965, -0.18703481171888114, -0.02798376941698385, 0.6308807679295904, 0.7148465705525415, 0.23037781330885523], dtype=np.float64)
        NUM_LEVELS = 2

        def _afb1d_low(y, h0):
            B, D, N = y.shape
            L = h0.shape[0]
            outsize = (N + L - 1) // 2
            p = 2 * (outsize - 1) - N + L
            yp = jnp.pad(y, ((0, 0), (0, 0), (p // 2, p - p // 2)))
            k = jnp.broadcast_to(h0[None, None, :], (D, 1, L))
            return jax.lax.conv_general_dilated(yp, k, window_strides=(2,), padding='VALID', dimension_numbers=('NCH', 'OIH', 'NCH'), feature_group_count=D)
        key = jax.random.key(seed)
        x = jax.random.normal(key, (8, 1024, 256), dtype=jnp.float32)
        h0 = jnp.asarray(DB4_DEC_LO[::-1].copy(), dtype=jnp.float32)
        return {'x': x, 'h0': h0}
    _L0_tok_all = _L0_tok_setup()
    _L0_tok_in = {k: v for k, v in _L0_tok_all.items() if k in ('h0',)}
    del _L0_tok_all

    def _L0_attn_setup():
        import jax, jax.numpy as jnp
        import numpy as np
        import math
        NEG_INF = -1e+38

        def wkv_scan(w, u, k, v):
            B, T, C = k.shape

            def step(carry, kv_t):
                a, b, pp = carry
                kt, vt = kv_t
                ww = u + kt
                q = jnp.maximum(pp, ww)
                e1 = jnp.exp(pp - q)
                e2 = jnp.exp(ww - q)
                y = (e1 * a + e2 * vt) / (e1 * b + e2)
                ww2 = pp + w
                q2 = jnp.maximum(ww2, kt)
                e1b = jnp.exp(ww2 - q2)
                e2b = jnp.exp(kt - q2)
                return ((e1b * a + e2b * vt, e1b * b + e2b, q2), y)
            init = (jnp.zeros((B, C), k.dtype), jnp.zeros((B, C), k.dtype), jnp.full((B, C), NEG_INF, k.dtype))
            kT = jnp.swapaxes(k, 0, 1)
            vT = jnp.swapaxes(v, 0, 1)
            _, ys = jax.lax.scan(step, init, (kT, vT))
            return jnp.swapaxes(ys, 0, 1)
        key = jax.random.key(seed)
        B, T, C = (16, 256, 256)
        k1, k2, k3, k4 = jax.random.split(key, 4)
        x = jax.random.normal(k1, (B, T, C), dtype=jnp.float32)
        scale = 0.02
        Wk = jax.random.normal(k2, (C, C), dtype=jnp.float32) * scale
        Wr = jax.random.normal(k3, (C, C), dtype=jnp.float32) * scale
        Wo = jax.random.normal(k4, (C, C), dtype=jnp.float32) * scale
        h = np.arange(C, dtype=np.float64)
        decay_speed = -5.0 + 8.0 * (h / (C - 1)) ** (0.7 + 1.3 * 1)
        zigzag = ((np.arange(C) + 1) % 3 - 1) * 0.5
        time_first = np.ones(C) * math.log(0.3) + zigzag
        return {'x': x, 'Wk': Wk, 'Wr': Wr, 'Wo': Wo, 'time_decay': jnp.asarray(decay_speed, dtype=jnp.float32), 'time_first': jnp.asarray(time_first, dtype=jnp.float32)}
    _L0_attn_all = _L0_attn_setup()
    _L0_attn_in = {k: v for k, v in _L0_attn_all.items() if k in ('Wk', 'Wr', 'Wo', 'time_decay', 'time_first')}
    del _L0_attn_all

    def _L0_ffn_setup():
        import jax, jax.numpy as jnp
        import numpy as np
        D_MODEL = 256
        D_FF = 1024
        NUM_EXPERTS = 8
        TOP_K = 2
        BATCH = 4
        SEQ = 512
        key = jax.random.key(seed)
        ks = jax.random.split(key, 8)
        s = 0.02
        x = jax.random.normal(ks[0], (BATCH, SEQ, D_MODEL), dtype=jnp.float32)
        router_w = jax.random.normal(ks[1], (D_MODEL, NUM_EXPERTS), dtype=jnp.float32) * s
        router_b = jnp.zeros((NUM_EXPERTS,), dtype=jnp.float32)
        W1 = jax.random.normal(ks[2], (NUM_EXPERTS, D_MODEL, D_FF), dtype=jnp.float32) * s
        b1 = jnp.zeros((NUM_EXPERTS, D_FF), dtype=jnp.float32)
        W2 = jax.random.normal(ks[3], (NUM_EXPERTS, D_FF, D_MODEL), dtype=jnp.float32) * s
        b2 = jnp.zeros((NUM_EXPERTS, D_MODEL), dtype=jnp.float32)
        return {'x': x, 'router_w': router_w, 'router_b': router_b, 'W1': W1, 'b1': b1, 'W2': W2, 'b2': b2}
    _L0_ffn_all = _L0_ffn_setup()
    _L0_ffn_in = {k: v for k, v in _L0_ffn_all.items() if k in ('router_w', 'router_b', 'W1', 'b1', 'W2', 'b2')}
    del _L0_ffn_all
    return {'x': x, 'L0_tok_h0': _L0_tok_in['h0'], 'L0_attn_Wk': _L0_attn_in['Wk'], 'L0_attn_Wr': _L0_attn_in['Wr'], 'L0_attn_Wo': _L0_attn_in['Wo'], 'L0_attn_time_decay': _L0_attn_in['time_decay'], 'L0_attn_time_first': _L0_attn_in['time_first'], 'L0_ffn_router_w': _L0_ffn_in['router_w'], 'L0_ffn_router_b': _L0_ffn_in['router_b'], 'L0_ffn_W1': _L0_ffn_in['W1'], 'L0_ffn_b1': _L0_ffn_in['b1'], 'L0_ffn_W2': _L0_ffn_in['W2'], 'L0_ffn_b2': _L0_ffn_in['b2']}

def reference(x, L0_tok_h0, L0_attn_Wk, L0_attn_Wr, L0_attn_Wo, L0_attn_time_decay, L0_attn_time_first, L0_ffn_router_w, L0_ffn_router_b, L0_ffn_W1, L0_ffn_b1, L0_ffn_W2, L0_ffn_b2):
    import jax
    import jax.numpy as jnp

    def _L0_tok_ref(x, h0):
        import jax, jax.numpy as jnp
        import numpy as np
        DB4_DEC_LO = np.array([-0.010597401784997278, 0.032883011666982945, 0.030841381835986965, -0.18703481171888114, -0.02798376941698385, 0.6308807679295904, 0.7148465705525415, 0.23037781330885523], dtype=np.float64)
        NUM_LEVELS = 2

        def _afb1d_low(y, h0):
            B, D, N = y.shape
            L = h0.shape[0]
            outsize = (N + L - 1) // 2
            p = 2 * (outsize - 1) - N + L
            yp = jnp.pad(y, ((0, 0), (0, 0), (p // 2, p - p // 2)))
            k = jnp.broadcast_to(h0[None, None, :], (D, 1, L))
            return jax.lax.conv_general_dilated(yp, k, window_strides=(2,), padding='VALID', dimension_numbers=('NCH', 'OIH', 'NCH'), feature_group_count=D)
        y = jnp.swapaxes(x, 1, 2)
        for _ in range(NUM_LEVELS):
            y = _afb1d_low(y, h0)
        return jnp.swapaxes(y, 1, 2)

    def _L0_attn_ref(x, Wk, Wr, Wo, time_decay, time_first):
        import jax, jax.numpy as jnp
        import numpy as np
        import math
        NEG_INF = -1e+38

        def wkv_scan(w, u, k, v):
            B, T, C = k.shape

            def step(carry, kv_t):
                a, b, pp = carry
                kt, vt = kv_t
                ww = u + kt
                q = jnp.maximum(pp, ww)
                e1 = jnp.exp(pp - q)
                e2 = jnp.exp(ww - q)
                y = (e1 * a + e2 * vt) / (e1 * b + e2)
                ww2 = pp + w
                q2 = jnp.maximum(ww2, kt)
                e1b = jnp.exp(ww2 - q2)
                e2b = jnp.exp(kt - q2)
                return ((e1b * a + e2b * vt, e1b * b + e2b, q2), y)
            init = (jnp.zeros((B, C), k.dtype), jnp.zeros((B, C), k.dtype), jnp.full((B, C), NEG_INF, k.dtype))
            kT = jnp.swapaxes(k, 0, 1)
            vT = jnp.swapaxes(v, 0, 1)
            _, ys = jax.lax.scan(step, init, (kT, vT))
            return jnp.swapaxes(ys, 0, 1)
        k = jnp.einsum('btc,hc->bth', x, Wk)
        r = jnp.einsum('btc,hc->bth', x, Wr)
        v = r
        w = -jnp.exp(time_decay)
        y = wkv_scan(w, time_first, k, v)
        out = jax.nn.sigmoid(r) * y
        return jnp.einsum('bth,ch->btc', out, Wo)

    def _L0_ffn_ref(x, router_w, router_b, W1, b1, W2, b2):
        import jax, jax.numpy as jnp
        import numpy as np
        D_MODEL = 256
        D_FF = 1024
        NUM_EXPERTS = 8
        TOP_K = 2
        BATCH = 4
        SEQ = 512
        logits = jnp.einsum('bsd,de->bse', x, router_w) + router_b
        topk_scores, topk_idx = jax.lax.top_k(logits, TOP_K)
        topk_gates = jax.nn.softmax(topk_scores, axis=-1)
        onehot = jax.nn.one_hot(topk_idx, NUM_EXPERTS, dtype=x.dtype)
        combine = jnp.einsum('bsk,bske->bse', topk_gates, onehot)
        combine_e = jnp.moveaxis(combine, -1, 0)

        def expert_step(acc, params):
            w1, bb1, w2, bb2, c = params
            h = jax.nn.relu(jnp.einsum('bsd,df->bsf', x, w1) + bb1)
            y = jnp.einsum('bsf,fd->bsd', h, w2) + bb2
            return (acc + y * c[..., None], None)
        out, _ = jax.lax.scan(expert_step, jnp.zeros_like(x), (W1, b1, W2, b2, combine_e))
        return out
    h = _L0_tok_ref(x, L0_tok_h0)
    h = h + _L0_attn_ref(_layernorm(h, axis=-1), L0_attn_Wk, L0_attn_Wr, L0_attn_Wo, L0_attn_time_decay, L0_attn_time_first)
    h = h + _L0_ffn_ref(_layernorm(h, axis=-1), L0_ffn_router_w, L0_ffn_router_b, L0_ffn_W1, L0_ffn_b1, L0_ffn_W2, L0_ffn_b2)
    return h

_drawn_inputs = setup_inputs


def setup_inputs(seed=0):
    import zlib

    import numpy as np

    out = dict(_drawn_inputs(seed))
    spreads = {'L0_ffn_router_b': (0.0, 0.1), 'L0_ffn_b1': (0.0, 0.1), 'L0_ffn_b2': (0.0, 0.1)}
    factors = {'L0_attn_Wk': 6.377, 'L0_attn_time_first': 61.648}
    for name, (base, spread) in spreads.items():
        noise = np.random.default_rng([zlib.crc32(name.encode()), seed]).standard_normal(out[name].shape)
        drawn = base * np.exp(spread * noise) if base else spread * noise
        out[name] = jnp.asarray(drawn.astype(out[name].dtype))
    for name, factor in factors.items():
        out[name] = (out[name] * factor).astype(out[name].dtype)
    return out
```

```python
from contextlib import ExitStack

import concourse.bass as bass
from concourse import mybir

ALU = mybir.AluOpType
ACT = mybir.ActivationFunctionType
F32 = mybir.dt.float32
F32R = mybir.dt.float32r
BF16 = mybir.dt.bfloat16
I32 = mybir.dt.int32
U32 = mybir.dt.uint32
AX = mybir.AxisListType

P = 128
B, T_IN, C = 32, 750, 256
TAPS = 8
T_MID = (T_IN + TAPS - 1) // 2
T = (T_MID + TAPS - 1) // 2
LEFT = TAPS - 2
NTOK = B * T
PAIRS = B // 2
HC = C // P
SEQ = 2 * HC
TP = T + 1
KI, NKI = 125, 6
KM, NKM = 126, 3
PAIR_TOK = 2 * T
REST = T - P
E, FF = 8, 1024
FC = FF // P
TS = 384
R = TS // P
NT = (2 * NTOK + E * (TS - 1)) // TS
MAXT = NTOK // TS
REG = NTOK + TS
ROW = C + 3
LIST = E * REG + TS
NOGRP = E * REG // R
WROW = 2 * FF + FC * C + FC
W2AT, B1AT = 2 * FF, 2 * FF + FC * C
NEG = -1e38
EPS = 1e-5
EMAX = 2.0 ** 54
BAND1, GAP, BAND2 = 2 * KM + LEFT, 126, KM // 2 + 3
AT1, AT2 = KI, KI + BAND1 + GAP
BANDS = AT2 + BAND2 + GAP


class Pair:

    def __init__(self, g, s):
        self.g, self.s = g, s

    def at(self, per_pair, more=0):
        return self.g * (2 * per_pair) + (per_pair * self.s + more)

    def slot_at(self, per_use, more=0):
        return self.g * per_use + more


def rounds(eng, body):
    body(Pair(0, 0), None, None)
    body(Pair(0, 1), Pair(0, 0), None)
    body(Pair(1, 0), Pair(0, 1), Pair(0, 0))
    body(Pair(1, 1), Pair(1, 0), Pair(0, 1))
    with eng.Fori(1, PAIRS // 2 - 1) as n:
        body(Pair(n + 1, 0), Pair(n, 1), Pair(n, 0))
        body(Pair(n + 1, 1), Pair(n + 1, 0), Pair(n, 1))
    last = PAIRS // 2 - 1
    body(None, Pair(last, 1), Pair(last, 0))
    body(None, None, Pair(last, 1))


def tokens_to_experts(nc, x, h0, wkT, wrT, woT, decay, first, rw, rb, out, rows, lists, ends):
    ctx = ExitStack()

    def sb(name, shape, dt=F32):
        return ctx.enter_context(nc.sbuf_tensor(name, shape, dt))

    def ps(name, n=1):
        return ctx.enter_context(nc.psum_tensor(name, [P, 512 * n], F32))

    def sem(name):
        return ctx.enter_context(nc.semaphore(name))

    with ctx:
        wk, wr, wo = sb("wk", [P, HC, C]), sb("wr", [P, HC, C]), sb("wo", [P, HC, C])
        rws, rbs = sb("rws", [P, HC, E]), sb("rbs", [P, E])
        taps = sb("taps", [P, TAPS])
        dec, u = sb("dec", [P, HC]), sb("u", [P, HC])
        w, uw = sb("w", [P, HC]), sb("uw", [P, HC])
        wseq = sb("wseq", [P, SEQ, TP])
        diag = sb("diag", [P, P], I32)
        bandi = sb("bandi", [P, BAND1 + GAP + BAND2], I32)
        band, btmp = sb("band", [P, BANDS]), sb("btmp", [P, BAND1 + GAP + BAND2])
        ident = sb("ident", [P, P])
        before, ones = sb("before", [P, P], BF16), sb("ones", [P, P], BF16)
        filt = sb("filt", [P, NKI, T])
        filt_rest = sb("filt_rest", [P, 3, 2, P])
        eid_i, eid = sb("eid_i", [P, E], I32), sb("eid", [P, E])
        reg_i = sb("reg_i", [P, E], I32)
        tok_i, tok = sb("tok_i", [P, 4], I32), sb("tok", [P, 3])
        c_eps, c_pow, c_neg = sb("c_eps", [P, 3]), sb("c_pow", [P, 3]), sb("c_neg", [P, 3])
        zrow, nobody = sb("zrow", [P, R * C]), sb("nobody", [P, LIST // P], U32)
        xin = sb("xin", [P, 2, 2, NKI, C])
        h = sb("h", [P, 2, 3, C])
        st1, st2 = sb("st1", [P, 3, 6]), sb("st2", [P, 3, 6])
        mv1, mv2 = sb("mv1", [P, 3, 2]), sb("mv2", [P, 3, 2])
        ve1, rs1, mr1, nb1 = (sb(n, [P, 3]) for n in ("ve1", "rs1", "mr1", "nb1"))
        ve2, rs2, mr2, nb2 = (sb(n, [P, 3]) for n in ("ve2", "rs2", "mr2", "nb2"))
        xn = sb("xn", [P, 3, C])
        xnT = sb("xnT", [P, HC, PAIR_TOK])
        kpad = sb("kpad", [P, SEQ, TP])
        v, er = sb("v", [P, 2, SEQ, T]), sb("er", [P, 2, SEQ * T])
        pp = sb("pp", [P, SEQ, TP])
        dl = sb("dl", [P, SEQ, T])
        up_s, dn_s, up_y, dn_y = (sb(n, [P, SEQ, T]) for n in ("up_s", "dn_s", "up_y", "dn_y"))
        e1s, e2s, e2sv = sb("e1s", [P, SEQ, TP]), sb("e2s", [P, SEQ, TP]), sb("e2sv", [P, SEQ, TP])
        e1y, e2y = sb("e1y", [P, SEQ, T]), sb("e2y", [P, SEQ, T])
        sa, sb_ = sb("sa", [P, SEQ, TP]), sb("sbb", [P, SEQ, TP])
        t1, t2, t3 = (sb(n, [P, SEQ, T]) for n in ("t1", "t2", "t3"))
        num, den, em, dsg = (sb(n, [P, SEQ * T]) for n in ("num", "den", "em", "dsg"))
        lnd, inv = sb("lnd", [P, SEQ * T]), sb("inv", [P, SEQ * T])
        oT = sb("oT", [P, HC, 3 * P])
        h1 = sb("h1", [P, 2, 3, C])
        xs = sb("xs", [P, 2, 3, ROW])
        x2T = sb("x2T", [P, HC, 3 * P])
        lg, eq, cand, oh1, lg2, cand2, oh2, place, pl1 = (
            sb(n, [P, 3, E]) for n in ("lg", "eq", "cand", "oh1", "lg2", "cand2", "oh2", "place", "pl1"))
        sel = sb("sel", [P, 3, E], BF16)
        m1, m2, i1, i2, dm, ed, ed1 = (sb(n, [P, 3]) for n in ("m1", "m2", "i1", "i2", "dm", "ed", "ed1"))
        slots, tid = sb("slots", [P, 2, 6], U32), sb("tid", [P, 2, 3], U32)

        conv_ps, wo_ps, kr_ps = ps("conv_ps", 2), ps("wo_ps", 2), [ps("kr_ps0"), ps("kr_ps1")]
        tp_ps, cnt_ps = ps("tp_ps"), ps("cnt_ps")
        lg_ps = cnt_ps[:, 0:24].rearrange("p (t e) -> p t e", e=E)
        rank_ps, tot_ps = cnt_ps[:, 32:56], cnt_ps[:, 64:72]

        params, loaded, tok_next = sem("params"), sem("loaded"), sem("tok_next")
        stats_seen, slots_seen, sp_seen = sem("stats_seen"), sem("slots_seen"), sem("sp_seen")
        iotas, consts, bands, filt_done, ready = sem("iotas"), sem("consts"), sem("bands"), sem("filt_done"), sem("ready")
        setup_act, pads = sem("setup_act"), sem("pads")
        x_loaded = [sem("x_loaded0"), sem("x_loaded1")]
        h1_stored = [sem("h1_stored0"), sem("h1_stored1")]
        rows_stored = [sem("rows_stored0"), sem("rows_stored1")]
        listed = [sem("listed0"), sem("listed1")]
        zeroed = sem("zeroed")
        conv_done, h_taken = sem("conv_done"), sem("h_taken")
        ln1, ln2 = sem("ln1"), sem("ln2")
        rstd1, rstd2 = sem("rstd1"), sem("rstd2")
        xn_ready, t1_done, t1_taken = sem("xn_ready"), sem("t1_done"), sem("t1_taken")
        kr_done, kr_taken, er_ready = sem("kr_done"), sem("kr_taken"), sem("er_ready")
        diffs, exps, state, t2_done, t3_done = sem("diffs"), sem("exps"), sem("state"), sem("t2_done"), sem("t3_done")
        inv_ready, o_ready, wo_done = sem("inv_ready"), sem("o_ready"), sem("wo_done")
        xn2_ready, t2T_done, t2T_taken = sem("xn2_ready"), sem("t2T_done"), sem("t2T_taken")
        lg_done, route, gate_exp, rank_done = sem("lg_done"), sem("route"), sem("gate_exp"), sem("rank_done")

        N_LN1, N_LN2, N_DIFF, N_STATE, N_ROUTE, N_RSTD = 6, 7, 9, 8, 25, 4

        block = ctx.enter_context(nc.Block())

        @block.sync
        def _(sp):
            sp.dma_start(taps[:, :], h0.rearrange("(a k) -> a k", a=1).partition_broadcast(P)).then_inc(params, 16)
            sp.dma_start(dec[:, :], decay).then_inc(params, 16)
            sp.dma_start(u[:, :], first).then_inc(params, 16)

            def end_of_waits():
                sp.sem_inc(sp_seen, 1)

            def load(q):
                if not isinstance(q.g, int) or q.g:
                    sp.wait_ge(conv_done, Pair(q.g - 1, q.s).at(1, 1))
                    end_of_waits()
                for b in range(2):
                    src = x[bass.ds(q.at(2, b), 1)].rearrange("a (s p) c -> (a p) s c", p=KI)
                    sp.dma_start(xin[0:KI, q.s, b], src).then_inc(x_loaded[q.s], 16)

            load(Pair(0, 0))
            for dst, src in ((wk, wkT), (wr, wrT), (wo, woT), (rws, rw)):
                sp.dma_start(dst[:, :, :], src.rearrange("(k p) n -> p k n", p=P)).then_inc(loaded, 16)
            sp.dma_start(rbs[:, :], rb.rearrange("(a k) -> a k", a=1).partition_broadcast(P)).then_inc(loaded, 16)
            load(Pair(0, 1))
            sp.wait_ge(pads, 2)
            sp.dma_start(lists.rearrange("(p n) a -> p (n a)", p=P), nobody[:, :]).then_inc(zeroed, 16)
            sp.dma_start(rows[NTOK:NTOK + 1, :], zrow[0:1, 0:ROW]).then_inc(zeroed, 16)
            sp.dma_start(out[NTOK:NTOK + TS, :].rearrange("(p r) c -> p (r c)", p=P),
                         zrow[:, :]).then_inc(zeroed, 16)

            def put(q, dst, src, done):
                seq = dst[bass.ds(q.at(PAIR_TOK), PAIR_TOK), :].rearrange("(b t) c -> b t c", b=2)
                sp.dma_start(seq[:, 0:P, :].rearrange("b t c -> t b c"), src[:, q.s, 0:2, :]).then_inc(done[q.s], 16)
                for b in range(2):
                    sp.dma_start(seq[b, P:T, :], src[b * REST:(b + 1) * REST, q.s, 2, :]).then_inc(done[q.s], 16)

            def store(q):
                sp.wait_ge(ln2, q.at(N_LN2, 1))
                end_of_waits()
                put(q, out, h1, h1_stored)
                sp.wait_ge(route, q.at(N_ROUTE, 21))
                end_of_waits()
                sp.wait_ge(xn2_ready, q.at(3, 3))
                end_of_waits()
                put(q, rows, xs, rows_stored)

            for s in range(2):
                load(Pair(1, s))
                store(Pair(0, s))
            with sp.Fori(1, PAIRS // 2 - 1) as n:
                for s in range(2):
                    load(Pair(n + 1, s))
                    store(Pair(n, s))
            for s in range(2):
                store(Pair(PAIRS // 2 - 1, s))
            sp.wait_ge(zeroed, 48)
            for s in range(2):
                sp.wait_ge(h1_stored[s], 48 * (PAIRS // 2))
                sp.wait_ge(rows_stored[s], 48 * (PAIRS // 2))
                sp.wait_ge(listed[s], 96 * (PAIRS // 2))

        @block.gpsimd
        def _(pool):
            pool.iota(diag[:, :], [[1, P]], base=0, channel_multiplier=-1).then_inc(iotas, 1)
            pool.iota(bandi[:, 0:BAND1 + GAP], [[1, BAND1 + GAP]], base=0, channel_multiplier=-2).then_inc(iotas, 1)
            pool.iota(bandi[:, BAND1 + GAP:], [[-2, BAND2]], base=LEFT, channel_multiplier=1).then_inc(iotas, 1)
            pool.iota(eid_i[:, :], [[1, E]], base=0, channel_multiplier=0).then_inc(iotas, 1)
            pool.iota(reg_i[:, :], [[REG, E]], base=0, channel_multiplier=0).then_inc(iotas, 1)
            pool.iota(tok_i[:, 0:2], [[T, 2]], base=0, channel_multiplier=1).then_inc(iotas, 1)
            pool.iota(tok_i[:, 2:4], [[P - REST, 2]], base=P, channel_multiplier=1).then_inc(iotas, 1)
            pool.memset(zrow[:, :], 0.0).then_inc(pads, 1)
            pool.memset(nobody[:, :], NTOK).then_inc(pads, 1)
            pool.memset(c_eps[:, :], EPS).then_inc(pads, 1)
            pool.memset(c_pow[:, :], -0.5).then_inc(pads, 1)
            pool.memset(c_neg[:, :], -1.0).then_inc(pads, 1)
            pool.memset(kpad[:, :, 0:1], NEG).then_inc(pads, 1)
            for pad in (e1s, e2s, e2sv):
                pool.memset(pad[:, :, 0:1], 0.0).then_inc(pads, 1)
            pool.wait_ge(pads, 9)

            def rstd(q, stats, n, mv, ve, rs, mr, nb, done):
                pool.wait_ge(stats, q.at(n, n))
                pool.wait_ge(done, q.at(N_RSTD))
                pool.tensor_tensor(ve[:, :], mv[:, :, 1], c_eps[:, :], ALU.add).then_inc(done, 1)
                pool.wait_ge(done, q.at(N_RSTD, 1))
                pool.tensor_tensor(rs[:, :], ve[:, :], c_pow[:, :], ALU.pow).then_inc(done, 1)
                pool.wait_ge(done, q.at(N_RSTD, 2))
                pool.tensor_tensor(mr[:, :], mv[:, :, 0], rs[:, :], ALU.mult).then_inc(done, 1)
                pool.wait_ge(done, q.at(N_RSTD, 3))
                pool.tensor_tensor(nb[:, :], mr[:, :], c_neg[:, :], ALU.mult).then_inc(done, 1)

            def body(p0, p1, p2):
                if p2:
                    rstd(p2, ln2, N_LN2, mv2, ve2, rs2, mr2, nb2, rstd2)
                if p1:
                    pool.wait_ge(exps, p1.at(4, 4))
                    pool.wait_ge(kr_taken, p1.at(4, 4))
                    pool.wait_ge(state, p1.at(N_STATE))
                    pool.tensor_tensor(t2[:, :, :], e2y[:, :, :], v[:, p1.s], ALU.mult).then_inc(t2_done, 1)
                if p0:
                    rstd(p0, ln1, N_LN1, mv1, ve1, rs1, mr1, nb1, rstd1)
                if p1:
                    pool.wait_ge(state, p1.at(N_STATE, 2))
                    pool.tensor_tensor(t3[:, :, :], e1y[:, :, :], sb_[:, :, 0:T], ALU.mult).then_inc(t3_done, 1)
                if p2:
                    pool.wait_ge(route, p2.at(N_ROUTE, 24))
                    pool.sem_inc(slots_seen, 1)
                    for c in range(6):
                        pool.indirect_dma_start(lists, bass.IndirectOffsetOnAxis(slots[:, p2.s, c:c + 1], 0),
                                                tid[:, p2.s, c % 3:c % 3 + 1], None).then_inc(listed[p2.s], 16)

            pool.wait_ge(zeroed, 48)
            rounds(pool, body)

        @block.scalar
        def _(act):
            act.preload_act_table_set("natural_log_exp_and_others")
            act.wait_ge(params, 48)
            act.activation(w[:, :], dec[:, :], ACT.Exp).then_inc(setup_act, 1)

            def body(p0, p1, p2):
                if p1:
                    act.wait_ge(state, p1.at(N_STATE))
                    act.wait_ge(t3_done, p1.at(1))
                    for k, (src, dst, sc) in enumerate(((up_s, e1s, -1.0), (dn_s, e2s, 1.0), (up_y, e1y, -1.0), (dn_y, e2y, 1.0))):
                        act.wait_ge(diffs, p1.at(N_DIFF, (5, 7, 8, 9)[k]))
                        act.activation(dst[:, :, 1:TP] if k < 2 else dst[:, :, :], src[:, :, :], ACT.Exp, scale=sc).then_inc(exps, 1)
                if p0:
                    act.wait_ge(conv_done, p0.at(1, 1))
                    if not isinstance(p0.g, int) or p0.g:
                        act.wait_ge(ln2, Pair(p0.g - 1, p0.s).at(N_LN2, 1))
                    act.activation(h[:, p0.s].rearrange("p t c -> p (t c)"), conv_ps[:, 0:3 * C], ACT.Copy).then_inc(h_taken, 1)
                if p2:
                    act.wait_ge(rstd2, p2.at(N_RSTD, N_RSTD))
                    act.wait_ge(rows_stored[p2.s], p2.slot_at(48))
                    for t in range(3):
                        act.activation(xs[:, p2.s, t, 0:C], h1[:, p2.s, t, :], ACT.Identity,
                                       bias=nb2[:, t:t + 1], scale=rs2[:, t:t + 1]).then_inc(xn2_ready, 1)
                    act.wait_ge(lg_done, p2.at(1))
                    for k in range(HC):
                        act.wait_ge(t2T_done, p2.at(HC, k + 1))
                        act.activation(x2T[:, k, :], tp_ps[:, 0:3 * P], ACT.Copy).then_inc(t2T_taken, 1)
                if p0:
                    act.wait_ge(rstd1, p0.at(N_RSTD, N_RSTD))
                    act.wait_ge(t1_done, p0.at(HC))
                    for t in range(3):
                        act.activation(xn[:, t, :], h[:, p0.s, t, :], ACT.Identity,
                                       bias=nb1[:, t:t + 1], scale=rs1[:, t:t + 1]).then_inc(xn_ready, 1)
                    act.wait_ge(kr_done, p0.at(4))
                    for k in range(HC):
                        act.wait_ge(t1_done, p0.at(HC, k + 1))
                        act.activation(xnT[:, k, :], tp_ps[:, 0:PAIR_TOK], ACT.Copy).then_inc(t1_taken, 1)
                if p2:
                    act.wait_ge(route, p2.at(N_ROUTE, 14))
                    act.activation(ed[:, :], dm[:, :], ACT.Exp).then_inc(gate_exp, 1)
                if p1:
                    act.wait_ge(state, p1.at(N_STATE, 8))
                    act.activation(lnd[:, :], dsg[:, :], ACT.Ln).then_inc(inv_ready, 1)
                    act.wait_ge(inv_ready, p1.at(2, 1))
                    act.wait_ge(o_ready, p1.at(2))
                    act.activation(inv[:, :], lnd[:, :], ACT.Exp, scale=-1.0).then_inc(inv_ready, 1)
                if p0:
                    act.wait_ge(diffs, p0.at(N_DIFF))
                    if not isinstance(p0.g, int) or p0.g:
                        act.wait_ge(t2_done, Pair(p0.g - 1, p0.s).at(1, 1))
                        act.wait_ge(state, Pair(p0.g - 1, p0.s).at(N_STATE, 8))
                    for k in range(HC):
                        act.wait_ge(kr_done, p0.at(4, k + 1))
                        act.activation(kpad[:, 2 * k:2 * k + 2, 1:TP], kr_ps[k][:, 0:PAIR_TOK].rearrange("p (b t) -> p b t", b=2),
                                       ACT.Copy).then_inc(kr_taken, 1)
                    for k in range(HC):
                        act.wait_ge(kr_done, p0.at(4, k + 3))
                        act.activation(v[:, p0.s, 2 * k:2 * k + 2, :], kr_ps[k][:, 0:PAIR_TOK].rearrange("p (b t) -> p b t", b=2),
                                       ACT.Copy).then_inc(kr_taken, 1)
                    act.wait_ge(kr_taken, p0.at(4, 4))
                    act.activation(er[:, p0.s], v[:, p0.s].rearrange("p a t -> p (a t)"), ACT.Exp, scale=-1.0).then_inc(er_ready, 1)

            rounds(act, body)

        @block.tensor
        def _(pe):
            pe.wait_ge(bands, 15)
            for s in range(NKI):
                dst = (conv_ps[:, 0:512], conv_ps[:, 512:1024], kr_ps[0][:, :])[s // 2]
                qs = [q for q in range(NKM) if -KI < KI * s - 2 * KM * q + LEFT < BAND1]
                for q in qs:
                    a = AT1 + KI * s - 2 * KM * q + LEFT
                    b = AT2 - (KM // 2) * q
                    last = pe.matmul(dst[0:KI, (s % 2) * T:(s % 2 + 1) * T], band[0:KM, a:a + KI], band[0:KM, b:b + T],
                                     start=q == qs[0], stop=q == qs[-1])
            last.then_inc(filt_done, 1)
            pe.wait_ge(ready, 1)
            pe.wait_ge(loaded, 16 * 5)
            pe.wait_ge(consts, 13)

            def transposes(src, dst, done, k, by_sequence):
                for t in range(3):
                    o = dst[:, t * P:(t + 1) * P]
                    if by_sequence:
                        o = dst[:, t * T:t * T + P] if t < 2 else dst[:, 0:PAIR_TOK].rearrange("p (b t) -> p b t", b=2)[:, :, P:T]
                    last = pe.transpose(o, src[:, t, k * P:(k + 1) * P], ident[:, :])
                last.then_inc(done, 1)

            def body(p0, p1, p2):
                if p2:
                    pe.wait_ge(o_ready, p2.at(2, 2))
                    pe.wait_ge(ln2, p2.at(N_LN2))
                    for t in range(3):
                        for k in range(HC):
                            last = pe.matmul(wo_ps[:, t * C:(t + 1) * C], oT[:, k, t * P:(t + 1) * P], wo[:, k, :], start=k == 0, stop=k == HC - 1)
                    last.then_inc(wo_done, 1)
                if p0:
                    pe.wait_ge(x_loaded[p0.s], p0.slot_at(32, 32))
                    pe.wait_ge(h_taken, p0.at(1))
                    for b in range(2):
                        for s in range(5):
                            pe.matmul(conv_ps[:, b * C:(b + 1) * C], filt[0:KI, s, 0:P], xin[0:KI, p0.s, b, s, :],
                                      start=s == 0, stop=s == 4)
                    for b in range(2):
                        for s in range(3):
                            last = pe.matmul(conv_ps[:, 2 * C:3 * C], filt_rest[0:KI, s, b, :], xin[0:KI, p0.s, b, 3 + s, :],
                                             start=b == 0 and s == 0, stop=b == 1 and s == 2)
                    last.then_inc(conv_done, 1)
                if p2:
                    pe.wait_ge(xn2_ready, p2.at(3, 3))
                    for k in range(HC):
                        if k == 0:
                            pe.wait_ge(t1_taken, p2.at(HC, 2 * HC) if p0 or p1 else HC * PAIRS)
                        else:
                            pe.wait_ge(t2T_taken, p2.at(HC, k))
                        transposes(xs[:, p2.s], tp_ps, t2T_done, k, False)
                    pe.wait_ge(t2T_taken, p2.at(HC, HC))
                    pe.wait_ge(route, p2.at(N_ROUTE))
                    for t in range(3):
                        for k in range(HC):
                            last = pe.matmul(cnt_ps[:, t * E:(t + 1) * E], x2T[:, k, t * P:(t + 1) * P], rws[:, k, :],
                                             start=k == 0, stop=k == HC - 1)
                    last.then_inc(lg_done, 1)
                if p0:
                    pe.wait_ge(xn_ready, p0.at(3, 3))
                    for k in range(HC):
                        pe.wait_ge(t1_taken, p0.at(HC, k))
                        if k == 0 and p2:
                            pe.wait_ge(t2T_taken, p2.at(HC, HC))
                        transposes(xn, tp_ps, t1_done, k, True)
                    pe.wait_ge(t1_taken, p0.at(HC, HC))
                    for j in range(4):
                        pe.wait_ge(kr_taken, p0.at(4, max(0, j - 1)))
                        m = j % 2
                        for k in range(HC):
                            last = pe.matmul(kr_ps[m][:, 0:PAIR_TOK], (wk, wr)[j // 2][:, k, m * P:(m + 1) * P], xnT[:, k, :],
                                             start=k == 0, stop=k == HC - 1)
                        last.then_inc(kr_done, 1)
                        if j == 1 and p2:
                            ranks(p2)
                elif p2:
                    ranks(p2)

            def ranks(q):
                pe.wait_ge(route, q.at(N_ROUTE, 13))
                flat = sel[:, :, :].rearrange("p t e -> p (t e)")
                pe.matmul(rank_ps[:, 2 * E:3 * E], ones[:, :], flat[:, 0:E], start=True, stop=False, skip_group_check=True)
                pe.matmul(rank_ps[:, E:3 * E], ones[:, :], flat[:, 0:2 * E], start=False, stop=False, skip_group_check=True)
                pe.matmul(rank_ps, before[:, :], flat, start=False, stop=True, skip_group_check=True)
                for t in range(3):
                    last = pe.matmul(tot_ps, ones[:, :], sel[:, t, :], start=t == 0, stop=t == 2)
                last.then_inc(rank_done, 1)

            rounds(pe, body)

        @block.vector
        def _(dve):
            dve.memset(band[:, :], 0.0).then_inc(consts, 1)
            dve.wait_ge(iotas, 7)
            dve.tensor_scalar(ident[:, :], diag[:, :], 0.0, None, ALU.is_equal).then_inc(consts, 1)
            dve.tensor_scalar(before[:, :], diag[:, :], 0.0, None, ALU.is_gt).then_inc(consts, 1)
            dve.memset(ones[:, :], 1.0).then_inc(consts, 1)
            dve.memset(wseq[:, :, :], 0.0).then_inc(consts, 1)
            dve.memset(filt_rest[:, :, :, :], 0.0).then_inc(consts, 1)
            dve.tensor_copy(eid[:, :], eid_i[:, :]).then_inc(consts, 1)
            dve.tensor_copy(ends[:, :], reg_i[:, :]).then_inc(consts, 1)
            dve.tensor_copy(tok[:, 0:2], tok_i[:, 0:2]).then_inc(consts, 1)
            dve.tensor_copy(tok[0:REST, 2:3], tok_i[0:REST, 2:3]).then_inc(consts, 1)
            dve.wait_ge(consts, 10)
            dve.tensor_scalar(tok[REST:P, 2:3], tok_i[REST:P, 2:3], float(T - REST), None, ALU.add).then_inc(consts, 1)
            dve.wait_ge(params, 48)
            active = band[:, AT1:AT2 + BAND2]
            dve.tensor_scalar(active, bandi[:, :], 0.0, taps[:, 0:1], ALU.is_equal, ALU.mult).then_inc(bands, 1)
            for k in range(1, TAPS):
                dve.wait_ge(bands, 2 * k - 1)
                dve.tensor_scalar(btmp[:, :], bandi[:, :], float(k), taps[:, k:k + 1], ALU.is_equal, ALU.mult).then_inc(bands, 1)
                dve.wait_ge(bands, 2 * k)
                dve.tensor_tensor(active, active, btmp[:, :], ALU.add).then_inc(bands, 1)
            dve.wait_ge(setup_act, 1)
            dve.tensor_scalar(w[:, :], w[:, :], -1.0, None, ALU.mult).then_inc(consts, 1)
            dve.wait_ge(consts, 12)
            dve.tensor_tensor(uw[:, :], u[:, :], w[:, :], ALU.add).then_inc(consts, 1)
            for k in range(HC):
                dve.tensor_scalar(wseq[:, 2 * k:2 * k + 2, :], wseq[:, 2 * k:2 * k + 2, :], w[:, k:k + 1], None, ALU.add).then_inc(consts, 1)
            dve.wait_ge(consts, 15)
            dve.memset(wseq[:, :, 0:1], -3e38).then_inc(consts, 1)
            dve.wait_ge(filt_done, 1)
            for n, src in enumerate((conv_ps[:, 0:2 * T], conv_ps[:, 512:512 + 2 * T], kr_ps[0][:, 0:2 * T])):
                dve.tensor_copy(filt[0:KI, 2 * n:2 * n + 2, :], src[0:KI, :].rearrange("p (s t) -> p s t", s=2)).then_inc(consts, 1)
            dve.wait_ge(consts, 19)
            dve.tensor_copy(filt_rest[0:KI, :, 0, 0:REST], filt[0:KI, 3:6, P:T]).then_inc(consts, 1)
            dve.tensor_copy(filt_rest[0:KI, :, 1, REST:P], filt[0:KI, 3:6, P:T]).then_inc(consts, 1)
            dve.wait_ge(consts, 21)
            dve.memset(btmp[:, 0:1], 0.0).then_inc(ready, 1)
            dve.wait_ge(pads, 9)
            dve.wait_ge(loaded, 16 * 5)

            def stats(q, src, st, mv, n, at, done):
                for t in range(3):
                    dve.bn_stats(st[:, t, :], src[:, t, :]).then_inc(done, 1)
                dve.wait_ge(done, q.at(n, at + 3))
                dve.sem_inc(stats_seen, 1)
                for t in range(3):
                    dve.bn_aggr(mv[:, t, :], st[:, t, :]).then_inc(done, 1)

            def body(p0, p1, p2):
                if p2:
                    dve.wait_ge(inv_ready, p2.at(2, 2))
                    dve.wait_ge(wo_done, p2.at(1))
                    for a, o in ((slice(0, P), oT[:, :, 0:2 * P]), (slice(P, T), oT[:, :, 2 * P:3 * P])):
                        dve.tensor_tensor(o.rearrange("p k (b t) -> p k b t", b=2), *(
                            i[:, :].rearrange("p (k b t) -> p k b t", k=HC, b=2)[:, :, :, a] for i in (num, inv)),
                            ALU.mult).then_inc(o_ready, 1)
                if p1:
                    dve.wait_ge(kr_taken, p1.at(4, 2))
                    dve.wait_ge(diffs, p1.at(N_DIFF))
                    dve.tensor_tensor_scan(pp[:, :, :].rearrange("p a t -> p (a t)"), wseq[:, :, :].rearrange("p a t -> p (a t)"),
                                           kpad[:, :, :].rearrange("p a t -> p (a t)"), NEG, ALU.add, ALU.max).then_inc(diffs, 1)
                    dve.wait_ge(diffs, p1.at(N_DIFF, 1))
                    for k in range(HC):
                        a = slice(2 * k, 2 * k + 2)
                        dve.scalar_tensor_tensor(out=dl[:, a, :], in0=kpad[:, a, 1:TP], scalar=u[:, k:k + 1], in1=pp[:, a, 0:T],
                                                 op0=ALU.add, op1=ALU.subtract).then_inc(diffs, 1)
                    dve.wait_ge(exps, p1.at(4))
                    for dst, op in ((up_s, ALU.max), (dn_s, ALU.min)):
                        for k in range(HC):
                            dve.wait_ge(diffs, p1.at(N_DIFF, 2 + k))
                            a = slice(2 * k, 2 * k + 2)
                            dve.tensor_scalar(dst[:, a, :], dl[:, a, :], uw[:, k:k + 1], 0.0, ALU.subtract, op).then_inc(diffs, 1)
                    for dst, op in ((up_y, ALU.max), (dn_y, ALU.min)):
                        dve.tensor_scalar(dst[:, :, :], dl[:, :, :], 0.0, None, op).then_inc(diffs, 1)
                if p2:
                    dve.wait_ge(wo_done, p2.at(1, 1))
                    dve.wait_ge(h1_stored[p2.s], p2.slot_at(48))
                    dve.wait_ge(xn2_ready, p2.at(3))
                    dve.tensor_tensor(h1[:, p2.s].rearrange("p t c -> p (t c)"), wo_ps[:, 0:3 * C],
                                      h[:, p2.s].rearrange("p t c -> p (t c)"), ALU.add).then_inc(ln2, 1)
                    dve.wait_ge(ln2, p2.at(N_LN2, 1))
                    dve.wait_ge(rstd2, p2.at(N_RSTD))
                    stats(p2, h1[:, p2.s], st2, mv2, N_LN2, 1, ln2)
                if p1:
                    dve.wait_ge(exps, p1.at(4, 2))
                    dve.wait_ge(kr_taken, p1.at(4, 4))
                    dve.wait_ge(state, p1.at(N_STATE))
                    dve.tensor_tensor(e2sv[:, :, 1:TP], e2s[:, :, 1:TP], v[:, p1.s], ALU.mult).then_inc(state, 1)
                    dve.wait_ge(t3_done, p1.at(1))
                    dve.tensor_tensor_scan(sb_[:, :, :].rearrange("p a t -> p (a t)"), e1s[:, :, :].rearrange("p a t -> p (a t)"),
                                           e2s[:, :, :].rearrange("p a t -> p (a t)"), 0.0, ALU.mult, ALU.add).then_inc(state, 1)
                    dve.wait_ge(state, p1.at(N_STATE, 1))
                    dve.tensor_tensor_scan(sa[:, :, :].rearrange("p a t -> p (a t)"), e1s[:, :, :].rearrange("p a t -> p (a t)"),
                                           e2sv[:, :, :].rearrange("p a t -> p (a t)"), 0.0, ALU.mult, ALU.add).then_inc(state, 1)
                if p0:
                    dve.wait_ge(h_taken, p0.at(1, 1))
                    dve.wait_ge(rstd1, p0.at(N_RSTD))
                    dve.wait_ge(ln1, p0.at(N_LN1))
                    stats(p0, h[:, p0.s], st1, mv1, N_LN1, 0, ln1)
                if p1:
                    dve.wait_ge(exps, p1.at(4, 3))
                    dve.wait_ge(state, p1.at(N_STATE, 3))
                    dve.tensor_tensor(t1[:, :, :], e1y[:, :, :], sa[:, :, 0:T], ALU.mult).then_inc(state, 1)
                    dve.wait_ge(er_ready, p1.at(1, 1))
                    dve.tensor_scalar(em[:, :], er[:, p1.s], EMAX, 1.0, ALU.min, ALU.add).then_inc(state, 1)
                    dve.wait_ge(t2_done, p1.at(1, 1))
                    dve.wait_ge(state, p1.at(N_STATE, 4))
                    dve.wait_ge(o_ready, p1.at(2))
                    dve.tensor_tensor(num[:, :], t1[:, :, :].rearrange("p a t -> p (a t)"),
                                      t2[:, :, :].rearrange("p a t -> p (a t)"), ALU.add).then_inc(state, 1)
                if p2:
                    route_a(p2)
                if p1:
                    dve.wait_ge(t3_done, p1.at(1, 1))
                    dve.wait_ge(exps, p1.at(4, 4))
                    dve.tensor_tensor(den[:, :], t3[:, :, :].rearrange("p a t -> p (a t)"),
                                      e2y[:, :, :].rearrange("p a t -> p (a t)"), ALU.add).then_inc(state, 1)
                    dve.wait_ge(state, p1.at(N_STATE, 7))
                    dve.wait_ge(inv_ready, p1.at(2))
                    dve.tensor_tensor(dsg[:, :], den[:, :], em[:, :], ALU.mult).then_inc(state, 1)
                if p2:
                    route_b(p2)

            def over_e(a):
                return a.unsqueeze(2).to_broadcast([P, 3, E])

            def over_t(a):
                return a.unsqueeze(1).to_broadcast([P, 3, E])

            def route_a(q):
                n = [0]

                def step(ins):
                    n[0] += 1
                    ins.then_inc(route, 1)

                def after(k):
                    dve.wait_ge(route, q.at(N_ROUTE, k))

                dve.wait_ge(lg_done, q.at(1, 1))
                after(0)
                step(dve.tensor_tensor(lg[:, :, :], lg_ps, over_t(rbs[:, :]), ALU.add))
                after(1)
                step(dve.tensor_reduce(m1[:, :], lg[:, :, :], AX.X, ALU.max))
                after(2)
                step(dve.tensor_tensor(eq[:, :, :], lg[:, :, :], over_e(m1[:, :]), ALU.is_equal))
                after(3)
                step(dve.scalar_tensor_tensor(out=cand[:, :, :], in0=eq[:, :, :], scalar=-float(E), in1=over_t(eid[:, :]),
                                              op0=ALU.mult, op1=ALU.add))
                after(4)
                step(dve.tensor_reduce(i1[:, :], cand[:, :, :], AX.X, ALU.min))
                after(5)
                step(dve.tensor_tensor(oh1[:, :, :], cand[:, :, :], over_e(i1[:, :]), ALU.is_equal))
                after(6)
                step(dve.scalar_tensor_tensor(out=lg2[:, :, :], in0=oh1[:, :, :], scalar=-3e38, in1=lg[:, :, :],
                                              op0=ALU.mult, op1=ALU.add))
                after(7)
                step(dve.tensor_reduce(m2[:, :], lg2[:, :, :], AX.X, ALU.max))
                after(8)
                step(dve.tensor_tensor(eq[:, :, :], lg2[:, :, :], over_e(m2[:, :]), ALU.is_equal))
                after(9)
                step(dve.scalar_tensor_tensor(out=cand2[:, :, :], in0=eq[:, :, :], scalar=-float(E), in1=over_t(eid[:, :]),
                                              op0=ALU.mult, op1=ALU.add))
                after(10)
                step(dve.tensor_reduce(i2[:, :], cand2[:, :, :], AX.X, ALU.min))
                after(11)
                step(dve.tensor_tensor(oh2[:, :, :], cand2[:, :, :], over_e(i2[:, :]), ALU.is_equal))
                after(12)
                step(dve.tensor_tensor(sel[:, :, :], oh1[:, :, :], oh2[:, :, :], ALU.add))
                step(dve.tensor_tensor(dm[:, :], m2[:, :], m1[:, :], ALU.subtract))
                dve.wait_ge(rows_stored[q.s], q.slot_at(48))
                step(dve.tensor_scalar(xs[:, q.s, :, C + 2], i1[:, :], float(E), None, ALU.add))
                dve.wait_ge(tok_next, q.at(1))
                dve.wait_ge(listed[q.s], q.slot_at(96))
                step(dve.tensor_copy(tid[:, q.s, :], tok[:, :]))
                assert n[0] == 16

            def route_b(q):
                def after(k):
                    dve.wait_ge(route, q.at(N_ROUTE, k))

                dve.wait_ge(gate_exp, q.at(1, 1))
                dve.tensor_scalar(ed1[:, :], ed[:, :], 1.0, None, ALU.add).then_inc(route, 1)
                dve.wait_ge(rank_done, q.at(1, 1))
                dve.tensor_tensor(place[:, :, :], rank_ps.rearrange("p (t e) -> p t e", e=E), over_t(ends[:, :]), ALU.add).then_inc(route, 1)
                after(17)
                dve.reciprocal(xs[:, q.s, :, C], ed1[:, :]).then_inc(route, 1)
                after(18)
                dve.tensor_tensor(pl1[:, :, :], place[:, :, :], oh1[:, :, :], ALU.mult).then_inc(route, 1)
                after(19)
                dve.tensor_tensor(xs[:, q.s, :, C + 1], ed[:, :], xs[:, q.s, :, C], ALU.mult).then_inc(route, 1)
                dve.tensor_tensor(lg2[:, :, :], place[:, :, :], oh2[:, :, :], ALU.mult).then_inc(route, 1)
                with nc.allow_low_precision("whole numbers"):
                    after(20)
                    dve.tensor_reduce(slots[:, q.s, 0:3], pl1[:, :, :], AX.X, ALU.add).then_inc(route, 1)
                    after(22)
                    dve.tensor_reduce(slots[:, q.s, 3:6], lg2[:, :, :], AX.X, ALU.add).then_inc(route, 1)
                dve.tensor_tensor(ends[:, :], tot_ps, ends[:, :], ALU.add).then_inc(route, 1)
                after(16)
                dve.tensor_scalar(tok[:, :], tok[:, :], float(PAIR_TOK), None, ALU.add).then_inc(tok_next, 1)

            rounds(dve, body)
            dve.wait_ge(route, N_ROUTE * PAIRS)




def tiles(eng, first, body, last):
    first()
    for s in range(2):
        body(Pair(0, s))
    with eng.Fori(1, (NT - 1) // 2) as n:
        for s in range(2):
            body(Pair(n, s))
    if NT % 2 == 0:
        body(Pair(NT // 2 - 1, 0))
    last(Pair((NT - 1) // 2, (NT - 1) % 2))


def experts(nc, ew, b2, out, rows, lists, ends):
    ctx = ExitStack()

    def sb(name, shape, dt=F32):
        return ctx.enter_context(nc.sbuf_tensor(name, shape, dt))

    def ps(name):
        return ctx.enter_context(nc.psum_tensor(name, [P, 512], F32))

    def sem(name):
        return ctx.enter_context(nc.semaphore(name))

    with ctx:
        NC = NT + 1
        jcol_i, jcol = sb("jcol_i", [P, NC], I32), sb("jcol", [P, NC])
        e_i, e_no = sb("e2_i", [P, E], I32), sb("e2_no", [P, E])
        lim_i, part_i, part = sb("lim_i", [P, MAXT], I32), sb("part_i", [P, R + 1], I32), sb("part", [P, R + 1])
        cnt, nts, ends_t, start_t, onesE = (sb(n, [P, E]) for n in ("cnt", "nts", "ends_t", "start_t", "onesE"))
        grp_e = sb("grp_e", [P, E])
        more = sb("more", [P, E, MAXT])
        past, oh, pick = (sb(n, [P, NC, E]) for n in ("past", "oh", "pick"))
        ej, ecl, grp, live, idx_f = (sb(n, [P, NC]) for n in ("ej", "ecl", "grp", "live", "idx_f"))
        table = sb("table", [P, NC, 3], U32)
        ident, ident_i = sb("ident2", [P, P]), sb("ident2_i", [P, P], I32)
        idx = sb("idx", [P, 2, 3], U32)
        raw = sb("raw", [P, 2, WROW])
        whi, wlo = sb("whi", [P, 2, B1AT], F32R), sb("wlo", [P, 2, B1AT], F32R)
        b1, b2s = sb("b1", [P, 2, FC]), sb("b2s", [P, 2, C])
        tid = sb("tid2", [P, 2, R], U32)
        xg = sb("xg", [P, 2, R, ROW])
        xhi, xlo = sb("xhi", [P, 2, HC, TS], F32R), sb("xlo", [P, 2, HC, TS], F32R)
        hid = sb("hid", [P, 2, TS])
        hhi, hlo = sb("hhi", [P, 4, TS], F32R), sb("hlo", [P, 4, TS], F32R)
        ysum, yout = sb("ysum", [P, 2, R, C]), sb("yout", [P, 2, R, C])
        tk, tk2, gA, gB = (sb(n, [P, R]) for n in ("tk", "tk2", "gA", "gB"))
        gate, dest = sb("gate", [P, 2, R]), sb("dest", [P, 2, R], U32)

        acc = [ps(f"acc{i}") for i in range(R)]
        hp = [ps("hp0"), ps("hp1")]
        xt = [ps("xt0"), ps("xt1")]

        iotas, tab = sem("iotas2"), sem("tab")
        idx_ready, waits_over = sem("idx_ready"), sem("waits_over")
        w_in, tid_in, x_in, b2_in, y_sent = ([sem(f"{n}{s}") for s in range(2)] for n in ("w_in", "tid_in", "x_in", "b2_in", "y_sent"))
        xt_done, xhi_done, xlo_done = sem("xt_done"), sem("xhi_done"), sem("xlo_done")
        whi_done, wlo_done, b1_done = sem("whi_done"), sem("wlo_done"), sem("b1_done")
        hp_done, hid_done, hhi_done, hlo_done = sem("hp_done"), sem("hid_done"), sem("hhi_done"), sem("hlo_done")
        acc_done, y_taken, y_ready, marks = sem("acc_done"), sem("y_taken"), sem("y_ready"), sem("marks")
        N_MARK = 6
        PIECE = B1AT // FC

        block = ctx.enter_context(nc.Block())

        def nxt(j):
            return Pair(j.g, 1) if j.s == 0 else Pair(j.g + 1, 0)

        def prev(j):
            return Pair(j.g - 1, 1) if j.s == 0 else Pair(j.g, 0)

        @block.gpsimd
        def _(pool):
            pool.iota(jcol_i[:, :], [[1, NC]], base=0, channel_multiplier=0).then_inc(iotas, 1)
            pool.iota(e_i[:, :], [[1, E]], base=0, channel_multiplier=0).then_inc(iotas, 1)
            pool.iota(lim_i[:, :], [[TS, MAXT]], base=0, channel_multiplier=0).then_inc(iotas, 1)
            pool.iota(part_i[:, 0:R], [[1, R]], base=0, channel_multiplier=R).then_inc(iotas, 1)
            pool.iota(part_i[:, R:R + 1], [[0, 1]], base=0, channel_multiplier=1).then_inc(iotas, 1)
            pool.iota(ident_i[:, :], [[1, P]], base=0, channel_multiplier=-1).then_inc(iotas, 1)
            groups = lists.rearrange("(g r) a -> g (r a)", r=R)

            def end_of_waits():
                pool.sem_inc(waits_over, 1)

            def gather_w(j):
                pool.indirect_dma_start(raw[:, j.s, :], None, ew, bass.IndirectOffsetOnAxis(idx[:, j.s, 0:1], 0)).then_inc(w_in[j.s], 16)

            def gather_tid(j):
                pool.indirect_dma_start(tid[:, j.s, :], None, groups, bass.IndirectOffsetOnAxis(idx[:, j.s, 1:2], 0)).then_inc(tid_in[j.s], 16)

            def gather_x(j):
                pool.wait_ge(tid_in[j.s], j.slot_at(16, 16))
                end_of_waits()
                for r in range(R):
                    pool.indirect_dma_start(xg[:, j.s, r, :], None, rows,
                                            bass.IndirectOffsetOnAxis(tid[:, j.s, r:r + 1], 0)).then_inc(x_in[j.s], 16)

            def gather_b2(j):
                pool.indirect_dma_start(b2s[:, j.s, :], None, b2, bass.IndirectOffsetOnAxis(idx[:, j.s, 2:3], 0)).then_inc(b2_in[j.s], 16)

            def first():
                pool.wait_ge(idx_ready, 1)
                gather_tid(Pair(0, 0))
                gather_w(Pair(0, 0))
                pool.wait_ge(idx_ready, 2)
                gather_tid(Pair(0, 1))
                gather_x(Pair(0, 0))
                gather_b2(Pair(0, 0))
                gather_w(Pair(0, 1))
                gather_x(Pair(0, 1))

            def body(j):
                after = Pair(j.g + 1, j.s)
                pool.wait_ge(idx_ready, after.at(1, 1))
                pool.wait_ge(wlo_done, j.at(FC, FC))
                pool.wait_ge(b1_done, j.at(1, 1))
                pool.wait_ge(marks, j.at(N_MARK, N_MARK))
                pool.wait_ge(x_in[j.s], j.slot_at(16 * R, 16 * R))
                end_of_waits()
                gather_w(after)
                gather_tid(after)
                pool.wait_ge(y_taken, j.at(R))
                end_of_waits()
                gather_b2(nxt(j))
                pool.wait_ge(xt_done, j.at(HC, HC))
                gather_x(after)
                send_after(j)

            def send_after(j):
                pool.wait_ge(y_ready, j.at(R, R))
                pool.wait_ge(y_sent[1 - j.s], j.g * (16 * R) + (16 * R * j.s))
                end_of_waits()
                for r in range(R):
                    pool.indirect_dma_start(out[:, :], bass.IndirectOffsetOnAxis(dest[:, j.s, r:r + 1], 0),
                                            yout[:, j.s, r, :], None, compute_op=ALU.add).then_inc(y_sent[j.s], 16)

            def last(j):
                send_after(j)
                pool.wait_ge(y_sent[j.s], j.slot_at(16 * R, 16 * R))
                pool.wait_ge(w_in[1 - j.s], 16 * (NC // 2))
                pool.wait_ge(tid_in[1 - j.s], 16 * (NC // 2))
                pool.wait_ge(x_in[1 - j.s], 16 * R * (NC // 2))

            tiles(pool, first, body, last)

        @block.scalar
        def _(act):
            def x_high(j, k):
                act.wait_ge(xt_done, j.at(HC, k + 1))
                act.activation(xhi[:, j.s, k, :], xt[k][:, 0:TS], ACT.Copy).then_inc(xhi_done, 1)

            def w_high(j, k):
                act.activation(whi[:, j.s, k * PIECE:(k + 1) * PIECE], raw[:, j.s, k * PIECE:(k + 1) * PIECE], ACT.Copy).then_inc(whi_done, 1)

            def first():
                act.wait_ge(w_in[0], 16)
                for k in range(FC):
                    w_high(Pair(0, 0), k)
                for k in range(HC):
                    x_high(Pair(0, 0), k)

            def body(j, more=True):
                n = nxt(j)
                for c in range(FC):
                    act.wait_ge(hp_done, j.at(FC, c + 1))
                    if c < 2:
                        act.wait_ge(hlo_done, j.at(FC))
                        act.wait_ge(b1_done, j.at(1, 1))
                    else:
                        act.wait_ge(hlo_done, j.at(FC, c - 1))
                    act.activation(hid[:, c % 2, :], hp[c % 2][:, 0:TS], ACT.Relu, bias=b1[:, j.s, c:c + 1]).then_inc(hid_done, 1)
                    if more:
                        if c == 0:
                            act.wait_ge(w_in[n.s], n.slot_at(16, 16))
                            act.wait_ge(acc_done, j.at(1))
                        w_high(n, c)
                        if c in (5, 6):
                            x_high(n, c - 5)
                for r in range(R):
                    act.wait_ge(y_taken, j.at(R, r + 1))
                    act.wait_ge(marks, j.at(N_MARK, N_MARK))
                    act.wait_ge(y_sent[j.s], j.slot_at(16 * R))
                    act.activation(yout[:, j.s, r, :], ysum[:, j.s, r, :], ACT.Copy, scale=gate[:, j.s, r:r + 1]).then_inc(y_ready, 1)

            tiles(act, first, body, lambda j: body(j, False))

        @block.tensor
        def _(pe):
            pe.wait_ge(tab, 2)

            def transposes(j):
                pe.wait_ge(x_in[j.s], j.slot_at(16 * R, 16 * R))
                pe.wait_ge(xlo_done, j.at(HC))
                for k in range(HC):
                    for r in range(R):
                        last = pe.transpose(xt[k][:, r * P:(r + 1) * P], xg[:, j.s, r, k * P:(k + 1) * P], ident[:, :])
                    last.then_inc(xt_done, 1)

            def up(j, c):
                pe.wait_ge(hid_done, j.at(FC, max(0, c - 1)))
                n = 0
                for k in range(HC):
                    at = k * FF + c * P
                    for w_, x_ in ((whi, xhi), (wlo, xhi), (whi, xlo)):
                        last = pe.matmul(hp[c % 2][:, 0:TS], w_[:, j.s, at:at + P], x_[:, j.s, k, :], start=n == 0, stop=n == 3 * HC - 1)
                        n += 1
                last.then_inc(hp_done, 1)

            def down(j, c):
                pe.wait_ge(hlo_done, j.at(FC, c + 1))
                if c == 0:
                    pe.wait_ge(y_taken, j.at(R))
                at = W2AT + c * C
                for r in range(R):
                    for n, (h_, w_) in enumerate(((hhi, whi), (hhi, wlo), (hlo, whi))):
                        last = pe.matmul(acc[r][:, 0:C], h_[:, c % 4, r * P:(r + 1) * P], w_[:, j.s, at:at + C],
                                         start=c == 0 and n == 0, stop=c == FC - 1 and n == 2)
                return last

            def body(j, more=True):
                pe.wait_ge(wlo_done, j.at(FC, FC))
                pe.wait_ge(xlo_done, j.at(HC, HC))
                for c in range(FC):
                    up(j, c)
                    if c >= 2:
                        down(j, c - 2)
                    if c == 4 and more:
                        transposes(nxt(j))
                down(j, FC - 2)
                down(j, FC - 1).then_inc(acc_done, 1)

            tiles(pe, lambda: transposes(Pair(0, 0)), body, lambda j: body(j, False))

        @block.vector
        def _(dve):
            def over_tiles(a):
                return a.unsqueeze(1).to_broadcast([P, NC, E])

            def over_e(a, n=NC):
                return a.unsqueeze(2).to_broadcast([P, n, E])

            steps = [0]

            def step(ins, wait=True):
                steps[0] += 1
                ins.then_inc(tab, 1)
                if wait:
                    dve.wait_ge(tab, steps[0])

            dve.wait_ge(iotas, 6)
            step(dve.tensor_copy(jcol[:, :], jcol_i[:, :]), False)
            step(dve.tensor_scalar(ident[:, :], ident_i[:, :], 0.0, None, ALU.is_equal), False)
            step(dve.tensor_copy(e_no[:, :], e_i[:, :]), False)
            step(dve.tensor_copy(part[:, :], part_i[:, :]))
            step(dve.scalar_tensor_tensor(out=cnt[:, :], in0=e_no[:, :], scalar=-float(REG), in1=ends[:, :], op0=ALU.mult, op1=ALU.add))
            step(dve.tensor_tensor(more[:, :, :], cnt[:, :].unsqueeze(2).to_broadcast([P, E, MAXT]),
                                   lim_i[:, :].unsqueeze(1).to_broadcast([P, E, MAXT]), ALU.is_gt))
            step(dve.tensor_reduce(nts[:, :], more[:, :, :], AX.X, ALU.add))
            step(dve.memset(onesE[:, :], 1.0))
            step(dve.tensor_tensor_scan(ends_t[:, :], onesE[:, :], nts[:, :], 0.0, ALU.mult, ALU.add))
            step(dve.tensor_tensor(start_t[:, :], ends_t[:, :], nts[:, :], ALU.subtract))
            step(dve.tensor_scalar(grp_e[:, :], e_no[:, :], float(REG // R), None, ALU.mult))
            step(dve.scalar_tensor_tensor(out=grp_e[:, :], in0=start_t[:, :], scalar=-float(P), in1=grp_e[:, :], op0=ALU.mult, op1=ALU.add))
            step(dve.tensor_tensor(past[:, :, :], over_e(jcol[:, :]), over_tiles(ends_t[:, :]), ALU.is_ge))
            step(dve.tensor_reduce(ej[:, :], past[:, :, :], AX.X, ALU.add))
            step(dve.tensor_tensor(oh[:, :, :], over_tiles(e_no[:, :]), over_e(ej[:, :]), ALU.is_equal))
            step(dve.tensor_tensor(pick[:, :, :], oh[:, :, :], over_tiles(grp_e[:, :]), ALU.mult))
            step(dve.tensor_reduce(grp[:, :], pick[:, :, :], AX.X, ALU.add))
            step(dve.scalar_tensor_tensor(out=grp[:, :], in0=jcol[:, :], scalar=float(P), in1=grp[:, :], op0=ALU.mult, op1=ALU.add))
            step(dve.tensor_scalar(live[:, :], ej[:, :], float(E), None, ALU.is_lt))
            step(dve.tensor_scalar(idx_f[:, :], grp[:, :], part[:, R:R + 1], -float(NOGRP), ALU.add, ALU.add))
            step(dve.tensor_tensor(idx_f[:, :], idx_f[:, :], live[:, :], ALU.mult))
            step(dve.tensor_scalar(table[:, :, 1], idx_f[:, :], float(NOGRP), None, ALU.add))
            step(dve.tensor_scalar(ecl[:, :], ej[:, :], float(E - 1), None, ALU.min))
            step(dve.tensor_copy(table[:, :, 2], ecl[:, :]))
            step(dve.tensor_scalar(table[:, :, 0], ecl[:, :], float(P), part[:, R:R + 1], ALU.mult, ALU.add))

            def indices(j):
                dve.tensor_copy(idx[:, j.s, :].unsqueeze(1), table[:, bass.ds(j.at(1), 1), :]).then_inc(idx_ready, 1)

            def w_low(j, k):
                a = slice(k * PIECE, (k + 1) * PIECE)
                dve.wait_ge(whi_done, j.at(FC, k + 1))
                dve.tensor_tensor(wlo[:, j.s, a], raw[:, j.s, a], whi[:, j.s, a].bitcast(F32), ALU.subtract).then_inc(wlo_done, 1)

            def x_low(j, k):
                dve.wait_ge(xhi_done, j.at(HC, k + 1))
                dve.tensor_tensor(xlo[:, j.s, k, :], xt[k][:, 0:TS], xhi[:, j.s, k, :].bitcast(F32), ALU.subtract).then_inc(xlo_done, 1)

            def bias(j):
                dve.tensor_copy(b1[:, j.s, :], raw[:, j.s, B1AT:WROW]).then_inc(b1_done, 1)

            def mark(j):
                def after(k):
                    dve.wait_ge(marks, j.at(N_MARK, k))

                e_j = ej[:, bass.ds(j.at(1), 1)]
                dve.wait_ge(tid_in[j.s], j.slot_at(16, 16))
                dve.wait_ge(x_in[j.s], j.slot_at(16 * R, 16 * R))
                after(0)
                dve.scalar_tensor_tensor(out=tk[:, :], in0=tid[:, j.s, :], scalar=-float(NTOK), in1=part[:, 0:R],
                                         op0=ALU.add, op1=ALU.subtract).then_inc(marks, 1)
                dve.scalar_tensor_tensor(out=gA[:, :], in0=xg[:, j.s, :, C + 2], scalar=e_j, in1=xg[:, j.s, :, C],
                                         op0=ALU.is_equal, op1=ALU.mult).then_inc(marks, 1)
                dve.scalar_tensor_tensor(out=gB[:, :], in0=xg[:, j.s, :, C + 2], scalar=e_j, in1=xg[:, j.s, :, C + 1],
                                         op0=ALU.not_equal, op1=ALU.mult).then_inc(marks, 1)
                after(1)
                dve.scalar_tensor_tensor(out=tk2[:, :], in0=tid[:, j.s, :], scalar=float(NTOK), in1=tk[:, :],
                                         op0=ALU.is_lt, op1=ALU.mult).then_inc(marks, 1)
                after(3)
                dve.tensor_tensor(gate[:, j.s, :], gA[:, :], gB[:, :], ALU.add).then_inc(marks, 1)
                after(4)
                dve.scalar_tensor_tensor(out=dest[:, j.s, :], in0=tk2[:, :], scalar=float(NTOK), in1=part[:, 0:R],
                                         op0=ALU.add, op1=ALU.add).then_inc(marks, 1)

            def first():
                indices(Pair(0, 0))
                indices(Pair(0, 1))
                mark(Pair(0, 0))
                dve.wait_ge(w_in[0], 16)
                bias(Pair(0, 0))
                for k in range(FC):
                    w_low(Pair(0, 0), k)
                for k in range(HC):
                    x_low(Pair(0, 0), k)

            def body(j, more=True):
                n = nxt(j)
                for c in range(FC):
                    dve.wait_ge(hid_done, j.at(FC, c + 1))
                    if c < 4:
                        dve.wait_ge(acc_done, j.at(1))
                    else:
                        dve.wait_ge(hp_done, j.at(FC, c - 1))
                    dve.tensor_copy(hhi[:, c % 4, :], hid[:, c % 2, :]).then_inc(hhi_done, 1)
                    dve.wait_ge(hhi_done, j.at(FC, c + 1))
                    dve.tensor_tensor(hlo[:, c % 4, :], hid[:, c % 2, :], hhi[:, c % 4, :].bitcast(F32), ALU.subtract).then_inc(hlo_done, 1)
                    if more:
                        if c == 0:
                            dve.wait_ge(w_in[n.s], n.slot_at(16, 16))
                            bias(n)
                        w_low(n, c)
                        if c == 1:
                            dve.wait_ge(w_in[j.s], j.slot_at(16, 16))
                            dve.wait_ge(tid_in[j.s], j.slot_at(16, 16))
                            dve.wait_ge(b2_in[j.s], j.slot_at(16, 16))
                            indices(Pair(j.g + 1, j.s))
                        if c == 5:
                            dve.wait_ge(y_ready, j.at(R))
                            dve.wait_ge(y_sent[n.s], j.g * (16 * R) + 16 * R * j.s)
                            mark(n)
                        if c in (6, 7):
                            x_low(n, c - 6)
                dve.wait_ge(acc_done, j.at(1, 1))
                dve.wait_ge(b2_in[j.s], j.slot_at(16, 16))
                dve.wait_ge(y_ready, j.at(R))
                for r in range(R):
                    dve.tensor_tensor(ysum[:, j.s, r, :], acc[r][:, 0:C], b2s[:, j.s, :], ALU.add).then_inc(y_taken, 1)

            tiles(dve, first, body, lambda j: body(j, False))


def audio_tower(nc, x, h0, wkT, wrT, woT, decay, first, rw, rb, ew, b2, out):
    rows = nc.dram_tensor("token_rows", (NTOK + 1, ROW), F32, kind="Internal").ap()
    lists = nc.dram_tensor("expert_lists", (LIST, 1), U32, kind="Internal").ap()
    with nc.sbuf_tensor("region_ends", [P, E], F32) as ends:
        tokens_to_experts(nc, x, h0, wkT, wrT, woT, decay, first, rw, rb, out, rows, lists, ends)
        experts(nc, ew, b2, out, rows, lists, ends)


def kernel(x, L0_tok_h0, L0_attn_Wk, L0_attn_Wr, L0_attn_Wo, L0_attn_time_decay, L0_attn_time_first,
           L0_ffn_router_w, L0_ffn_router_b, L0_ffn_W1, L0_ffn_b1, L0_ffn_W2, L0_ffn_b2):
    import numpy as np
    import concourse.bacc as bacc
    from concourse.bass_utils import run_bass_kernel_spmd

    def arr(a):
        return np.asarray(a)

    w1 = arr(L0_ffn_W1).reshape(E, HC, P, FF).transpose(0, 2, 1, 3).reshape(E, P, HC * FF)
    w2 = arr(L0_ffn_W2).reshape(E, FC, P, C).transpose(0, 2, 1, 3).reshape(E, P, FC * C)
    b1 = arr(L0_ffn_b1).reshape(E, FC, P).transpose(0, 2, 1)
    ins = {
        "x": arr(x), "h0": arr(L0_tok_h0),
        "wkT": arr(L0_attn_Wk).T, "wrT": arr(L0_attn_Wr).T, "woT": arr(L0_attn_Wo).T,
        "decay": arr(L0_attn_time_decay).reshape(HC, P).T, "first": arr(L0_attn_time_first).reshape(HC, P).T,
        "rw": arr(L0_ffn_router_w), "rb": arr(L0_ffn_router_b),
        "ew": np.concatenate([w1, w2, b1], axis=2).reshape(E * P, WROW), "b2": arr(L0_ffn_b2),
    }
    nc = bacc.Bacc("TRN2", target_bir_lowering=False, num_devices=1)
    arrays, args = {}, {}
    for name, a in ins.items():
        arrays[f"in_{name}"] = np.ascontiguousarray(a)
        args[name] = nc.dram_tensor(f"in_{name}", a.shape, mybir.dt.from_np(a.dtype), kind="ExternalInput").ap()
    out = nc.dram_tensor("out_rows", (NTOK + TS, C), F32, kind="ExternalOutput").ap()
    audio_tower(nc, **args, out=out)
    r = run_bass_kernel_spmd(nc, [arrays], core_ids=[0])
    return r.results[0]["out_rows"][0:NTOK].reshape(B, T, C)
```

```python
from contextlib import ExitStack

import concourse.bass as bass
from concourse import mybir

ALU = mybir.AluOpType
ACT = mybir.ActivationFunctionType
F32 = mybir.dt.float32
F32R = mybir.dt.float32r
BF16 = mybir.dt.bfloat16
I32 = mybir.dt.int32
U32 = mybir.dt.uint32
AX = mybir.AxisListType

P = 128
B, T_IN, C = 32, 750, 256
TAPS = 8
T_MID = (T_IN + TAPS - 1) // 2
T = (T_MID + TAPS - 1) // 2
LEFT = TAPS - 2
NTOK = B * T
PAIRS = B // 2
HC = C // P
SEQ = 2 * HC
TP = T + 1
REST = T - P
K_FIRST = (4 * (P - 1) + 4) // P
K_REST = -(-(T_IN - (4 * P - 3 * LEFT)) // P)
STARTS = [P * n for n in range(K_FIRST)] + [T_IN - P * (K_REST - n) for n in range(K_REST)]
NKI = len(STARTS)
assert K_FIRST * P > 4 * (P - 1) + 3 and STARTS[K_FIRST] <= 4 * P - 3 * LEFT
KM, NKM = 126, 3
PAIR_TOK = 2 * T
E, FF = 8, 1024
FC = FF // P
TS = 384
R = TS // P
NT = (2 * NTOK + E * (TS - 1)) // TS
MAXT = NTOK // TS
REG = NTOK + TS
ROW = C + 3
LIST = E * REG + TS
NOGRP = E * REG // R
WROW = 2 * FF + FC * C + FC
W2AT, B1AT = 2 * FF, 2 * FF + FC * C
NEG = -1e38
EPS = 1e-5
EMAX = 2.0 ** 54
BAND1, GAP, BAND2 = 2 * KM + LEFT, P, KM // 2 + 3
AT1, AT2 = P, P + BAND1 + GAP
BANDS = AT2 + BAND2 + GAP


class Pair:

    def __init__(self, g, s):
        self.g, self.s = g, s

    def at(self, per_pair, more=0):
        return self.g * (2 * per_pair) + (per_pair * self.s + more)

    def first(self):
        return isinstance(self.g, int) and self.g == 0 and self.s == 0

    def last(self):
        return isinstance(self.g, int) and 2 * self.g + self.s == PAIRS - 1

    def slot_at(self, per_use, more=0):
        return self.g * per_use + more


STEPS = 5


def rounds(eng, body, until=PAIRS):
    def pairs(i):
        return [Pair((i - lag) // 2, (i - lag) % 2) if 0 <= i - lag < PAIRS else None for lag in range(STEPS)]

    ahead = STEPS // 2 + 1
    for i in range(2 * ahead):
        body(*pairs(i))
    with eng.Fori(1, until // 2 - ahead + 1) as n:
        for s in range(2):
            body(*(Pair(n + (ahead - 1 - (lag + 1 - s) // 2), (s - lag) % 2) for lag in range(STEPS)))
    for i in range(until, PAIRS + STEPS - 1):
        body(*pairs(i))


def tokens_to_experts(nc, x, h0, wkT, wrT, woT, decay, first, rw, rb, out, rows, lists, ends):
    ctx = ExitStack()

    def sb(name, shape, dt=F32):
        return ctx.enter_context(nc.sbuf_tensor(name, shape, dt))

    def ps(name, n=1):
        return ctx.enter_context(nc.psum_tensor(name, [P, 512 * n], F32))

    def sem(name):
        return ctx.enter_context(nc.semaphore(name))

    with ctx:
        wk, wr, wo = sb("wk", [P, HC, C]), sb("wr", [P, HC, C]), sb("wo", [P, HC, C])
        rws, rbs = sb("rws", [P, HC, E]), sb("rbs", [P, E])
        taps = sb("taps", [P, TAPS])
        dec, u = sb("dec", [P, HC]), sb("u", [P, HC])
        w, uw = sb("w", [P, HC]), sb("uw", [P, HC])
        wseq = sb("wseq", [P, SEQ, TP])
        diag = sb("diag", [P, P], I32)
        bandi = sb("bandi", [P, BAND1 + GAP + BAND2], I32)
        band, btmp = sb("band", [P, BANDS]), sb("btmp", [P, BAND1 + GAP + BAND2])
        ident = sb("ident", [P, P])
        before, ones = sb("before", [P, P], BF16), sb("ones", [P, P], BF16)
        filt = sb("filt", [P, K_FIRST, P])
        filt_rest = sb("filt_rest", [P, K_REST, 2, P])
        eid_i, eid = sb("eid_i", [P, E], I32), sb("eid", [P, E])
        reg_i = sb("reg_i", [P, E], I32)
        tok_i, tok = sb("tok_i", [P, 4], I32), sb("tok", [P, 3])
        c_eps, c_pow, c_neg = sb("c_eps", [P, 3]), sb("c_pow", [P, 3]), sb("c_neg", [P, 3])
        zrow, nobody = sb("zrow", [P, R * C]), sb("nobody", [P, LIST // P], U32)
        xin = sb("xin", [P, 2, 2, NKI, C])
        h = sb("h", [P, 3 * PAIRS, C])
        st1, st2 = sb("st1", [P, 3, 6]), sb("st2", [P, 3, 6])
        mv1, mv2 = sb("mv1", [P, 3, 2]), sb("mv2", [P, 3, 2])
        ve1, rs1, mr1, nb1 = (sb(n, [P, 3]) for n in ("ve1", "rs1", "mr1", "nb1"))
        ve2, rs2, mr2, nb2 = (sb(n, [P, 3]) for n in ("ve2", "rs2", "mr2", "nb2"))
        xn = sb("xn", [P, 3, C])
        xnT = sb("xnT", [P, HC, PAIR_TOK])
        kpad = sb("kpad", [P, 2, SEQ, TP])
        v, er = sb("v", [P, 2, SEQ, T]), sb("er", [P, SEQ * T])
        pp = sb("pp", [P, SEQ, TP])
        dl = sb("dl", [P, SEQ, T])
        up_s, dn_s = sb("up_s", [P, SEQ, T]), sb("dn_s", [P, SEQ, T])
        e1s, e2s, e2sv = sb("e1s", [P, SEQ, TP]), sb("e2s", [P, SEQ, TP]), sb("e2sv", [P, SEQ, TP])
        e1y, e2y = sb("e1y", [P, SEQ, T]), sb("e2y", [P, SEQ, T])
        sa, sb_ = sb("sa", [P, SEQ, TP]), sb("sbb", [P, SEQ, TP])
        t1, t2, t3 = (sb(n, [P, SEQ, T]) for n in ("t1", "t2", "t3"))
        num, den, dsg = (sb(n, [P, SEQ * T]) for n in ("num", "den", "dsg"))
        lnd, inv = sb("lnd", [P, SEQ * T]), sb("inv", [P, SEQ * T])
        oT = sb("oT", [P, HC, 3 * P])
        h1 = sb("h1", [P, 2, 3, C])
        xs = sb("xs", [P, 2, 3, ROW])
        x2T = sb("x2T", [P, HC, 3 * P])
        lg, eq, cand, oh1, lg2, cand2, oh2, place, pl1 = (
            sb(n, [P, 3, E]) for n in ("lg", "eq", "cand", "oh1", "lg2", "cand2", "oh2", "place", "pl1"))
        sel = sb("sel", [P, 3, E], BF16)
        m1, m2, i1, i2, dm, ed, ed1 = (sb(n, [P, 3]) for n in ("m1", "m2", "i1", "i2", "dm", "ed", "ed1"))
        slots, tid = sb("slots", [P, 2, 6], U32), sb("tid", [P, 2, 3], U32)

        conv_ps, wo_ps, kr_ps = ps("conv_ps", 2), ps("wo_ps", 2), [ps("kr_ps0"), ps("kr_ps1")]
        tp_ps, cnt_ps = ps("tp_ps"), ps("cnt_ps")
        lg_ps = cnt_ps[:, 0:24].rearrange("p (t e) -> p t e", e=E)
        rank_ps, tot_ps = cnt_ps[:, 32:56], cnt_ps[:, 64:72]

        params, loaded, tok_next = sem("params"), sem("loaded"), sem("tok_next")
        stats_seen, slots_seen, sp_seen, act_seen = sem("stats_seen"), sem("slots_seen"), sem("sp_seen"), sem("act_seen")
        iotas, consts, bands, filt_done, ready = sem("iotas"), sem("consts"), sem("bands"), sem("filt_done"), sem("ready")
        setup_act, pads = sem("setup_act"), sem("pads")
        x_loaded = [sem("x_loaded0"), sem("x_loaded1")]
        h1_stored = [sem("h1_stored0"), sem("h1_stored1")]
        rows_stored = [sem("rows_stored0"), sem("rows_stored1")]
        listed = [sem("listed0"), sem("listed1")]
        zeroed = sem("zeroed")
        conv_done, h_taken = sem("conv_done"), sem("h_taken")
        ln1, ln2 = sem("ln1"), sem("ln2")
        rstd1, rstd2 = sem("rstd1"), sem("rstd2")
        xn_ready, t1_done, t1_taken = sem("xn_ready"), sem("t1_done"), sem("t1_taken")
        kr_done, kr_taken, er_ready = sem("kr_done"), sem("kr_taken"), sem("er_ready")
        diffs, clamped, exps, state, t2_done, t3_done = sem("diffs"), sem("clamped"), sem("exps"), sem("state"), sem("t2_done"), sem("t3_done")
        inv_ready, o_ready, wo_done = sem("inv_ready"), sem("o_ready"), sem("wo_done")
        xn2_ready, t2T_done, t2T_taken = sem("xn2_ready"), sem("t2T_done"), sem("t2T_taken")
        lg_done, route, gate_exp, rank_done = sem("lg_done"), sem("route"), sem("gate_exp"), sem("rank_done")

        N_LN1, N_LN2, N_DIFF, N_STATE, N_ROUTE, N_RSTD = 6, 7, 7, 8, 25, 4

        def tile_of_h(q, t):
            return h[:, bass.ds(q.at(3, t), 1), :].rearrange("p a c -> p (a c)")

        block = ctx.enter_context(nc.Block())

        @block.sync
        def _(sp):
            sp.dma_start(taps[:, :], h0.rearrange("(a k) -> a k", a=1).partition_broadcast(P)).then_inc(params, 16)
            sp.dma_start(dec[:, :], decay).then_inc(params, 16)
            sp.dma_start(u[:, :], first).then_inc(params, 16)

            def end_of_waits():
                sp.sem_inc(sp_seen, 1)

            def load(q):
                if not isinstance(q.g, int) or q.g:
                    sp.wait_ge(conv_done, q.at(1, -1))
                    end_of_waits()
                for b in range(2):
                    for lo, n in ((0, K_FIRST), (K_FIRST, K_REST)):
                        src = x[bass.ds(q.at(2, b), 1), STARTS[lo]:STARTS[lo] + n * P, :].rearrange("a (s p) c -> (a p) s c", p=P)
                        sp.dma_start(xin[:, q.s, b, lo:lo + n], src).then_inc(x_loaded[q.s], 16)

            load(Pair(0, 0))
            for dst, src in ((wk, wkT), (wr, wrT), (wo, woT), (rws, rw)):
                sp.dma_start(dst[:, :, :], src.rearrange("(k p) n -> p k n", p=P)).then_inc(loaded, 16)
            sp.dma_start(rbs[:, :], rb.rearrange("(a k) -> a k", a=1).partition_broadcast(P)).then_inc(loaded, 16)
            load(Pair(0, 1))
            sp.wait_ge(pads, 2)
            sp.dma_start(lists.rearrange("(p n) a -> p (n a)", p=P), nobody[:, :]).then_inc(zeroed, 16)
            sp.dma_start(rows[NTOK:NTOK + 1, :], zrow[0:1, 0:ROW]).then_inc(zeroed, 16)
            sp.dma_start(out[NTOK:NTOK + TS, :].rearrange("(p r) c -> p (r c)", p=P),
                         zrow[:, :]).then_inc(zeroed, 16)

            def put(q, dst, src, done):
                seq = dst[bass.ds(q.at(PAIR_TOK), PAIR_TOK), :].rearrange("(b t) c -> b t c", b=2)
                sp.dma_start(seq[:, 0:P, :].rearrange("b t c -> t b c"), src[:, q.s, 0:2, :]).then_inc(done[q.s], 16)
                for b in range(2):
                    sp.dma_start(seq[b, P:T, :], src[b * REST:(b + 1) * REST, q.s, 2, :]).then_inc(done[q.s], 16)

            def body(p0, p1, p2, p3, p4):
                if p3:
                    sp.wait_ge(ln2, p3.at(N_LN2, 1))
                    end_of_waits()
                    put(p3, out, h1, h1_stored)
                if p4:
                    sp.wait_ge(route, p4.at(N_ROUTE, 21))
                    end_of_waits()
                    put(p4, rows, xs, rows_stored)
                if p0 and not (isinstance(p0.g, int) and p0.g == PAIRS // 2 - 1):
                    load(Pair(p0.g + 1, p0.s))

            rounds(sp, body, PAIRS - 2)
            sp.wait_ge(zeroed, 48)
            for s in range(2):
                sp.wait_ge(h1_stored[s], 48 * (PAIRS // 2))
                sp.wait_ge(rows_stored[s], 48 * (PAIRS // 2))
                sp.wait_ge(listed[s], 96 * (PAIRS // 2))

        @block.gpsimd
        def _(pool):
            pool.iota(diag[:, :], [[1, P]], base=0, channel_multiplier=-1).then_inc(iotas, 1)
            pool.iota(bandi[:, 0:BAND1 + GAP], [[1, BAND1 + GAP]], base=0, channel_multiplier=-2).then_inc(iotas, 1)
            pool.iota(bandi[:, BAND1 + GAP:], [[-2, BAND2]], base=LEFT, channel_multiplier=1).then_inc(iotas, 1)
            pool.iota(eid_i[:, :], [[1, E]], base=0, channel_multiplier=0).then_inc(iotas, 1)
            pool.iota(reg_i[:, :], [[REG, E]], base=0, channel_multiplier=0).then_inc(iotas, 1)
            pool.iota(tok_i[:, 0:2], [[T, 2]], base=0, channel_multiplier=1).then_inc(iotas, 1)
            pool.iota(tok_i[:, 2:4], [[P - REST, 2]], base=P, channel_multiplier=1).then_inc(iotas, 1)
            pool.memset(zrow[:, :], 0.0).then_inc(pads, 1)
            pool.memset(nobody[:, :], NTOK).then_inc(pads, 1)
            pool.memset(c_eps[:, :], EPS).then_inc(pads, 1)
            pool.memset(c_pow[:, :], -0.5).then_inc(pads, 1)
            pool.memset(c_neg[:, :], -1.0).then_inc(pads, 1)
            pool.memset(kpad[:, :, :, 0:1], NEG).then_inc(pads, 1)
            for pad in (e1s, e2s, e2sv):
                pool.memset(pad[:, :, 0:1], 0.0).then_inc(pads, 1)
            pool.wait_ge(pads, 9)

            def rstd(q, stats, n, mv, ve, rs, mr, nb, done):
                pool.wait_ge(stats, q.at(n, n))
                pool.wait_ge(done, q.at(N_RSTD))
                pool.tensor_tensor(ve[:, :], mv[:, :, 1], c_eps[:, :], ALU.add).then_inc(done, 1)
                pool.wait_ge(done, q.at(N_RSTD, 1))
                pool.tensor_tensor(rs[:, :], ve[:, :], c_pow[:, :], ALU.pow).then_inc(done, 1)
                pool.wait_ge(done, q.at(N_RSTD, 2))
                pool.tensor_tensor(mr[:, :], mv[:, :, 0], rs[:, :], ALU.mult).then_inc(done, 1)
                pool.wait_ge(done, q.at(N_RSTD, 3))
                pool.tensor_tensor(nb[:, :], mr[:, :], c_neg[:, :], ALU.mult).then_inc(done, 1)

            def body(p0, p1, p2, p3, p4):
                if p3:
                    rstd(p3, ln2, N_LN2, mv2, ve2, rs2, mr2, nb2, rstd2)
                if p2:
                    pool.wait_ge(exps, p2.at(4, 4))
                    pool.wait_ge(kr_taken, p2.at(4, 4))
                    pool.wait_ge(state, p2.at(N_STATE))
                    pool.tensor_tensor(t2[:, :, :], e2y[:, :, :], v[:, p2.s], ALU.mult).then_inc(t2_done, 1)
                    pool.wait_ge(state, p2.at(N_STATE, 2))
                    pool.tensor_tensor(t3[:, :, :], e1y[:, :, :], sb_[:, :, 0:T], ALU.mult).then_inc(t3_done, 1)
                if p0:
                    pool.wait_ge(xn_ready, p0.at(3))
                    rstd(p0, ln1, N_LN1, mv1, ve1, rs1, mr1, nb1, rstd1)
                if p4:
                    pool.wait_ge(route, p4.at(N_ROUTE, 24))
                    pool.sem_inc(slots_seen, 1)
                    for c in range(6):
                        pool.indirect_dma_start(lists, bass.IndirectOffsetOnAxis(slots[:, p4.s, c:c + 1], 0),
                                                tid[:, p4.s, c % 3:c % 3 + 1], None).then_inc(listed[p4.s], 16)

            pool.wait_ge(zeroed, 48)
            rounds(pool, body)

        @block.scalar
        def _(act):
            act.preload_act_table_set("natural_log_exp_and_others")
            act.wait_ge(params, 48)
            act.activation(w[:, :], dec[:, :], ACT.Exp).then_inc(setup_act, 1)

            def body(p0, p1, p2, p3, p4):
                if p1:
                    act.wait_ge(rstd1, p1.at(N_RSTD, N_RSTD))
                    act.wait_ge(t1_done, p1.at(HC))
                    act.sem_inc(act_seen, 1)
                    for t in range(3):
                        act.activation(xn[:, t, :], tile_of_h(p1, t), ACT.Identity,
                                       bias=nb1[:, t:t + 1], scale=rs1[:, t:t + 1]).then_inc(xn_ready, 1)
                if p2:
                    act.wait_ge(state, p2.at(N_STATE))
                    act.wait_ge(t3_done, p2.at(1))
                    act.wait_ge(kr_taken, p2.at(4, 4))
                    act.activation(er[:, :], v[:, p2.s].rearrange("p a t -> p (a t)"), ACT.Exp, scale=-1.0).then_inc(er_ready, 1)
                    for k, (src, dst, sc) in enumerate(((up_s, e1s, -1.0), (dn_s, e2s, 1.0))):
                        act.wait_ge(diffs, p2.at(N_DIFF, (5, 7)[k]))
                        act.activation(dst[:, :, 1:TP], src[:, :, :], ACT.Exp, scale=sc).then_inc(exps, 1)
                    act.wait_ge(diffs, p2.at(N_DIFF, 3))
                    for sign, dst in ((1.0, e1y), (-1.0, e2y)):
                        act.activation(dst[:, :, :], dl[:, :, :], ACT.Relu, scale=sign).then_inc(clamped, 1)
                if p1:
                    act.wait_ge(kr_done, p1.at(4))
                    for k in range(HC):
                        act.wait_ge(t1_done, p1.at(HC, k + 1))
                        act.activation(xnT[:, k, :], kr_ps[k][:, 0:PAIR_TOK], ACT.Copy).then_inc(t1_taken, 1)
                if p0:
                    act.wait_ge(conv_done, p0.at(1, 1))
                    act.sem_inc(act_seen, 1)
                    act.activation(h[:, bass.ds(p0.at(3), 3), :], conv_ps[:, 0:3 * C].rearrange("p (t c) -> p t c", c=C),
                                   ACT.Copy).then_inc(h_taken, 1)
                if p2:
                    for k, dst in enumerate((e1y, e2y)):
                        act.wait_ge(clamped, p2.at(2, k + 1))
                        act.activation(dst[:, :, :], dst[:, :, :], ACT.Exp, scale=-1.0).then_inc(exps, 1)
                if p4:
                    act.wait_ge(route, p4.at(N_ROUTE, 14))
                    act.activation(ed[:, :], dm[:, :], ACT.Exp).then_inc(gate_exp, 1)

                def kr(j):
                    k = j % 2
                    dst = (kpad[:, p1.s, 2 * k:2 * k + 2, 1:TP], v[:, p1.s, 2 * k:2 * k + 2, :])[j // 2]
                    act.wait_ge(kr_done, p1.at(4, j + 1))
                    act.activation(dst, kr_ps[k][:, 0:PAIR_TOK].rearrange("p (b t) -> p b t", b=2), ACT.Copy).then_inc(kr_taken, 1)

                if p1:
                    kr(0)
                if p3:
                    act.wait_ge(rstd2, p3.at(N_RSTD, N_RSTD))
                    act.wait_ge(rows_stored[p3.s], p3.slot_at(48))
                    for t in range(3):
                        act.activation(xs[:, p3.s, t, 0:C], h1[:, p3.s, t, :], ACT.Identity,
                                       bias=nb2[:, t:t + 1], scale=rs2[:, t:t + 1]).then_inc(xn2_ready, 1)
                if p1:
                    kr(1)
                for k in range(HC):
                    if p3:
                        act.wait_ge(lg_done, p3.at(1))
                        act.wait_ge(t2T_done, p3.at(HC, k + 1))
                        act.activation(x2T[:, k, :], tp_ps[:, 0:3 * P], ACT.Copy).then_inc(t2T_taken, 1)
                    if p1:
                        kr(2 + k)
                if p2:
                    act.wait_ge(state, p2.at(N_STATE, 8))
                    act.activation(lnd[:, :], dsg[:, :], ACT.Ln).then_inc(inv_ready, 1)
                    act.wait_ge(inv_ready, p2.at(2, 1))
                    act.wait_ge(o_ready, p2.at(2))
                    act.activation(inv[:, :], lnd[:, :], ACT.Exp, scale=-1.0).then_inc(inv_ready, 1)

            rounds(act, body)

        @block.tensor
        def _(pe):
            pe.wait_ge(bands, 15)
            for s, start in enumerate(STARTS):
                o, n = (0, P) if s < K_FIRST else (P, REST)
                dst = conv_ps[:, s * P:(s + 1) * P] if s < K_FIRST else conv_ps[:, 512 + (s - K_FIRST) * REST:512 + (s - K_FIRST + 1) * REST]
                qs = [q for q in range(NKM) if -P < start - 2 * KM * q + LEFT < BAND1]
                for q in qs:
                    a = AT1 + start - 2 * KM * q + LEFT
                    b = AT2 - (KM // 2) * q + o
                    last = pe.matmul(dst, band[0:KM, a:a + P], band[0:KM, b:b + n], start=q == qs[0], stop=q == qs[-1])
            last.then_inc(filt_done, 1)
            pe.wait_ge(ready, 1)
            pe.wait_ge(loaded, 16 * 5)
            pe.wait_ge(consts, 13)

            def transposes(src, dst, done, k, by_sequence):
                for t in range(3):
                    o = dst[:, t * P:(t + 1) * P]
                    if by_sequence:
                        o = dst[:, t * T:t * T + P] if t < 2 else dst[:, 0:PAIR_TOK].rearrange("p (b t) -> p b t", b=2)[:, :, P:T]
                    last = pe.transpose(o, src[:, t, k * P:(k + 1) * P], ident[:, :])
                last.then_inc(done, 1)

            def conv_first(q):
                pe.wait_ge(x_loaded[q.s], q.slot_at(64, 64))
                pe.wait_ge(h_taken, q.at(1))
                for b in range(2):
                    for s in range(K_FIRST):
                        pe.matmul(conv_ps[:, b * C:(b + 1) * C], filt[:, s, :], xin[:, q.s, b, s, :],
                                  start=s == 0, stop=s == K_FIRST - 1)

            def conv_rest(q):
                for b in range(2):
                    for s in range(K_REST):
                        last = pe.matmul(conv_ps[:, 2 * C:3 * C], filt_rest[:, s, b, :], xin[:, q.s, b, K_FIRST + s, :],
                                         start=b == 0 and s == 0, stop=b == 1 and s == K_REST - 1)
                last.then_inc(conv_done, 1)

            def project(q):
                pe.wait_ge(o_ready, q.at(2, 2))
                pe.wait_ge(ln2, q.at(N_LN2))
                for t in range(3):
                    for k in range(HC):
                        last = pe.matmul(wo_ps[:, t * C:(t + 1) * C], oT[:, k, t * P:(t + 1) * P], wo[:, k, :], start=k == 0, stop=k == HC - 1)
                last.then_inc(wo_done, 1)

            def kr(q, j):
                pe.wait_ge(kr_taken, q.at(4, max(0, j - 1)))
                m = j % 2
                for k in range(HC):
                    last = pe.matmul(kr_ps[m][:, 0:PAIR_TOK], (wk, wr)[j // 2][:, k, m * P:(m + 1) * P], xnT[:, k, :],
                                     start=k == 0, stop=k == HC - 1)
                last.then_inc(kr_done, 1)

            def body(p0, p1, p2, p3, p4):
                if p0:
                    conv_first(p0)
                if p3:
                    project(p3)
                if p1:
                    pe.wait_ge(xn_ready, p1.at(3, 3))
                    pe.wait_ge(kr_taken, p1.at(4))
                    for k in range(HC):
                        transposes(xn, kr_ps[k], t1_done, k, True)
                if p0:
                    conv_rest(p0)
                if p4:
                    ranks(p4)
                if p1:
                    pe.wait_ge(t1_taken, p1.at(HC, HC))
                    kr(p1, 0)
                    kr(p1, 1)
                for k in range(HC):
                    if p3:
                        pe.wait_ge(xn2_ready, p3.at(3, 3))
                        pe.wait_ge(t2T_taken, p3.at(HC, k))
                        transposes(xs[:, p3.s], tp_ps, t2T_done, k, False)
                    if p1:
                        kr(p1, 2 + k)
                if p3:
                    pe.wait_ge(t2T_taken, p3.at(HC, HC))
                    pe.wait_ge(route, p3.at(N_ROUTE))
                    for t in range(3):
                        for k in range(HC):
                            last = pe.matmul(cnt_ps[:, t * E:(t + 1) * E], x2T[:, k, t * P:(t + 1) * P], rws[:, k, :],
                                             start=k == 0, stop=k == HC - 1)
                    last.then_inc(lg_done, 1)

            def ranks(q):
                pe.wait_ge(route, q.at(N_ROUTE, 13))
                flat = sel[:, :, :].rearrange("p t e -> p (t e)")
                pe.matmul(rank_ps[:, 2 * E:3 * E], ones[:, :], flat[:, 0:E], start=True, stop=False, skip_group_check=True)
                pe.matmul(rank_ps[:, E:3 * E], ones[:, :], flat[:, 0:2 * E], start=False, stop=False, skip_group_check=True)
                pe.matmul(rank_ps, before[:, :], flat, start=False, stop=True, skip_group_check=True)
                for t in range(3):
                    last = pe.matmul(tot_ps, ones[:, :], sel[:, t, :], start=t == 0, stop=t == 2)
                last.then_inc(rank_done, 1)

            rounds(pe, body)

        @block.vector
        def _(dve):
            dve.memset(band[:, :], 0.0).then_inc(consts, 1)
            dve.wait_ge(iotas, 7)
            dve.tensor_scalar(ident[:, :], diag[:, :], 0.0, None, ALU.is_equal).then_inc(consts, 1)
            dve.tensor_scalar(before[:, :], diag[:, :], 0.0, None, ALU.is_gt).then_inc(consts, 1)
            dve.memset(ones[:, :], 1.0).then_inc(consts, 1)
            dve.memset(wseq[:, :, :], 0.0).then_inc(consts, 1)
            dve.memset(filt_rest[:, :, :, :], 0.0).then_inc(consts, 1)
            dve.tensor_copy(eid[:, :], eid_i[:, :]).then_inc(consts, 1)
            dve.tensor_copy(ends[:, :], reg_i[:, :]).then_inc(consts, 1)
            dve.tensor_copy(tok[:, 0:2], tok_i[:, 0:2]).then_inc(consts, 1)
            dve.tensor_copy(tok[0:REST, 2:3], tok_i[0:REST, 2:3]).then_inc(consts, 1)
            dve.wait_ge(consts, 10)
            dve.tensor_scalar(tok[REST:P, 2:3], tok_i[REST:P, 2:3], float(T - REST), None, ALU.add).then_inc(consts, 1)
            dve.wait_ge(params, 48)
            active = band[:, AT1:AT2 + BAND2]
            dve.tensor_scalar(active, bandi[:, :], 0.0, taps[:, 0:1], ALU.is_equal, ALU.mult).then_inc(bands, 1)
            for k in range(1, TAPS):
                dve.wait_ge(bands, 2 * k - 1)
                dve.tensor_scalar(btmp[:, :], bandi[:, :], float(k), taps[:, k:k + 1], ALU.is_equal, ALU.mult).then_inc(bands, 1)
                dve.wait_ge(bands, 2 * k)
                dve.tensor_tensor(active, active, btmp[:, :], ALU.add).then_inc(bands, 1)
            dve.wait_ge(setup_act, 1)
            dve.tensor_scalar(w[:, :], w[:, :], -1.0, None, ALU.mult).then_inc(consts, 1)
            dve.wait_ge(consts, 12)
            dve.tensor_tensor(uw[:, :], u[:, :], w[:, :], ALU.add).then_inc(consts, 1)
            for k in range(HC):
                dve.tensor_scalar(wseq[:, 2 * k:2 * k + 2, :], wseq[:, 2 * k:2 * k + 2, :], w[:, k:k + 1], None, ALU.add).then_inc(consts, 1)
            dve.wait_ge(consts, 15)
            dve.memset(wseq[:, :, 0:1], -3e38).then_inc(consts, 1)
            dve.wait_ge(filt_done, 1)
            dve.tensor_copy(filt[:, :, :], conv_ps[:, 0:K_FIRST * P].rearrange("p (s t) -> p s t", t=P)).then_inc(consts, 1)
            rest = conv_ps[:, 512:512 + K_REST * REST].rearrange("p (s t) -> p s t", t=REST)
            for b in range(2):
                dve.tensor_copy(filt_rest[:, :, b, b * REST:(b + 1) * REST], rest).then_inc(consts, 1)
            dve.wait_ge(consts, 19)
            dve.memset(btmp[:, 0:1], 0.0).then_inc(ready, 1)
            dve.wait_ge(pads, 9)
            dve.wait_ge(loaded, 16 * 5)

            def aggregate(q, st, mv, n, at, done):
                dve.wait_ge(done, q.at(n, at))
                dve.sem_inc(stats_seen, 1)
                for t in range(3):
                    dve.bn_aggr(mv[:, t, :], st[:, t, :]).then_inc(done, 1)

            def flat(a):
                return a[:, :, :].rearrange("p a t -> p (a t)")

            def body(p0, p1, p2, p3, p4):
                def route_to(k):
                    if p4:
                        while routed[0] < k:
                            router[routed[0]](p4)
                            routed[0] += 1

                routed = [0]
                if p2:
                    dve.wait_ge(kr_taken, p2.at(4, 2))
                    dve.wait_ge(diffs, p2.at(N_DIFF))
                    dve.tensor_tensor_scan(flat(pp), flat(wseq), kpad[:, p2.s].rearrange("p a t -> p (a t)"), NEG,
                                           ALU.add, ALU.max).then_inc(diffs, 1)
                route_to(1)
                if p2:
                    dve.wait_ge(clamped, p2.at(2))
                    for k in range(HC):
                        dve.wait_ge(diffs, p2.at(N_DIFF, 1))
                        a = slice(2 * k, 2 * k + 2)
                        dve.scalar_tensor_tensor(out=dl[:, a, :], in0=kpad[:, p2.s, a, 1:TP], scalar=u[:, k:k + 1], in1=pp[:, a, 0:T],
                                                 op0=ALU.add, op1=ALU.subtract).then_inc(diffs, 1)
                        route_to(2 + k)
                if p3:
                    dve.wait_ge(inv_ready, p3.at(2, 2))
                    dve.wait_ge(wo_done, p3.at(1))
                    for n, (a, o) in enumerate(((slice(0, P), oT[:, :, 0:2 * P]), (slice(P, T), oT[:, :, 2 * P:3 * P]))):
                        dve.tensor_tensor(o.rearrange("p k (b t) -> p k b t", b=2), *(
                            i[:, :].rearrange("p (k b t) -> p k b t", k=HC, b=2)[:, :, :, a] for i in (num, inv)),
                            ALU.mult).then_inc(o_ready, 1)
                        route_to(4 + n)
                if p2:
                    dve.wait_ge(exps, p2.at(4))
                    for n, (dst, op) in enumerate(((up_s, ALU.max), (dn_s, ALU.min))):
                        for k in range(HC):
                            dve.wait_ge(diffs, p2.at(N_DIFF, 2 + k))
                            a = slice(2 * k, 2 * k + 2)
                            dve.tensor_scalar(dst[:, a, :], dl[:, a, :], uw[:, k:k + 1], 0.0, ALU.subtract, op).then_inc(diffs, 1)
                            route_to(6 + 2 * n + k)
                route_to(14)
                if p3:
                    dve.wait_ge(wo_done, p3.at(1, 1))
                    dve.wait_ge(h1_stored[p3.s], p3.slot_at(48))
                    dve.wait_ge(xn2_ready, p3.at(3))
                    dve.tensor_tensor(h1[:, p3.s], wo_ps[:, 0:3 * C].rearrange("p (t c) -> p t c", c=C),
                                      h[:, bass.ds(p3.at(3), 3), :], ALU.add).then_inc(ln2, 1)
                    route_to(15)
                    dve.wait_ge(ln2, p3.at(N_LN2, 1))
                    dve.wait_ge(rstd2, p3.at(N_RSTD))
                    for t in range(3):
                        dve.bn_stats(st2[:, t, :], h1[:, p3.s, t, :]).then_inc(ln2, 1)
                        route_to(16)
                    aggregate(p3, st2, mv2, N_LN2, 4, ln2)
                if p2:
                    dve.wait_ge(exps, p2.at(4, 2))
                    dve.wait_ge(kr_taken, p2.at(4, 4))
                    dve.wait_ge(state, p2.at(N_STATE))
                    dve.tensor_tensor(e2sv[:, :, 1:TP], e2s[:, :, 1:TP], v[:, p2.s], ALU.mult).then_inc(state, 1)
                    dve.wait_ge(t3_done, p2.at(1))
                    dve.tensor_tensor_scan(flat(sb_), flat(e1s), flat(e2s), 0.0, ALU.mult, ALU.add).then_inc(state, 1)
                    route_to(18)
                    dve.wait_ge(state, p2.at(N_STATE, 1))
                    dve.tensor_tensor_scan(flat(sa), flat(e1s), flat(e2sv), 0.0, ALU.mult, ALU.add).then_inc(state, 1)
                route_to(20)
                if p2:
                    dve.wait_ge(exps, p2.at(4, 3))
                    dve.wait_ge(state, p2.at(N_STATE, 3))
                    dve.tensor_tensor(t1[:, :, :], e1y[:, :, :], sa[:, :, 0:T], ALU.mult).then_inc(state, 1)
                if p0:
                    dve.wait_ge(h_taken, p0.at(1, 1))
                    dve.wait_ge(ln1, p0.at(N_LN1))
                    dve.sem_inc(stats_seen, 1)
                    for t in range(3):
                        dve.bn_stats(st1[:, t, :], tile_of_h(p0, t)).then_inc(ln1, 1)
                        route_to(21 + t)
                    dve.wait_ge(rstd1, p0.at(N_RSTD))
                    aggregate(p0, st1, mv1, N_LN1, 3, ln1)
                route_to(N_ROUTE)
                if p2:
                    dve.wait_ge(er_ready, p2.at(1, 1))
                    dve.tensor_scalar(er[:, :], er[:, :], EMAX, 1.0, ALU.min, ALU.add).then_inc(state, 1)
                    dve.wait_ge(t2_done, p2.at(1, 1))
                    dve.wait_ge(state, p2.at(N_STATE, 4))
                    dve.wait_ge(o_ready, p2.at(2))
                    dve.tensor_tensor(num[:, :], flat(t1), flat(t2), ALU.add).then_inc(state, 1)
                    dve.wait_ge(t3_done, p2.at(1, 1))
                    dve.wait_ge(exps, p2.at(4, 4))
                    dve.tensor_tensor(den[:, :], flat(t3), flat(e2y), ALU.add).then_inc(state, 1)
                    dve.wait_ge(state, p2.at(N_STATE, 7))
                    dve.wait_ge(inv_ready, p2.at(2))
                    dve.tensor_tensor(dsg[:, :], den[:, :], er[:, :], ALU.mult).then_inc(state, 1)

            def over_e(a):
                return a.unsqueeze(2).to_broadcast([P, 3, E])

            def over_t(a):
                return a.unsqueeze(1).to_broadcast([P, 3, E])

            def route_step(ins):
                ins.then_inc(route, 1)

            def after(q, k):
                dve.wait_ge(route, q.at(N_ROUTE, k))

            def logits(q):
                dve.wait_ge(lg_done, q.at(1, 1))
                after(q, 0)
                route_step(dve.tensor_tensor(lg[:, :, :], lg_ps, over_t(rbs[:, :]), ALU.add))

            def best(q):
                after(q, 1)
                route_step(dve.tensor_reduce(m1[:, :], lg[:, :, :], AX.X, ALU.max))

            def is_best(q):
                after(q, 2)
                route_step(dve.tensor_tensor(eq[:, :, :], lg[:, :, :], over_e(m1[:, :]), ALU.is_equal))

            def best_numbers(q):
                after(q, 3)
                route_step(dve.scalar_tensor_tensor(out=cand[:, :, :], in0=eq[:, :, :], scalar=-float(E), in1=over_t(eid[:, :]),
                                                    op0=ALU.mult, op1=ALU.add))

            def first_number(q):
                after(q, 4)
                route_step(dve.tensor_reduce(i1[:, :], cand[:, :, :], AX.X, ALU.min))

            def is_first(q):
                after(q, 5)
                route_step(dve.tensor_tensor(oh1[:, :, :], cand[:, :, :], over_e(i1[:, :]), ALU.is_equal))

            def other_logits(q):
                after(q, 6)
                route_step(dve.scalar_tensor_tensor(out=lg2[:, :, :], in0=oh1[:, :, :], scalar=-3e38, in1=lg[:, :, :],
                                                    op0=ALU.mult, op1=ALU.add))

            def second(q):
                after(q, 7)
                route_step(dve.tensor_reduce(m2[:, :], lg2[:, :, :], AX.X, ALU.max))

            def is_second_best(q):
                after(q, 8)
                route_step(dve.tensor_tensor(eq[:, :, :], lg2[:, :, :], over_e(m2[:, :]), ALU.is_equal))

            def second_numbers(q):
                after(q, 9)
                route_step(dve.scalar_tensor_tensor(out=cand2[:, :, :], in0=eq[:, :, :], scalar=-float(E), in1=over_t(eid[:, :]),
                                                    op0=ALU.mult, op1=ALU.add))

            def second_number(q):
                after(q, 10)
                route_step(dve.tensor_reduce(i2[:, :], cand2[:, :, :], AX.X, ALU.min))

            def is_second(q):
                after(q, 11)
                route_step(dve.tensor_tensor(oh2[:, :, :], cand2[:, :, :], over_e(i2[:, :]), ALU.is_equal))

            def selected(q):
                after(q, 12)
                route_step(dve.tensor_tensor(sel[:, :, :], oh1[:, :, :], oh2[:, :, :], ALU.add))

            def difference(q):
                route_step(dve.tensor_tensor(dm[:, :], m2[:, :], m1[:, :], ALU.subtract))

            def first_expert(q):
                dve.wait_ge(rows_stored[q.s], q.slot_at(48))
                route_step(dve.tensor_scalar(xs[:, q.s, :, C + 2], i1[:, :], float(E), None, ALU.add))

            def numbers(q):
                dve.wait_ge(tok_next, q.at(1))
                dve.wait_ge(listed[q.s], q.slot_at(96))
                route_step(dve.tensor_copy(tid[:, q.s, :], tok[:, :]))

            def gate_sum(q):
                dve.wait_ge(gate_exp, q.at(1, 1))
                route_step(dve.tensor_scalar(ed1[:, :], ed[:, :], 1.0, None, ALU.add))

            def places(q):
                dve.wait_ge(rank_done, q.at(1, 1))
                route_step(dve.tensor_tensor(place[:, :, :], rank_ps.rearrange("p (t e) -> p t e", e=E), over_t(ends[:, :]), ALU.add))

            def first_gate(q):
                after(q, 17)
                route_step(dve.reciprocal(xs[:, q.s, :, C], ed1[:, :]))

            def first_places(q):
                after(q, 18)
                route_step(dve.tensor_tensor(pl1[:, :, :], place[:, :, :], oh1[:, :, :], ALU.mult))

            def second_gate(q):
                after(q, 19)
                route_step(dve.tensor_tensor(xs[:, q.s, :, C + 1], ed[:, :], xs[:, q.s, :, C], ALU.mult))

            def second_places(q):
                route_step(dve.tensor_tensor(lg2[:, :, :], place[:, :, :], oh2[:, :, :], ALU.mult))

            def first_place(q):
                after(q, 20)
                with nc.allow_low_precision("whole numbers"):
                    route_step(dve.tensor_reduce(slots[:, q.s, 0:3], pl1[:, :, :], AX.X, ALU.add))

            def second_place(q):
                after(q, 22)
                with nc.allow_low_precision("whole numbers"):
                    route_step(dve.tensor_reduce(slots[:, q.s, 3:6], lg2[:, :, :], AX.X, ALU.add))

            def new_ends(q):
                route_step(dve.tensor_tensor(ends[:, :], tot_ps, ends[:, :], ALU.add))
                after(q, 16)
                dve.tensor_scalar(tok[:, :], tok[:, :], float(PAIR_TOK), None, ALU.add).then_inc(tok_next, 1)

            router = [logits, best, is_best, best_numbers, first_number, is_first, other_logits, second, is_second_best,
                      second_numbers, second_number, is_second, selected, difference, first_expert, numbers, gate_sum,
                      places, first_gate, first_places, second_gate, second_places, first_place, second_place, new_ends]
            assert len(router) == N_ROUTE
            rounds(dve, body)
            dve.wait_ge(route, N_ROUTE * PAIRS)




def tiles(eng, first, body, last):
    first()
    for s in range(2):
        body(Pair(0, s))
    with eng.Fori(1, (NT - 1) // 2) as n:
        for s in range(2):
            body(Pair(n, s))
    if NT % 2 == 0:
        body(Pair(NT // 2 - 1, 0))
    last(Pair((NT - 1) // 2, (NT - 1) % 2))


def experts(nc, ew, b2, out, rows, lists, ends):
    ctx = ExitStack()

    def sb(name, shape, dt=F32):
        return ctx.enter_context(nc.sbuf_tensor(name, shape, dt))

    def ps(name):
        return ctx.enter_context(nc.psum_tensor(name, [P, 512], F32))

    def sem(name):
        return ctx.enter_context(nc.semaphore(name))

    with ctx:
        NC = NT + 1
        jcol_i, jcol = sb("jcol_i", [P, NC], I32), sb("jcol", [P, NC])
        e_i, e_no = sb("e2_i", [P, E], I32), sb("e2_no", [P, E])
        lim_i, part_i, part = sb("lim_i", [P, MAXT], I32), sb("part_i", [P, R + 1], I32), sb("part", [P, R + 1])
        cnt, nts, ends_t, start_t, onesE = (sb(n, [P, E]) for n in ("cnt", "nts", "ends_t", "start_t", "onesE"))
        grp_e = sb("grp_e", [P, E])
        more = sb("more", [P, E, MAXT])
        past, oh, pick = (sb(n, [P, NC, E]) for n in ("past", "oh", "pick"))
        ej, ecl, grp, live, idx_f = (sb(n, [P, NC]) for n in ("ej", "ecl", "grp", "live", "idx_f"))
        table = sb("table", [P, NC, 3], U32)
        ident, ident_i = sb("ident2", [P, P]), sb("ident2_i", [P, P], I32)
        idx = sb("idx", [P, 2, 3], U32)
        raw = sb("raw", [P, 2, WROW])
        whi, wlo = sb("whi", [P, 2, B1AT], F32R), sb("wlo", [P, 2, B1AT], F32R)
        b1, b2s = sb("b1", [P, 2, FC]), sb("b2s", [P, 2, C])
        tid = sb("tid2", [P, 2, R], U32)
        xg = sb("xg", [P, 2, R, ROW])
        xhi, xlo = sb("xhi", [P, 2, HC, TS], F32R), sb("xlo", [P, 2, HC, TS], F32R)
        hid = sb("hid", [P, 2, TS])
        hhi, hlo = sb("hhi", [P, 4, TS], F32R), sb("hlo", [P, 4, TS], F32R)
        ysum, yout = sb("ysum", [P, 2, R, C]), sb("yout", [P, 2, R, C])
        tk, tk2, gA, gB = (sb(n, [P, R]) for n in ("tk", "tk2", "gA", "gB"))
        gate, dest = sb("gate", [P, 2, R]), sb("dest", [P, 2, R], U32)

        acc = [ps(f"acc{i}") for i in range(R)]
        hp = [ps("hp0"), ps("hp1")]
        xt = [ps("xt0"), ps("xt1")]

        iotas, tab = sem("iotas2"), sem("tab")
        idx_ready, waits_over = sem("idx_ready"), sem("waits_over")
        w_in, tid_in, x_in, b2_in, y_sent = ([sem(f"{n}{s}") for s in range(2)] for n in ("w_in", "tid_in", "x_in", "b2_in", "y_sent"))
        xt_done, xhi_done, xlo_done = sem("xt_done"), sem("xhi_done"), sem("xlo_done")
        whi_done, wlo_done, b1_done = sem("whi_done"), sem("wlo_done"), sem("b1_done")
        hp_done, hid_done, hhi_done, hlo_done = sem("hp_done"), sem("hid_done"), sem("hhi_done"), sem("hlo_done")
        acc_done, y_taken, y_ready, marks = sem("acc_done"), sem("y_taken"), sem("y_ready"), sem("marks")
        N_MARK = 6
        PIECE = B1AT // FC

        block = ctx.enter_context(nc.Block())

        def nxt(j):
            return Pair(j.g, 1) if j.s == 0 else Pair(j.g + 1, 0)

        def prev(j):
            return Pair(j.g - 1, 1) if j.s == 0 else Pair(j.g, 0)

        @block.gpsimd
        def _(pool):
            pool.iota(jcol_i[:, :], [[1, NC]], base=0, channel_multiplier=0).then_inc(iotas, 1)
            pool.iota(e_i[:, :], [[1, E]], base=0, channel_multiplier=0).then_inc(iotas, 1)
            pool.iota(lim_i[:, :], [[TS, MAXT]], base=0, channel_multiplier=0).then_inc(iotas, 1)
            pool.iota(part_i[:, 0:R], [[1, R]], base=0, channel_multiplier=R).then_inc(iotas, 1)
            pool.iota(part_i[:, R:R + 1], [[0, 1]], base=0, channel_multiplier=1).then_inc(iotas, 1)
            pool.iota(ident_i[:, :], [[1, P]], base=0, channel_multiplier=-1).then_inc(iotas, 1)
            groups = lists.rearrange("(g r) a -> g (r a)", r=R)

            def end_of_waits():
                pool.sem_inc(waits_over, 1)

            def gather_w(j):
                pool.indirect_dma_start(raw[:, j.s, :], None, ew, bass.IndirectOffsetOnAxis(idx[:, j.s, 0:1], 0)).then_inc(w_in[j.s], 16)

            def gather_tid(j):
                pool.indirect_dma_start(tid[:, j.s, :], None, groups, bass.IndirectOffsetOnAxis(idx[:, j.s, 1:2], 0)).then_inc(tid_in[j.s], 16)

            def gather_x(j):
                pool.wait_ge(tid_in[j.s], j.slot_at(16, 16))
                end_of_waits()
                for r in range(R):
                    pool.indirect_dma_start(xg[:, j.s, r, :], None, rows,
                                            bass.IndirectOffsetOnAxis(tid[:, j.s, r:r + 1], 0)).then_inc(x_in[j.s], 16)

            def gather_b2(j):
                pool.indirect_dma_start(b2s[:, j.s, :], None, b2, bass.IndirectOffsetOnAxis(idx[:, j.s, 2:3], 0)).then_inc(b2_in[j.s], 16)

            def first():
                pool.wait_ge(idx_ready, 1)
                gather_tid(Pair(0, 0))
                gather_w(Pair(0, 0))
                pool.wait_ge(idx_ready, 2)
                gather_tid(Pair(0, 1))
                gather_x(Pair(0, 0))
                gather_b2(Pair(0, 0))
                gather_w(Pair(0, 1))
                gather_x(Pair(0, 1))

            def body(j):
                after = Pair(j.g + 1, j.s)
                pool.wait_ge(idx_ready, after.at(1, 1))
                pool.wait_ge(wlo_done, j.at(FC, FC))
                pool.wait_ge(b1_done, j.at(1, 1))
                pool.wait_ge(marks, j.at(N_MARK, N_MARK))
                pool.wait_ge(x_in[j.s], j.slot_at(16 * R, 16 * R))
                end_of_waits()
                gather_w(after)
                gather_tid(after)
                pool.wait_ge(y_taken, j.at(R))
                end_of_waits()
                gather_b2(nxt(j))
                pool.wait_ge(xt_done, j.at(HC, HC))
                if not j.first():
                    send(prev(j))
                gather_x(after)

            def send(j):
                pool.wait_ge(y_ready, j.at(R, R))
                if not j.first():
                    pool.wait_ge(y_sent[1 - j.s], prev(j).slot_at(16 * R, 16 * R))
                end_of_waits()
                for r in range(R):
                    pool.indirect_dma_start(out[:, :], bass.IndirectOffsetOnAxis(dest[:, j.s, r:r + 1], 0),
                                            yout[:, j.s, r, :], None, compute_op=ALU.add).then_inc(y_sent[j.s], 16)

            def last(j):
                send(prev(j))
                send(j)
                pool.wait_ge(y_sent[j.s], j.slot_at(16 * R, 16 * R))
                pool.wait_ge(w_in[1 - j.s], 16 * (NC // 2))
                pool.wait_ge(tid_in[1 - j.s], 16 * (NC // 2))
                pool.wait_ge(x_in[1 - j.s], 16 * R * (NC // 2))

            tiles(pool, first, body, last)

        @block.scalar
        def _(act):
            def x_high(j, k):
                act.wait_ge(xt_done, j.at(HC, k + 1))
                act.activation(xhi[:, j.s, k, :], xt[k][:, 0:TS], ACT.Copy).then_inc(xhi_done, 1)

            def w_high(j, k):
                act.activation(whi[:, j.s, k * PIECE:(k + 1) * PIECE], raw[:, j.s, k * PIECE:(k + 1) * PIECE], ACT.Copy).then_inc(whi_done, 1)

            def first():
                act.wait_ge(w_in[0], 16)
                for k in range(FC):
                    w_high(Pair(0, 0), k)
                for k in range(HC):
                    x_high(Pair(0, 0), k)

            def gated(j):
                for r in range(R):
                    act.wait_ge(y_taken, j.at(R, r + 1))
                    act.wait_ge(marks, j.at(N_MARK, N_MARK))
                    act.wait_ge(y_sent[j.s], j.slot_at(16 * R))
                    act.activation(yout[:, j.s, r, :], ysum[:, j.s, r, :], ACT.Copy, scale=gate[:, j.s, r:r + 1]).then_inc(y_ready, 1)

            def body(j, more=True):
                n = nxt(j)
                for c in range(FC):
                    act.wait_ge(hp_done, j.at(FC, c + 1))
                    if c < 2:
                        act.wait_ge(hlo_done, j.at(FC))
                        act.wait_ge(b1_done, j.at(1, 1))
                    else:
                        act.wait_ge(hlo_done, j.at(FC, c - 1))
                    act.activation(hid[:, c % 2, :], hp[c % 2][:, 0:TS], ACT.Relu, bias=b1[:, j.s, c:c + 1]).then_inc(hid_done, 1)
                    if c == 1 and not j.first():
                        gated(prev(j))
                    if more:
                        if c == 0:
                            act.wait_ge(w_in[n.s], n.slot_at(16, 16))
                            act.wait_ge(acc_done, j.at(1))
                        w_high(n, c)
                        if c in (5, 6):
                            x_high(n, c - 5)
                if not more:
                    gated(j)

            tiles(act, first, body, lambda j: body(j, False))

        @block.tensor
        def _(pe):
            pe.wait_ge(tab, 2)

            def transposes(j):
                pe.wait_ge(x_in[j.s], j.slot_at(16 * R, 16 * R))
                pe.wait_ge(xlo_done, j.at(HC))
                for k in range(HC):
                    for r in range(R):
                        last = pe.transpose(xt[k][:, r * P:(r + 1) * P], xg[:, j.s, r, k * P:(k + 1) * P], ident[:, :])
                    last.then_inc(xt_done, 1)

            def up(j, c):
                pe.wait_ge(hid_done, j.at(FC, max(0, c - 1)))
                n = 0
                for k in range(HC):
                    at = k * FF + c * P
                    for w_, x_ in ((whi, xhi), (wlo, xhi), (whi, xlo)):
                        last = pe.matmul(hp[c % 2][:, 0:TS], w_[:, j.s, at:at + P], x_[:, j.s, k, :], start=n == 0, stop=n == 3 * HC - 1)
                        n += 1
                last.then_inc(hp_done, 1)

            def down(j, c):
                pe.wait_ge(hlo_done, j.at(FC, c + 1))
                if c == 0:
                    pe.wait_ge(y_taken, j.at(R))
                at = W2AT + c * C
                for r in range(R):
                    for n, (h_, w_) in enumerate(((hhi, whi), (hhi, wlo), (hlo, whi))):
                        last = pe.matmul(acc[r][:, 0:C], h_[:, c % 4, r * P:(r + 1) * P], w_[:, j.s, at:at + C],
                                         start=c == 0 and n == 0, stop=c == FC - 1 and n == 2)
                return last

            def body(j, more=True):
                pe.wait_ge(wlo_done, j.at(FC, FC))
                pe.wait_ge(xlo_done, j.at(HC, HC))
                for c in range(FC):
                    up(j, c)
                    if c >= 2:
                        down(j, c - 2)
                    if c == 4 and more:
                        transposes(nxt(j))
                down(j, FC - 2)
                down(j, FC - 1).then_inc(acc_done, 1)

            tiles(pe, lambda: transposes(Pair(0, 0)), body, lambda j: body(j, False))

        @block.vector
        def _(dve):
            def over_tiles(a):
                return a.unsqueeze(1).to_broadcast([P, NC, E])

            def over_e(a, n=NC):
                return a.unsqueeze(2).to_broadcast([P, n, E])

            steps = [0]

            def step(ins, wait=True):
                steps[0] += 1
                ins.then_inc(tab, 1)
                if wait:
                    dve.wait_ge(tab, steps[0])

            dve.wait_ge(iotas, 6)
            step(dve.tensor_copy(jcol[:, :], jcol_i[:, :]), False)
            step(dve.tensor_scalar(ident[:, :], ident_i[:, :], 0.0, None, ALU.is_equal), False)
            step(dve.tensor_copy(e_no[:, :], e_i[:, :]), False)
            step(dve.tensor_copy(part[:, :], part_i[:, :]))
            step(dve.scalar_tensor_tensor(out=cnt[:, :], in0=e_no[:, :], scalar=-float(REG), in1=ends[:, :], op0=ALU.mult, op1=ALU.add))
            step(dve.tensor_tensor(more[:, :, :], cnt[:, :].unsqueeze(2).to_broadcast([P, E, MAXT]),
                                   lim_i[:, :].unsqueeze(1).to_broadcast([P, E, MAXT]), ALU.is_gt))
            step(dve.tensor_reduce(nts[:, :], more[:, :, :], AX.X, ALU.add))
            step(dve.memset(onesE[:, :], 1.0))
            step(dve.tensor_tensor_scan(ends_t[:, :], onesE[:, :], nts[:, :], 0.0, ALU.mult, ALU.add))
            step(dve.tensor_tensor(start_t[:, :], ends_t[:, :], nts[:, :], ALU.subtract))
            step(dve.tensor_scalar(grp_e[:, :], e_no[:, :], float(REG // R), None, ALU.mult))
            step(dve.scalar_tensor_tensor(out=grp_e[:, :], in0=start_t[:, :], scalar=-float(P), in1=grp_e[:, :], op0=ALU.mult, op1=ALU.add))
            step(dve.tensor_tensor(past[:, :, :], over_e(jcol[:, :]), over_tiles(ends_t[:, :]), ALU.is_ge))
            step(dve.tensor_reduce(ej[:, :], past[:, :, :], AX.X, ALU.add))
            step(dve.tensor_tensor(oh[:, :, :], over_tiles(e_no[:, :]), over_e(ej[:, :]), ALU.is_equal))
            step(dve.tensor_tensor(pick[:, :, :], oh[:, :, :], over_tiles(grp_e[:, :]), ALU.mult))
            step(dve.tensor_reduce(grp[:, :], pick[:, :, :], AX.X, ALU.add))
            step(dve.scalar_tensor_tensor(out=grp[:, :], in0=jcol[:, :], scalar=float(P), in1=grp[:, :], op0=ALU.mult, op1=ALU.add))
            step(dve.tensor_scalar(live[:, :], ej[:, :], float(E), None, ALU.is_lt))
            step(dve.tensor_scalar(idx_f[:, :], grp[:, :], part[:, R:R + 1], -float(NOGRP), ALU.add, ALU.add))
            step(dve.tensor_tensor(idx_f[:, :], idx_f[:, :], live[:, :], ALU.mult))
            step(dve.tensor_scalar(table[:, :, 1], idx_f[:, :], float(NOGRP), None, ALU.add))
            step(dve.tensor_scalar(ecl[:, :], ej[:, :], float(E - 1), None, ALU.min))
            step(dve.tensor_copy(table[:, :, 2], ecl[:, :]))
            step(dve.tensor_scalar(table[:, :, 0], ecl[:, :], float(P), part[:, R:R + 1], ALU.mult, ALU.add))

            def indices(j):
                dve.tensor_copy(idx[:, j.s, :].unsqueeze(1), table[:, bass.ds(j.at(1), 1), :]).then_inc(idx_ready, 1)

            def w_low(j, k):
                a = slice(k * PIECE, (k + 1) * PIECE)
                dve.wait_ge(whi_done, j.at(FC, k + 1))
                dve.tensor_tensor(wlo[:, j.s, a], raw[:, j.s, a], whi[:, j.s, a].bitcast(F32), ALU.subtract).then_inc(wlo_done, 1)

            def x_low(j, k):
                dve.wait_ge(xhi_done, j.at(HC, k + 1))
                dve.tensor_tensor(xlo[:, j.s, k, :], xt[k][:, 0:TS], xhi[:, j.s, k, :].bitcast(F32), ALU.subtract).then_inc(xlo_done, 1)

            def bias(j):
                dve.tensor_copy(b1[:, j.s, :], raw[:, j.s, B1AT:WROW]).then_inc(b1_done, 1)

            def mark(j):
                def after(k):
                    dve.wait_ge(marks, j.at(N_MARK, k))

                e_j = ej[:, bass.ds(j.at(1), 1)]
                dve.wait_ge(tid_in[j.s], j.slot_at(16, 16))
                dve.wait_ge(x_in[j.s], j.slot_at(16 * R, 16 * R))
                after(0)
                dve.scalar_tensor_tensor(out=tk[:, :], in0=tid[:, j.s, :], scalar=-float(NTOK), in1=part[:, 0:R],
                                         op0=ALU.add, op1=ALU.subtract).then_inc(marks, 1)
                dve.scalar_tensor_tensor(out=gA[:, :], in0=xg[:, j.s, :, C + 2], scalar=e_j, in1=xg[:, j.s, :, C],
                                         op0=ALU.is_equal, op1=ALU.mult).then_inc(marks, 1)
                dve.scalar_tensor_tensor(out=gB[:, :], in0=xg[:, j.s, :, C + 2], scalar=e_j, in1=xg[:, j.s, :, C + 1],
                                         op0=ALU.not_equal, op1=ALU.mult).then_inc(marks, 1)
                after(1)
                dve.scalar_tensor_tensor(out=tk2[:, :], in0=tid[:, j.s, :], scalar=float(NTOK), in1=tk[:, :],
                                         op0=ALU.is_lt, op1=ALU.mult).then_inc(marks, 1)
                after(3)
                dve.tensor_tensor(gate[:, j.s, :], gA[:, :], gB[:, :], ALU.add).then_inc(marks, 1)
                after(4)
                dve.scalar_tensor_tensor(out=dest[:, j.s, :], in0=tk2[:, :], scalar=float(NTOK), in1=part[:, 0:R],
                                         op0=ALU.add, op1=ALU.add).then_inc(marks, 1)

            def first():
                indices(Pair(0, 0))
                indices(Pair(0, 1))
                mark(Pair(0, 0))
                dve.wait_ge(w_in[0], 16)
                bias(Pair(0, 0))
                for k in range(FC):
                    w_low(Pair(0, 0), k)
                for k in range(HC):
                    x_low(Pair(0, 0), k)

            def body(j, more=True):
                n = nxt(j)
                for c in range(FC):
                    dve.wait_ge(hid_done, j.at(FC, c + 1))
                    if c < 4:
                        dve.wait_ge(acc_done, j.at(1))
                    else:
                        dve.wait_ge(hp_done, j.at(FC, c - 1))
                    dve.tensor_copy(hhi[:, c % 4, :], hid[:, c % 2, :]).then_inc(hhi_done, 1)
                    dve.wait_ge(hhi_done, j.at(FC, c + 1))
                    dve.tensor_tensor(hlo[:, c % 4, :], hid[:, c % 2, :], hhi[:, c % 4, :].bitcast(F32), ALU.subtract).then_inc(hlo_done, 1)
                    if more:
                        if c == 0:
                            dve.wait_ge(w_in[n.s], n.slot_at(16, 16))
                            bias(n)
                        w_low(n, c)
                        if c == 1:
                            dve.wait_ge(w_in[j.s], j.slot_at(16, 16))
                            dve.wait_ge(tid_in[j.s], j.slot_at(16, 16))
                            dve.wait_ge(b2_in[j.s], j.slot_at(16, 16))
                            indices(Pair(j.g + 1, j.s))
                        if c in (6, 7):
                            x_low(n, c - 6)
                        if c == 7:
                            if not j.first():
                                dve.wait_ge(y_ready, j.at(R))
                                dve.wait_ge(y_sent[n.s], prev(j).slot_at(16 * R, 16 * R))
                            mark(n)
                dve.wait_ge(acc_done, j.at(1, 1))
                dve.wait_ge(b2_in[j.s], j.slot_at(16, 16))
                dve.wait_ge(y_ready, prev(j).at(R) if not j.first() else 0)
                for r in range(R):
                    dve.tensor_tensor(ysum[:, j.s, r, :], acc[r][:, 0:C], b2s[:, j.s, :], ALU.add).then_inc(y_taken, 1)

            tiles(dve, first, body, lambda j: body(j, False))


def audio_tower(nc, x, h0, wkT, wrT, woT, decay, first, rw, rb, ew, b2, out):
    rows = nc.dram_tensor("token_rows", (NTOK + 1, ROW), F32, kind="Internal").ap()
    lists = nc.dram_tensor("expert_lists", (LIST, 1), U32, kind="Internal").ap()
    with nc.sbuf_tensor("region_ends", [P, E], F32) as ends:
        tokens_to_experts(nc, x, h0, wkT, wrT, woT, decay, first, rw, rb, out, rows, lists, ends)
        experts(nc, ew, b2, out, rows, lists, ends)


def kernel(x, L0_tok_h0, L0_attn_Wk, L0_attn_Wr, L0_attn_Wo, L0_attn_time_decay, L0_attn_time_first,
           L0_ffn_router_w, L0_ffn_router_b, L0_ffn_W1, L0_ffn_b1, L0_ffn_W2, L0_ffn_b2):
    import numpy as np
    import concourse.bacc as bacc
    from concourse.bass_utils import run_bass_kernel_spmd

    def arr(a):
        return np.asarray(a)

    w1 = arr(L0_ffn_W1).reshape(E, HC, P, FF).transpose(0, 2, 1, 3).reshape(E, P, HC * FF)
    w2 = arr(L0_ffn_W2).reshape(E, FC, P, C).transpose(0, 2, 1, 3).reshape(E, P, FC * C)
    b1 = arr(L0_ffn_b1).reshape(E, FC, P).transpose(0, 2, 1)
    ins = {
        "x": arr(x), "h0": arr(L0_tok_h0),
        "wkT": arr(L0_attn_Wk).T, "wrT": arr(L0_attn_Wr).T, "woT": arr(L0_attn_Wo).T,
        "decay": arr(L0_attn_time_decay).reshape(HC, P).T, "first": arr(L0_attn_time_first).reshape(HC, P).T,
        "rw": arr(L0_ffn_router_w), "rb": arr(L0_ffn_router_b),
        "ew": np.concatenate([w1, w2, b1], axis=2).reshape(E * P, WROW), "b2": arr(L0_ffn_b2),
    }
    nc = bacc.Bacc("TRN2", target_bir_lowering=False, num_devices=1)
    arrays, args = {}, {}
    for name, a in ins.items():
        arrays[f"in_{name}"] = np.ascontiguousarray(a)
        args[name] = nc.dram_tensor(f"in_{name}", a.shape, mybir.dt.from_np(a.dtype), kind="ExternalInput").ap()
    out = nc.dram_tensor("out_rows", (NTOK + TS, C), F32, kind="ExternalOutput").ap()
    audio_tower(nc, **args, out=out)
    r = run_bass_kernel_spmd(nc, [arrays], core_ids=[0])
    return r.results[0]["out_rows"][0:NTOK].reshape(B, T, C)
```

```python
from contextlib import ExitStack

import concourse.bass as bass
from concourse import mybir

ALU = mybir.AluOpType
ACT = mybir.ActivationFunctionType
F32 = mybir.dt.float32
F32R = mybir.dt.float32r
BF16 = mybir.dt.bfloat16
I32 = mybir.dt.int32
U32 = mybir.dt.uint32
AX = mybir.AxisListType

P = 128
B, T_IN, C = 32, 750, 256
TAPS = 8
T_MID = (T_IN + TAPS - 1) // 2
T = (T_MID + TAPS - 1) // 2
LEFT = TAPS - 2
NTOK = B * T
PAIRS = B // 2
HC = C // P
SEQ = 2 * HC
TP = T + 1
REST = T - P
K_FIRST = (4 * (P - 1) + 4) // P
K_REST = -(-(T_IN - (4 * P - 3 * LEFT)) // P)
STARTS = [P * n for n in range(K_FIRST)] + [T_IN - P * (K_REST - n) for n in range(K_REST)]
NKI = len(STARTS)
assert K_FIRST * P > 4 * (P - 1) + 3 and STARTS[K_FIRST] <= 4 * P - 3 * LEFT
KM, NKM = 126, 3
PAIR_TOK = 2 * T
E, FF = 8, 1024
FC = FF // P
TS = 384
R = TS // P
NT = (2 * NTOK + E * (TS - 1)) // TS
MAXT = NTOK // TS
REG = NTOK + TS
NC = NT + 1
ROW = C + 3
LIST = E * REG + TS
NOGRP = E * REG // R
WROW = 2 * FF + FC * C + FC
W2AT, B1AT = 2 * FF, 2 * FF + FC * C
NEG = -1e38
EPS = 1e-5
EMAX = 2.0 ** 54
BAND1, BAND2 = 2 * P + 2 * KM + LEFT, 4 * KM + 2 * T
TAP0 = P + 2 * (KM - 1)
TAPR = LEFT + KM - 1 + 2 * KM
ROW1, ROW2 = BAND1 + 2 * (KM - 1), BAND2 + KM - 1


class Pair:

    def __init__(self, g, s):
        self.g, self.s = g, s

    def at(self, per_pair, more=0):
        return self.g * (2 * per_pair) + (per_pair * self.s + more)

    def first(self):
        return isinstance(self.g, int) and self.g == 0 and self.s == 0

    def last(self):
        return isinstance(self.g, int) and 2 * self.g + self.s == PAIRS - 1

    def slot_at(self, per_use, more=0):
        return self.g * per_use + more


STEPS = 5


class Tables:

    def __init__(self, nc, ctx):
        def sb(name, shape, dt=F32):
            return ctx.enter_context(nc.sbuf_tensor(name, shape, dt))

        self.jcol_i, self.jcol = sb("jcol_i", [P, NC], I32), sb("jcol", [P, NC])
        self.lim_i = sb("lim_i", [P, MAXT], I32)
        self.part_i, self.part = sb("part_i", [P, R + 1], I32), sb("part", [P, R + 1])
        self.ej = sb("ej", [P, NC])
        self.table = sb("table", [P, NC, 3], U32)
        self.ident = sb("ident", [P, P])


def rounds(eng, body, until=PAIRS):
    def pairs(i):
        return [Pair((i - lag) // 2, (i - lag) % 2) if 0 <= i - lag < PAIRS else None for lag in range(STEPS)]

    ahead = STEPS // 2 + 1
    for i in range(2 * ahead):
        body(*pairs(i))
    with eng.Fori(1, until // 2 - ahead + 1) as n:
        for s in range(2):
            body(*(Pair(n + (ahead - 1 - (lag + 1 - s) // 2), (s - lag) % 2) for lag in range(STEPS)))
    for i in range(until, PAIRS + STEPS - 1):
        body(*pairs(i))


def tokens_to_experts(nc, x, taps, taps_down, wkT, wrT, woT, decay, first, rw, rb, out, rows, lists, tables):
    ctx = ExitStack()

    def sb(name, shape, dt=F32):
        return ctx.enter_context(nc.sbuf_tensor(name, shape, dt))

    def ps(name, n=1):
        return ctx.enter_context(nc.psum_tensor(name, [P, 512 * n], F32))

    def sem(name):
        return ctx.enter_context(nc.semaphore(name))

    with ctx:
        wk, wr, wo = sb("wk", [P, HC, C]), sb("wr", [P, HC, C]), sb("wo", [P, HC, C])
        rws, rbs = sb("rws", [P, HC, E]), sb("rbs", [P, E])
        dec, u = sb("dec", [P, HC]), sb("u", [P, HC])
        w, uw, nuw = sb("w", [P, HC]), sb("uw", [P, HC]), sb("nuw", [P, HC])
        wseq = sb("wseq", [P, SEQ, TP])
        diag = sb("diag", [P, P], I32)
        band1, band2 = sb("band1", [P, BAND1]), sb("band2", [P, BAND2])
        ident = tables.ident
        before, ones = sb("before", [P, P], BF16), sb("ones", [P, P], BF16)
        filt = sb("filt", [P, K_FIRST, P])
        filt_rest = sb("filt_rest", [P, K_REST, 2, P])
        eid_i, eid = sb("eid_i", [P, E], I32), sb("eid", [P, E])
        reg_i = sb("reg_i", [P, E], I32)
        ends = sb("region_ends", [P, E])
        tok_i, tok = sb("tok_i", [P, 4], I32), sb("tok", [P, 3])
        c_eps, c_pow, c_neg = sb("c_eps", [P, 3]), sb("c_pow", [P, 3]), sb("c_neg", [P, 3])
        zrow, nobody = sb("zrow", [P, R * C]), sb("nobody", [P, LIST // P], U32)
        xin = sb("xin", [P, 2, 2, NKI, C])
        h = sb("h", [P, 3 * PAIRS, C])
        st1, st2 = sb("st1", [P, 3, 6]), sb("st2", [P, 3, 6])
        mv1, mv2 = sb("mv1", [P, 3, 2]), sb("mv2", [P, 3, 2])
        ve1, rs1, mr1, nb1 = (sb(n, [P, 3]) for n in ("ve1", "rs1", "mr1", "nb1"))
        ve2, rs2, mr2, nb2 = (sb(n, [P, 3]) for n in ("ve2", "rs2", "mr2", "nb2"))
        xn = sb("xn", [P, 3, C])
        xnT = sb("xnT", [P, HC, PAIR_TOK])
        kpad = sb("kpad", [P, 2, SEQ, TP])
        v, er = sb("v", [P, 2, SEQ, T]), sb("er", [P, SEQ * T])
        pp = sb("pp", [P, SEQ, TP])
        dl = sb("dl", [P, SEQ, T])
        up_s, dn_s = sb("up_s", [P, SEQ, T]), sb("dn_s", [P, SEQ, T])
        e1s, e2s, e2sv = sb("e1s", [P, SEQ, TP]), sb("e2s", [P, SEQ, TP]), sb("e2sv", [P, SEQ, TP])
        e1y, e2y = sb("e1y", [P, SEQ, T]), sb("e2y", [P, SEQ, T])
        sa, sb_ = sb("sa", [P, SEQ, TP]), sb("sbb", [P, SEQ, TP])
        t1, t2, t3 = (sb(n, [P, SEQ, T]) for n in ("t1", "t2", "t3"))
        num, den, dsg = (sb(n, [P, SEQ * T]) for n in ("num", "den", "dsg"))
        lnd, inv = sb("lnd", [P, SEQ * T]), sb("inv", [P, SEQ * T])
        oT = sb("oT", [P, HC, 3 * P])
        h1 = sb("h1", [P, 2, 3, C])
        xs = sb("xs", [P, 2, 3, ROW])
        x2T = sb("x2T", [P, HC, 3 * P])
        lg, eq, cand, oh1, lg2, cand2, oh2, place, pl1 = (
            sb(n, [P, 3, E]) for n in ("lg", "eq", "cand", "oh1", "lg2", "cand2", "oh2", "place", "pl1"))
        sel = sb("sel", [P, 3, E], BF16)
        m1, m2, i1, i2, dm, ed, ed1 = (sb(n, [P, 3]) for n in ("m1", "m2", "i1", "i2", "dm", "ed", "ed1"))
        slots, tid = sb("slots", [P, 2, 6], U32), sb("tid", [P, 2, 3], U32)

        jcol_i, jcol, lim_i, part_i, part = tables.jcol_i, tables.jcol, tables.lim_i, tables.part_i, tables.part
        ej, table, e_no = tables.ej, tables.table, eid
        cnt, nts, ends_t, start_t, onesE = (sb(n, [P, E]) for n in ("cnt", "nts", "ends_t", "start_t", "onesE"))
        grp_e = sb("grp_e", [P, E])
        more = sb("more", [P, E, MAXT])
        past, oh, pick = (sb(n, [P, NC, E]) for n in ("past", "oh", "pick"))
        ecl, grp, live, idx_f = (sb(n, [P, NC]) for n in ("ecl", "grp", "live", "idx_f"))

        conv_ps, wo_ps, kr_ps = ps("conv_ps", 2), ps("wo_ps", 2), [ps("kr_ps0"), ps("kr_ps1")]
        tp_ps, cnt_ps = ps("tp_ps"), ps("cnt_ps")
        x2_ps = tp_ps[:, 0:3 * P], wo_ps[:, 512:512 + 3 * P]
        lg_ps = cnt_ps[:, 0:24].rearrange("p (t e) -> p t e", e=E)
        rank_ps, tot_ps = cnt_ps[:, 32:56], cnt_ps[:, 64:72]

        params, loaded, tok_next = sem("params"), sem("loaded"), sem("tok_next")
        stats_seen, slots_seen, sp_seen, act_seen = sem("stats_seen"), sem("slots_seen"), sem("sp_seen"), sem("act_seen")
        tab = sem("tab")
        iotas, consts, bands, filt_done, ready = sem("iotas"), sem("consts"), sem("bands"), sem("filt_done"), sem("ready")
        setup_act, pads = sem("setup_act"), sem("pads")
        x_loaded = [sem("x_loaded0"), sem("x_loaded1")]
        h1_stored = [sem("h1_stored0"), sem("h1_stored1")]
        rows_stored = [sem("rows_stored0"), sem("rows_stored1")]
        listed = [sem("listed0"), sem("listed1")]
        zeroed = sem("zeroed")
        conv_done, h_taken = sem("conv_done"), sem("h_taken")
        ln1, ln2 = sem("ln1"), sem("ln2")
        rstd1, rstd2 = sem("rstd1"), sem("rstd2")
        xn_ready, t1_done, t1_taken = sem("xn_ready"), sem("t1_done"), sem("t1_taken")
        kr_done, kr_taken, er_ready = sem("kr_done"), sem("kr_taken"), sem("er_ready")
        diffs, clamped, exps, state, t2_done, t3_done = sem("diffs"), sem("clamped"), sem("exps"), sem("state"), sem("t2_done"), sem("t3_done")
        inv_ready, o_ready, wo_done = sem("inv_ready"), sem("o_ready"), sem("wo_done")
        xn2_ready, t2T_done, t2T_taken = sem("xn2_ready"), sem("t2T_done"), sem("t2T_taken")
        lg_done, route, gate_exp, rank_done = sem("lg_done"), sem("route"), sem("gate_exp"), sem("rank_done")

        N_LN1, N_LN2, N_DIFF, N_STATE, N_ROUTE, N_RSTD = 6, 7, 5, 8, 25, 4

        def tile_of_h(q, t):
            return h[:, bass.ds(q.at(3, t), 1), :].rearrange("p a c -> p (a c)")

        block = ctx.enter_context(nc.Block())

        @block.sync
        def _(sp):
            for dst, src, step in ((band1, taps, 2), (band2, taps_down, 1)):
                sp.dma_start(dst[0:KM, :], bass.AP(src.tensor, src.offset, [[step, KM], [1, dst.shape[1]]])).then_inc(bands, 16)
            sp.dma_start(dec[:, :], decay).then_inc(params, 16)
            sp.dma_start(u[:, :], first).then_inc(params, 16)

            def end_of_waits():
                sp.sem_inc(sp_seen, 1)

            def load(q):
                if not isinstance(q.g, int) or q.g:
                    sp.wait_ge(conv_done, q.at(1, -1))
                    end_of_waits()
                for b in range(2):
                    for lo, n in ((0, K_FIRST), (K_FIRST, K_REST)):
                        src = x[bass.ds(q.at(2, b), 1), STARTS[lo]:STARTS[lo] + n * P, :].rearrange("a (s p) c -> (a p) s c", p=P)
                        sp.dma_start(xin[:, q.s, b, lo:lo + n], src).then_inc(x_loaded[q.s], 16)

            load(Pair(0, 0))
            for dst, src in ((wk, wkT), (wr, wrT), (wo, woT), (rws, rw)):
                sp.dma_start(dst[:, :, :], src.rearrange("(k p) n -> p k n", p=P)).then_inc(loaded, 16)
            sp.dma_start(rbs[:, :], rb.rearrange("(a k) -> a k", a=1).partition_broadcast(P)).then_inc(loaded, 16)
            load(Pair(0, 1))
            sp.wait_ge(pads, 2)
            sp.dma_start(lists.rearrange("(p n) a -> p (n a)", p=P), nobody[:, :]).then_inc(zeroed, 16)
            sp.dma_start(rows[NTOK:NTOK + 1, :], zrow[0:1, 0:ROW]).then_inc(zeroed, 16)
            sp.dma_start(out[NTOK:NTOK + TS, :].rearrange("(p r) c -> p (r c)", p=P),
                         zrow[:, :]).then_inc(zeroed, 16)

            def put(q, dst, src, done):
                seq = dst[bass.ds(q.at(PAIR_TOK), PAIR_TOK), :].rearrange("(b t) c -> b t c", b=2)
                sp.dma_start(seq[:, 0:P, :].rearrange("b t c -> t b c"), src[:, q.s, 0:2, :]).then_inc(done[q.s], 16)
                for b in range(2):
                    sp.dma_start(seq[b, P:T, :], src[b * REST:(b + 1) * REST, q.s, 2, :]).then_inc(done[q.s], 16)

            def body(p0, p1, p2, p3, p4):
                if p3:
                    sp.wait_ge(ln2, p3.at(N_LN2, 1))
                    end_of_waits()
                    put(p3, out, h1, h1_stored)
                if p4:
                    sp.wait_ge(route, p4.at(N_ROUTE, 21))
                    end_of_waits()
                    put(p4, rows, xs, rows_stored)
                if p0 and not (isinstance(p0.g, int) and p0.g == PAIRS // 2 - 1):
                    load(Pair(p0.g + 1, p0.s))

            rounds(sp, body, PAIRS - 2)
            sp.wait_ge(zeroed, 48)
            for s in range(2):
                sp.wait_ge(h1_stored[s], 48 * (PAIRS // 2))
                sp.wait_ge(rows_stored[s], 48 * (PAIRS // 2))
                sp.wait_ge(listed[s], 96 * (PAIRS // 2))

        @block.gpsimd
        def _(pool):
            pool.iota(diag[:, :], [[1, P]], base=0, channel_multiplier=-1).then_inc(iotas, 1)
            pool.iota(eid_i[:, :], [[1, E]], base=0, channel_multiplier=0).then_inc(iotas, 1)
            pool.iota(reg_i[:, :], [[REG, E]], base=0, channel_multiplier=0).then_inc(iotas, 1)
            pool.iota(tok_i[:, 0:2], [[T, 2]], base=0, channel_multiplier=1).then_inc(iotas, 1)
            pool.iota(tok_i[:, 2:4], [[P - REST, 2]], base=P, channel_multiplier=1).then_inc(iotas, 1)
            pool.iota(jcol_i[:, :], [[1, NC]], base=0, channel_multiplier=0).then_inc(iotas, 1)
            pool.iota(lim_i[:, :], [[TS, MAXT]], base=0, channel_multiplier=0).then_inc(iotas, 1)
            pool.iota(part_i[:, 0:R], [[1, R]], base=0, channel_multiplier=R).then_inc(iotas, 1)
            pool.iota(part_i[:, R:R + 1], [[0, 1]], base=0, channel_multiplier=1).then_inc(iotas, 1)
            pool.memset(zrow[:, :], 0.0).then_inc(pads, 1)
            pool.memset(nobody[:, :], NTOK).then_inc(pads, 1)
            pool.memset(c_eps[:, :], EPS).then_inc(pads, 1)
            pool.memset(c_pow[:, :], -0.5).then_inc(pads, 1)
            pool.memset(c_neg[:, :], -1.0).then_inc(pads, 1)
            pool.memset(kpad[:, :, :, 0:1], NEG).then_inc(pads, 1)
            for pad in (e1s, e2s, e2sv):
                pool.memset(pad[:, :, 0:1], 0.0).then_inc(pads, 1)
            pool.wait_ge(pads, 9)

            def rstd(q, stats, n, mv, ve, rs, mr, nb, done):
                pool.wait_ge(stats, q.at(n, n))
                pool.wait_ge(done, q.at(N_RSTD))
                pool.tensor_tensor(ve[:, :], mv[:, :, 1], c_eps[:, :], ALU.add).then_inc(done, 1)
                pool.wait_ge(done, q.at(N_RSTD, 1))
                pool.tensor_tensor(rs[:, :], ve[:, :], c_pow[:, :], ALU.pow).then_inc(done, 1)
                pool.wait_ge(done, q.at(N_RSTD, 2))
                pool.tensor_tensor(mr[:, :], mv[:, :, 0], rs[:, :], ALU.mult).then_inc(done, 1)
                pool.wait_ge(done, q.at(N_RSTD, 3))
                pool.tensor_tensor(nb[:, :], mr[:, :], c_neg[:, :], ALU.mult).then_inc(done, 1)

            def body(p0, p1, p2, p3, p4):
                if p2:
                    pool.wait_ge(exps, p2.at(4, 3))
                    pool.wait_ge(kr_taken, p2.at(4, 4))
                    pool.wait_ge(state, p2.at(N_STATE))
                    pool.tensor_tensor(t2[:, :, :], e2y[:, :, :], v[:, p2.s], ALU.mult).then_inc(t2_done, 1)
                if p3:
                    rstd(p3, ln2, N_LN2, mv2, ve2, rs2, mr2, nb2, rstd2)
                if p2:
                    pool.wait_ge(exps, p2.at(4, 4))
                    pool.wait_ge(state, p2.at(N_STATE, 2))
                    pool.tensor_tensor(t3[:, :, :], e1y[:, :, :], sb_[:, :, 0:T], ALU.mult).then_inc(t3_done, 1)
                if p0:
                    pool.wait_ge(xn_ready, p0.at(3))
                    rstd(p0, ln1, N_LN1, mv1, ve1, rs1, mr1, nb1, rstd1)
                if p4:
                    pool.wait_ge(route, p4.at(N_ROUTE, 24))
                    pool.sem_inc(slots_seen, 1)
                    for c in range(6):
                        pool.indirect_dma_start(lists, bass.IndirectOffsetOnAxis(slots[:, p4.s, c:c + 1], 0),
                                                tid[:, p4.s, c % 3:c % 3 + 1], None).then_inc(listed[p4.s], 16)

            pool.wait_ge(zeroed, 48)
            rounds(pool, body)

        @block.scalar
        def _(act):
            act.preload_act_table_set("natural_log_exp_and_others")
            act.wait_ge(params, 32)
            act.activation(w[:, :], dec[:, :], ACT.Exp).then_inc(setup_act, 1)

            act.wait_ge(consts, 13)

            def body(p0, p1, p2, p3, p4):
                if p2:
                    act.wait_ge(state, p2.at(N_STATE))
                    act.wait_ge(t3_done, p2.at(1))
                    for k in range(HC):
                        act.wait_ge(diffs, p2.at(N_DIFF, 2 + k))
                        a = slice(2 * k, 2 * k + 2)
                        act.activation(up_s[:, a, :], dl[:, a, :], ACT.Relu, bias=nuw[:, k:k + 1]).then_inc(clamped, 1)
                    act.wait_ge(diffs, p2.at(N_DIFF, 5))
                    act.activation(e2s[:, :, 1:TP], dn_s[:, :, :], ACT.Exp).then_inc(exps, 1)
                    act.wait_ge(clamped, p2.at(4, 2))
                    act.activation(e1s[:, :, 1:TP], up_s[:, :, :], ACT.Exp, scale=-1.0).then_inc(exps, 1)
                if p1:
                    act.wait_ge(kr_done, p1.at(4))
                    for k in range(HC):
                        act.wait_ge(t1_done, p1.at(HC, k + 1))
                        act.activation(xnT[:, k, :], kr_ps[k][:, 0:PAIR_TOK], ACT.Copy).then_inc(t1_taken, 1)
                if p2:
                    for sign, dst in ((-1.0, e2y), (1.0, e1y)):
                        act.activation(dst[:, :, :], dl[:, :, :], ACT.Relu, scale=sign).then_inc(clamped, 1)
                    for k, dst in enumerate((e2y, e1y)):
                        act.wait_ge(clamped, p2.at(4, k + 3))
                        act.activation(dst[:, :, :], dst[:, :, :], ACT.Exp, scale=-1.0).then_inc(exps, 1)
                    act.wait_ge(kr_taken, p2.at(4, 4))
                    act.activation(er[:, :], v[:, p2.s].rearrange("p a t -> p (a t)"), ACT.Exp, scale=-1.0).then_inc(er_ready, 1)
                if p0:
                    act.wait_ge(conv_done, p0.at(1, 1))
                    act.sem_inc(act_seen, 1)
                    act.activation(h[:, bass.ds(p0.at(3), 3), :], conv_ps[:, 0:3 * C].rearrange("p (t c) -> p t c", c=C),
                                   ACT.Copy).then_inc(h_taken, 1)
                if p4:
                    act.wait_ge(route, p4.at(N_ROUTE, 14))
                    act.activation(ed[:, :], dm[:, :], ACT.Exp).then_inc(gate_exp, 1)

                def kr(j):
                    k = j % 2
                    dst = (kpad[:, p1.s, 2 * k:2 * k + 2, 1:TP], v[:, p1.s, 2 * k:2 * k + 2, :])[j // 2]
                    act.wait_ge(kr_done, p1.at(4, j + 1))
                    act.activation(dst, kr_ps[k][:, 0:PAIR_TOK].rearrange("p (b t) -> p b t", b=2), ACT.Copy).then_inc(kr_taken, 1)

                if p1:
                    kr(0)
                    kr(1)
                if p3:
                    act.wait_ge(rstd2, p3.at(N_RSTD, N_RSTD))
                    act.wait_ge(rows_stored[p3.s], p3.slot_at(48))
                    for t in range(3):
                        act.activation(xs[:, p3.s, t, 0:C], h1[:, p3.s, t, :], ACT.Identity,
                                       bias=nb2[:, t:t + 1], scale=rs2[:, t:t + 1]).then_inc(xn2_ready, 1)
                for k in range(HC):
                    if p3:
                        act.wait_ge(lg_done, p3.at(1))
                        act.wait_ge(t2T_done, p3.at(HC, k + 1))
                        act.activation(x2T[:, k, :], x2_ps[k], ACT.Copy).then_inc(t2T_taken, 1)
                    if p0 and k == 1:
                        act.wait_ge(rstd1, p0.at(N_RSTD, N_RSTD))
                        act.wait_ge(t1_done, p0.at(HC))
                        act.sem_inc(act_seen, 1)
                        for t in range(3):
                            act.activation(xn[:, t, :], tile_of_h(p0, t), ACT.Identity,
                                           bias=nb1[:, t:t + 1], scale=rs1[:, t:t + 1]).then_inc(xn_ready, 1)
                    if p1:
                        kr(2 + k)
                if p2:
                    act.wait_ge(state, p2.at(N_STATE, 8))
                    act.activation(lnd[:, :], dsg[:, :], ACT.Ln).then_inc(inv_ready, 1)
                    act.wait_ge(inv_ready, p2.at(2, 1))
                    act.wait_ge(o_ready, p2.at(2))
                    act.activation(inv[:, :], lnd[:, :], ACT.Exp, scale=-1.0).then_inc(inv_ready, 1)

            rounds(act, body)

        @block.tensor
        def _(pe):
            pe.wait_ge(bands, 32)
            mats = []
            for s, start in enumerate(STARTS):
                o, n = (0, P) if s < K_FIRST else (P, REST)
                dst = conv_ps[:, s * P:(s + 1) * P] if s < K_FIRST else conv_ps[:, 512 + (s - K_FIRST) * REST:512 + (s - K_FIRST + 1) * REST]
                for q in range(NKM):
                    a = P + start - 2 * KM * q + LEFT
                    if 0 < a < BAND1 - P:
                        b = 2 * KM + 2 * o - KM * q
                        mats.append((dst, band1[0:KM, a:a + P], band2[0:KM, b:b + 2 * n:2], s))
            for i, (dst, lhs, rhs, s) in enumerate(mats):
                last = pe.matmul(dst, lhs, rhs, start=i == 0 or mats[i - 1][3] != s, stop=i == len(mats) - 1 or mats[i + 1][3] != s)
            last.then_inc(filt_done, 1)
            pe.wait_ge(ready, 3)
            pe.wait_ge(consts, 4)

            def transposes(src, dst, done, k, by_sequence):
                for t in range(3):
                    o = dst[:, t * P:(t + 1) * P]
                    if by_sequence:
                        o = dst[:, t * T:t * T + P] if t < 2 else dst[:, 0:PAIR_TOK].rearrange("p (b t) -> p b t", b=2)[:, :, P:T]
                    last = pe.transpose(o, src[:, t, k * P:(k + 1) * P], ident[:, :])
                last.then_inc(done, 1)

            def conv_first(q):
                pe.wait_ge(x_loaded[q.s], q.slot_at(64, 64))
                pe.wait_ge(h_taken, q.at(1))
                for b in range(2):
                    for s in range(K_FIRST):
                        pe.matmul(conv_ps[:, b * C:(b + 1) * C], filt[:, s, :], xin[:, q.s, b, s, :],
                                  start=s == 0, stop=s == K_FIRST - 1)

            def conv_rest(q):
                for b in range(2):
                    for s in range(K_REST):
                        last = pe.matmul(conv_ps[:, 2 * C:3 * C], filt_rest[:, s, b, :], xin[:, q.s, b, K_FIRST + s, :],
                                         start=b == 0 and s == 0, stop=b == 1 and s == K_REST - 1)
                last.then_inc(conv_done, 1)

            def project(q):
                pe.wait_ge(o_ready, q.at(2, 2))
                pe.wait_ge(ln2, q.at(N_LN2))
                for t in range(3):
                    for k in range(HC):
                        last = pe.matmul(wo_ps[:, t * C:(t + 1) * C], oT[:, k, t * P:(t + 1) * P], wo[:, k, :], start=k == 0, stop=k == HC - 1)
                last.then_inc(wo_done, 1)

            def kr(q, j):
                pe.wait_ge(kr_taken, q.at(4, max(0, j - 1)))
                m = j % 2
                for k in range(HC):
                    last = pe.matmul(kr_ps[m][:, 0:PAIR_TOK], (wk, wr)[j // 2][:, k, m * P:(m + 1) * P], xnT[:, k, :],
                                     start=k == 0, stop=k == HC - 1)
                last.then_inc(kr_done, 1)

            def body(p0, p1, p2, p3, p4):
                if p0:
                    conv_first(p0)
                if p1:
                    pe.wait_ge(xn_ready, p1.at(3, 3))
                    pe.wait_ge(kr_taken, p1.at(4))
                    for k in range(HC):
                        transposes(xn, kr_ps[k], t1_done, k, True)
                if p3:
                    project(p3)
                if p0:
                    conv_rest(p0)
                if p1:
                    if p1.first():
                        pe.wait_ge(loaded, 16 * 5)
                    pe.wait_ge(t1_taken, p1.at(HC, HC))
                    kr(p1, 0)
                if p4:
                    ranks(p4)
                if p1:
                    kr(p1, 1)
                    kr(p1, 2)
                if p3:
                    pe.wait_ge(xn2_ready, p3.at(3, 3))
                    pe.wait_ge(ln2, p3.at(N_LN2, 1))
                    pe.wait_ge(t2T_taken, p3.at(HC))
                    for k in range(HC):
                        transposes(xs[:, p3.s], x2_ps[k], t2T_done, k, False)
                if p1:
                    kr(p1, 3)
                if p3:
                    pe.wait_ge(t2T_taken, p3.at(HC, HC))
                    pe.wait_ge(route, p3.at(N_ROUTE))
                    for t in range(3):
                        for k in range(HC):
                            last = pe.matmul(cnt_ps[:, t * E:(t + 1) * E], x2T[:, k, t * P:(t + 1) * P], rws[:, k, :],
                                             start=k == 0, stop=k == HC - 1)
                    last.then_inc(lg_done, 1)

            def ranks(q):
                pe.wait_ge(route, q.at(N_ROUTE, 13))
                flat = sel[:, :, :].rearrange("p t e -> p (t e)")
                pe.matmul(rank_ps[:, 2 * E:3 * E], ones[:, :], flat[:, 0:E], start=True, stop=False, skip_group_check=True)
                pe.matmul(rank_ps[:, E:3 * E], ones[:, :], flat[:, 0:2 * E], start=False, stop=False, skip_group_check=True)
                pe.matmul(rank_ps, before[:, :], flat, start=False, stop=True, skip_group_check=True)
                for t in range(3):
                    last = pe.matmul(tot_ps, ones[:, :], sel[:, t, :], start=t == 0, stop=t == 2)
                last.then_inc(rank_done, 1)

            rounds(pe, body)

        @block.vector
        def _(dve):
            dve.wait_ge(iotas, 5)
            dve.tensor_scalar(ident[:, :], diag[:, :], 0.0, None, ALU.is_equal).then_inc(consts, 1)
            dve.tensor_scalar(before[:, :], diag[:, :], 0.0, None, ALU.is_gt).then_inc(consts, 1)
            dve.memset(ones[:, :], 1.0).then_inc(consts, 1)
            dve.memset(wseq[:, :, :], 0.0).then_inc(consts, 1)
            dve.memset(filt_rest[:, :, :, :], 0.0).then_inc(consts, 1)
            dve.tensor_copy(eid[:, :], eid_i[:, :]).then_inc(consts, 1)
            dve.tensor_copy(ends[:, :], reg_i[:, :]).then_inc(consts, 1)
            dve.tensor_copy(tok[:, 0:2], tok_i[:, 0:2]).then_inc(consts, 1)
            dve.tensor_copy(tok[0:REST, 2:3], tok_i[0:REST, 2:3]).then_inc(consts, 1)
            dve.wait_ge(consts, 9)
            dve.tensor_scalar(tok[REST:P, 2:3], tok_i[REST:P, 2:3], float(T - REST), None, ALU.add).then_inc(consts, 1)
            dve.wait_ge(params, 32)
            dve.wait_ge(setup_act, 1)
            dve.tensor_scalar(w[:, :], w[:, :], -1.0, None, ALU.mult).then_inc(consts, 1)
            dve.wait_ge(consts, 11)
            dve.tensor_tensor(uw[:, :], u[:, :], w[:, :], ALU.add).then_inc(consts, 1)
            dve.wait_ge(consts, 12)
            dve.tensor_scalar(nuw[:, :], uw[:, :], -1.0, None, ALU.mult).then_inc(consts, 1)
            dve.wait_ge(filt_done, 1)
            dve.tensor_copy(filt[:, :, :], conv_ps[:, 0:K_FIRST * P].rearrange("p (s t) -> p s t", t=P)).then_inc(ready, 1)
            rest = conv_ps[:, 512:512 + K_REST * REST].rearrange("p (s t) -> p s t", t=REST)
            for b in range(2):
                dve.tensor_copy(filt_rest[:, :, b, b * REST:(b + 1) * REST], rest).then_inc(ready, 1)
            for k in range(HC):
                dve.tensor_scalar(wseq[:, 2 * k:2 * k + 2, :], wseq[:, 2 * k:2 * k + 2, :], w[:, k:k + 1], None, ALU.add).then_inc(consts, 1)
            dve.wait_ge(consts, 15)
            dve.memset(wseq[:, :, 0:1], -3e38).then_inc(consts, 1)
            dve.wait_ge(consts, 16)
            dve.wait_ge(pads, 9)
            dve.wait_ge(loaded, 16 * 5)

            def aggregate(q, st, mv, n, at, done):
                dve.wait_ge(done, q.at(n, at))
                dve.sem_inc(stats_seen, 1)
                for t in range(3):
                    dve.bn_aggr(mv[:, t, :], st[:, t, :]).then_inc(done, 1)

            def flat(a):
                return a[:, :, :].rearrange("p a t -> p (a t)")

            def body(p0, p1, p2, p3, p4):
                def route_to(k):
                    if p4:
                        while routed[0] < k:
                            router[routed[0]](p4)
                            routed[0] += 1

                routed = [0]
                if p2:
                    dve.wait_ge(kr_taken, p2.at(4, 2))
                    dve.wait_ge(diffs, p2.at(N_DIFF))
                    dve.tensor_tensor_scan(flat(pp), flat(wseq), kpad[:, p2.s].rearrange("p a t -> p (a t)"), NEG,
                                           ALU.add, ALU.max).then_inc(diffs, 1)
                route_to(1)
                if p2:
                    dve.wait_ge(clamped, p2.at(4))
                    for k in range(HC):
                        dve.wait_ge(diffs, p2.at(N_DIFF, 1))
                        a = slice(2 * k, 2 * k + 2)
                        dve.scalar_tensor_tensor(out=dl[:, a, :], in0=kpad[:, p2.s, a, 1:TP], scalar=u[:, k:k + 1], in1=pp[:, a, 0:T],
                                                 op0=ALU.add, op1=ALU.subtract).then_inc(diffs, 1)
                        route_to(2 + k)
                if p2:
                    dve.wait_ge(exps, p2.at(4))
                    for k in range(HC):
                        dve.wait_ge(diffs, p2.at(N_DIFF, 2 + k))
                        a = slice(2 * k, 2 * k + 2)
                        dve.tensor_scalar(dn_s[:, a, :], dl[:, a, :], uw[:, k:k + 1], 0.0, ALU.subtract, ALU.min).then_inc(diffs, 1)
                        route_to(4 + k)
                if p3:
                    dve.wait_ge(inv_ready, p3.at(2, 2))
                    dve.wait_ge(wo_done, p3.at(1))
                    for n, (a, o) in enumerate(((slice(0, P), oT[:, :, 0:2 * P]), (slice(P, T), oT[:, :, 2 * P:3 * P]))):
                        dve.tensor_tensor(o.rearrange("p k (b t) -> p k b t", b=2), *(
                            i[:, :].rearrange("p (k b t) -> p k b t", k=HC, b=2)[:, :, :, a] for i in (num, inv)),
                            ALU.mult).then_inc(o_ready, 1)
                        route_to(6 + n)
                route_to(8)
                if p2:
                    dve.wait_ge(exps, p2.at(4, 1))
                    dve.wait_ge(kr_taken, p2.at(4, 4))
                    dve.wait_ge(state, p2.at(N_STATE))
                    dve.tensor_tensor(e2sv[:, :, 1:TP], e2s[:, :, 1:TP], v[:, p2.s], ALU.mult).then_inc(state, 1)
                route_to(9)
                if p2:
                    dve.wait_ge(exps, p2.at(4, 2))
                    dve.wait_ge(t3_done, p2.at(1))
                    dve.tensor_tensor_scan(flat(sb_), flat(e1s), flat(e2s), 0.0, ALU.mult, ALU.add).then_inc(state, 1)
                    route_to(10)
                    dve.wait_ge(state, p2.at(N_STATE, 1))
                    dve.tensor_tensor_scan(flat(sa), flat(e1s), flat(e2sv), 0.0, ALU.mult, ALU.add).then_inc(state, 1)
                route_to(11)
                if p3:
                    dve.wait_ge(wo_done, p3.at(1, 1))
                    dve.wait_ge(h1_stored[p3.s], p3.slot_at(48))
                    dve.wait_ge(xn2_ready, p3.at(3))
                    dve.tensor_tensor(h1[:, p3.s], wo_ps[:, 0:3 * C].rearrange("p (t c) -> p t c", c=C),
                                      h[:, bass.ds(p3.at(3), 3), :], ALU.add).then_inc(ln2, 1)
                    route_to(12)
                    dve.wait_ge(ln2, p3.at(N_LN2, 1))
                    dve.wait_ge(rstd2, p3.at(N_RSTD))
                    for t in range(3):
                        dve.bn_stats(st2[:, t, :], h1[:, p3.s, t, :]).then_inc(ln2, 1)
                        route_to(13 + t)
                    aggregate(p3, st2, mv2, N_LN2, 4, ln2)
                route_to(18)
                if p2:
                    dve.wait_ge(exps, p2.at(4, 4))
                    dve.wait_ge(state, p2.at(N_STATE, 3))
                    dve.tensor_tensor(t1[:, :, :], e1y[:, :, :], sa[:, :, 0:T], ALU.mult).then_inc(state, 1)
                if p0:
                    dve.wait_ge(h_taken, p0.at(1, 1))
                    dve.wait_ge(ln1, p0.at(N_LN1))
                    dve.sem_inc(stats_seen, 1)
                    for t in range(3):
                        dve.bn_stats(st1[:, t, :], tile_of_h(p0, t)).then_inc(ln1, 1)
                        route_to(19 + t)
                    dve.wait_ge(rstd1, p0.at(N_RSTD))
                    aggregate(p0, st1, mv1, N_LN1, 3, ln1)
                route_to(22)
                if p2:
                    dve.wait_ge(t2_done, p2.at(1, 1))
                    dve.wait_ge(state, p2.at(N_STATE, 4))
                    dve.wait_ge(o_ready, p2.at(2))
                    dve.tensor_tensor(num[:, :], flat(t1), flat(t2), ALU.add).then_inc(state, 1)
                    dve.wait_ge(er_ready, p2.at(1, 1))
                    dve.tensor_scalar(er[:, :], er[:, :], EMAX, 1.0, ALU.min, ALU.add).then_inc(state, 1)
                    route_to(23)
                route_to(N_ROUTE)
                if p2:
                    dve.wait_ge(t3_done, p2.at(1, 1))
                    dve.wait_ge(exps, p2.at(4, 3))
                    dve.tensor_tensor(den[:, :], flat(t3), flat(e2y), ALU.add).then_inc(state, 1)
                    dve.wait_ge(state, p2.at(N_STATE, 7))
                    dve.wait_ge(inv_ready, p2.at(2))
                    dve.tensor_tensor(dsg[:, :], den[:, :], er[:, :], ALU.mult).then_inc(state, 1)

            def over_e(a):
                return a.unsqueeze(2).to_broadcast([P, 3, E])

            def over_t(a):
                return a.unsqueeze(1).to_broadcast([P, 3, E])

            def route_step(ins):
                ins.then_inc(route, 1)

            def after(q, k):
                dve.wait_ge(route, q.at(N_ROUTE, k))

            def logits(q):
                dve.wait_ge(lg_done, q.at(1, 1))
                after(q, 0)
                route_step(dve.tensor_tensor(lg[:, :, :], lg_ps, over_t(rbs[:, :]), ALU.add))

            def best(q):
                after(q, 1)
                route_step(dve.tensor_reduce(m1[:, :], lg[:, :, :], AX.X, ALU.max))

            def is_best(q):
                after(q, 2)
                route_step(dve.tensor_tensor(eq[:, :, :], lg[:, :, :], over_e(m1[:, :]), ALU.is_equal))

            def best_numbers(q):
                after(q, 3)
                route_step(dve.scalar_tensor_tensor(out=cand[:, :, :], in0=eq[:, :, :], scalar=-float(E), in1=over_t(eid[:, :]),
                                                    op0=ALU.mult, op1=ALU.add))

            def first_number(q):
                after(q, 4)
                route_step(dve.tensor_reduce(i1[:, :], cand[:, :, :], AX.X, ALU.min))

            def is_first(q):
                after(q, 5)
                route_step(dve.tensor_tensor(oh1[:, :, :], cand[:, :, :], over_e(i1[:, :]), ALU.is_equal))

            def other_logits(q):
                after(q, 6)
                route_step(dve.scalar_tensor_tensor(out=lg2[:, :, :], in0=oh1[:, :, :], scalar=-3e38, in1=lg[:, :, :],
                                                    op0=ALU.mult, op1=ALU.add))

            def second(q):
                after(q, 7)
                route_step(dve.tensor_reduce(m2[:, :], lg2[:, :, :], AX.X, ALU.max))

            def is_second_best(q):
                after(q, 8)
                route_step(dve.tensor_tensor(eq[:, :, :], lg2[:, :, :], over_e(m2[:, :]), ALU.is_equal))

            def second_numbers(q):
                after(q, 9)
                route_step(dve.scalar_tensor_tensor(out=cand2[:, :, :], in0=eq[:, :, :], scalar=-float(E), in1=over_t(eid[:, :]),
                                                    op0=ALU.mult, op1=ALU.add))

            def second_number(q):
                after(q, 10)
                route_step(dve.tensor_reduce(i2[:, :], cand2[:, :, :], AX.X, ALU.min))

            def is_second(q):
                after(q, 11)
                route_step(dve.tensor_tensor(oh2[:, :, :], cand2[:, :, :], over_e(i2[:, :]), ALU.is_equal))

            def selected(q):
                after(q, 12)
                route_step(dve.tensor_tensor(sel[:, :, :], oh1[:, :, :], oh2[:, :, :], ALU.add))

            def difference(q):
                route_step(dve.tensor_tensor(dm[:, :], m2[:, :], m1[:, :], ALU.subtract))

            def first_expert(q):
                dve.wait_ge(rows_stored[q.s], q.slot_at(48))
                route_step(dve.tensor_scalar(xs[:, q.s, :, C + 2], i1[:, :], float(E), None, ALU.add))

            def numbers(q):
                dve.wait_ge(tok_next, q.at(1))
                dve.wait_ge(listed[q.s], q.slot_at(96))
                route_step(dve.tensor_copy(tid[:, q.s, :], tok[:, :]))

            def gate_sum(q):
                dve.wait_ge(gate_exp, q.at(1, 1))
                route_step(dve.tensor_scalar(ed1[:, :], ed[:, :], 1.0, None, ALU.add))

            def places(q):
                dve.wait_ge(rank_done, q.at(1, 1))
                route_step(dve.tensor_tensor(place[:, :, :], rank_ps.rearrange("p (t e) -> p t e", e=E), over_t(ends[:, :]), ALU.add))

            def first_gate(q):
                after(q, 17)
                route_step(dve.reciprocal(xs[:, q.s, :, C], ed1[:, :]))

            def first_places(q):
                after(q, 18)
                route_step(dve.tensor_tensor(pl1[:, :, :], place[:, :, :], oh1[:, :, :], ALU.mult))

            def second_gate(q):
                after(q, 19)
                route_step(dve.tensor_tensor(xs[:, q.s, :, C + 1], ed[:, :], xs[:, q.s, :, C], ALU.mult))

            def second_places(q):
                route_step(dve.tensor_tensor(lg2[:, :, :], place[:, :, :], oh2[:, :, :], ALU.mult))

            def first_place(q):
                after(q, 20)
                with nc.allow_low_precision("whole numbers"):
                    route_step(dve.tensor_reduce(slots[:, q.s, 0:3], pl1[:, :, :], AX.X, ALU.add))

            def second_place(q):
                after(q, 22)
                with nc.allow_low_precision("whole numbers"):
                    route_step(dve.tensor_reduce(slots[:, q.s, 3:6], lg2[:, :, :], AX.X, ALU.add))

            def new_ends(q):
                route_step(dve.tensor_tensor(ends[:, :], tot_ps, ends[:, :], ALU.add))
                after(q, 16)
                dve.tensor_scalar(tok[:, :], tok[:, :], float(PAIR_TOK), None, ALU.add).then_inc(tok_next, 1)

            router = [logits, best, is_best, best_numbers, first_number, is_first, other_logits, second, is_second_best,
                      second_numbers, second_number, is_second, selected, difference, first_expert, numbers, gate_sum,
                      places, first_gate, first_places, second_gate, second_places, first_place, second_place, new_ends]
            assert len(router) == N_ROUTE
            rounds(dve, body)
            dve.wait_ge(route, N_ROUTE * PAIRS)

            def over_tiles(a):
                return a.unsqueeze(1).to_broadcast([P, NC, E])

            def over_experts(a, n=NC):
                return a.unsqueeze(2).to_broadcast([P, n, E])

            steps = [0]

            def step(ins, wait=True):
                steps[0] += 1
                ins.then_inc(tab, 1)
                if wait:
                    dve.wait_ge(tab, steps[0])

            dve.wait_ge(iotas, 9)
            step(dve.tensor_copy(jcol[:, :], jcol_i[:, :]), False)
            step(dve.memset(onesE[:, :], 1.0), False)
            step(dve.tensor_copy(part[:, :], part_i[:, :]))
            step(dve.scalar_tensor_tensor(out=cnt[:, :], in0=e_no[:, :], scalar=-float(REG), in1=ends[:, :], op0=ALU.mult, op1=ALU.add))
            step(dve.tensor_tensor(more[:, :, :], cnt[:, :].unsqueeze(2).to_broadcast([P, E, MAXT]),
                                   lim_i[:, :].unsqueeze(1).to_broadcast([P, E, MAXT]), ALU.is_gt))
            step(dve.tensor_reduce(nts[:, :], more[:, :, :], AX.X, ALU.add))
            step(dve.tensor_tensor_scan(ends_t[:, :], onesE[:, :], nts[:, :], 0.0, ALU.mult, ALU.add))
            step(dve.tensor_tensor(start_t[:, :], ends_t[:, :], nts[:, :], ALU.subtract))
            step(dve.tensor_scalar(grp_e[:, :], e_no[:, :], float(REG // R), None, ALU.mult))
            step(dve.scalar_tensor_tensor(out=grp_e[:, :], in0=start_t[:, :], scalar=-float(P), in1=grp_e[:, :], op0=ALU.mult, op1=ALU.add))
            step(dve.tensor_tensor(past[:, :, :], over_experts(jcol[:, :]), over_tiles(ends_t[:, :]), ALU.is_ge))
            step(dve.tensor_reduce(ej[:, :], past[:, :, :], AX.X, ALU.add))
            step(dve.tensor_tensor(oh[:, :, :], over_tiles(e_no[:, :]), over_experts(ej[:, :]), ALU.is_equal))
            step(dve.tensor_tensor(pick[:, :, :], oh[:, :, :], over_tiles(grp_e[:, :]), ALU.mult))
            step(dve.tensor_reduce(grp[:, :], pick[:, :, :], AX.X, ALU.add))
            step(dve.scalar_tensor_tensor(out=grp[:, :], in0=jcol[:, :], scalar=float(P), in1=grp[:, :], op0=ALU.mult, op1=ALU.add))
            step(dve.tensor_scalar(live[:, :], ej[:, :], float(E), None, ALU.is_lt))
            step(dve.tensor_scalar(idx_f[:, :], grp[:, :], part[:, R:R + 1], -float(NOGRP), ALU.add, ALU.add))
            step(dve.tensor_tensor(idx_f[:, :], idx_f[:, :], live[:, :], ALU.mult))
            step(dve.tensor_scalar(table[:, :, 1], idx_f[:, :], float(NOGRP), None, ALU.add))
            step(dve.tensor_scalar(ecl[:, :], ej[:, :], float(E - 1), None, ALU.min))
            step(dve.tensor_copy(table[:, :, 2], ecl[:, :]))
            step(dve.tensor_scalar(table[:, :, 0], ecl[:, :], float(P), part[:, R:R + 1], ALU.mult, ALU.add))




def tiles(eng, first, body, last):
    first()
    for s in range(2):
        body(Pair(0, s))
    with eng.Fori(1, (NT - 1) // 2) as n:
        for s in range(2):
            body(Pair(n, s))
    if NT % 2 == 0:
        body(Pair(NT // 2 - 1, 0))
    last(Pair((NT - 1) // 2, (NT - 1) % 2))


def experts(nc, ew, b2, out, rows, lists, tables):
    ctx = ExitStack()

    def sb(name, shape, dt=F32):
        return ctx.enter_context(nc.sbuf_tensor(name, shape, dt))

    def ps(name):
        return ctx.enter_context(nc.psum_tensor(name, [P, 512], F32))

    def sem(name):
        return ctx.enter_context(nc.semaphore(name))

    with ctx:
        idx = sb("idx", [P, 2, 3], U32)
        raw = sb("raw", [P, 2, WROW])
        whi, wlo = sb("whi", [P, 2, B1AT], F32R), sb("wlo", [P, 2, B1AT], F32R)
        b1, b2s = sb("b1", [P, 2, FC]), sb("b2s", [P, 2, C])
        tid = sb("tid2", [P, 2, R], U32)
        xg = sb("xg", [P, 2, R, ROW])
        xhi, xlo = sb("xhi", [P, 2, HC, TS], F32R), sb("xlo", [P, 2, HC, TS], F32R)
        hid = sb("hid", [P, 2, TS])
        hhi, hlo = sb("hhi", [P, 4, TS], F32R), sb("hlo", [P, 4, TS], F32R)
        ysum, yout = sb("ysum", [P, 2, R, C]), sb("yout", [P, 2, R, C])
        tk, tk2, gA, gB = (sb(n, [P, R]) for n in ("tk", "tk2", "gA", "gB"))
        gate, dest = sb("gate", [P, 2, R]), sb("dest", [P, 2, R], U32)

        acc = [ps(f"acc{i}") for i in range(R)]
        hp = [ps("hp0"), ps("hp1")]
        xt = [ps("xt0"), ps("xt1")]

        idx_ready, waits_over = sem("idx_ready"), sem("waits_over")
        w_in, tid_in, x_in, b2_in, y_sent = ([sem(f"{n}{s}") for s in range(2)] for n in ("w_in", "tid_in", "x_in", "b2_in", "y_sent"))
        xt_done, xhi_done, xlo_done = sem("xt_done"), sem("xhi_done"), sem("xlo_done")
        whi_done, wlo_done, b1_done = sem("whi_done"), sem("wlo_done"), sem("b1_done")
        hp_done, hid_done, hhi_done, hlo_done = sem("hp_done"), sem("hid_done"), sem("hhi_done"), sem("hlo_done")
        acc_done, y_taken, y_ready, marks = sem("acc_done"), sem("y_taken"), sem("y_ready"), sem("marks")
        N_MARK = 6
        PIECE = B1AT // FC
        ej, part, table, ident = tables.ej, tables.part, tables.table, tables.ident

        block = ctx.enter_context(nc.Block())

        def nxt(j):
            return Pair(j.g, 1) if j.s == 0 else Pair(j.g + 1, 0)

        def prev(j):
            return Pair(j.g - 1, 1) if j.s == 0 else Pair(j.g, 0)

        @block.gpsimd
        def _(pool):
            groups = lists.rearrange("(g r) a -> g (r a)", r=R)

            def end_of_waits():
                pool.sem_inc(waits_over, 1)

            def gather_w(j):
                pool.indirect_dma_start(raw[:, j.s, :], None, ew, bass.IndirectOffsetOnAxis(idx[:, j.s, 0:1], 0)).then_inc(w_in[j.s], 16)

            def gather_tid(j):
                pool.indirect_dma_start(tid[:, j.s, :], None, groups, bass.IndirectOffsetOnAxis(idx[:, j.s, 1:2], 0)).then_inc(tid_in[j.s], 16)

            def gather_x(j):
                pool.wait_ge(tid_in[j.s], j.slot_at(16, 16))
                end_of_waits()
                for r in range(R):
                    pool.indirect_dma_start(xg[:, j.s, r, :], None, rows,
                                            bass.IndirectOffsetOnAxis(tid[:, j.s, r:r + 1], 0)).then_inc(x_in[j.s], 16)

            def gather_b2(j):
                pool.indirect_dma_start(b2s[:, j.s, :], None, b2, bass.IndirectOffsetOnAxis(idx[:, j.s, 2:3], 0)).then_inc(b2_in[j.s], 16)

            def first():
                pool.wait_ge(idx_ready, 1)
                gather_tid(Pair(0, 0))
                gather_w(Pair(0, 0))
                gather_x(Pair(0, 0))
                pool.wait_ge(idx_ready, 2)
                gather_tid(Pair(0, 1))
                gather_b2(Pair(0, 0))
                gather_w(Pair(0, 1))
                gather_x(Pair(0, 1))

            def body(j):
                after = Pair(j.g + 1, j.s)
                pool.wait_ge(idx_ready, after.at(1, 1))
                pool.wait_ge(wlo_done, j.at(FC, FC))
                pool.wait_ge(b1_done, j.at(1, 1))
                pool.wait_ge(marks, j.at(N_MARK, N_MARK))
                pool.wait_ge(x_in[j.s], j.slot_at(16 * R, 16 * R))
                end_of_waits()
                gather_w(after)
                gather_tid(after)
                pool.wait_ge(y_taken, j.at(R))
                end_of_waits()
                gather_b2(nxt(j))
                pool.wait_ge(xt_done, j.at(HC, HC))
                if not j.first():
                    send(prev(j))
                gather_x(after)

            def send(j):
                pool.wait_ge(y_ready, j.at(R, R))
                if not j.first():
                    pool.wait_ge(y_sent[1 - j.s], prev(j).slot_at(16 * R, 16 * R))
                end_of_waits()
                for r in range(R):
                    pool.indirect_dma_start(out[:, :], bass.IndirectOffsetOnAxis(dest[:, j.s, r:r + 1], 0),
                                            yout[:, j.s, r, :], None, compute_op=ALU.add).then_inc(y_sent[j.s], 16)

            def last(j):
                send(prev(j))
                send(j)
                pool.wait_ge(y_sent[j.s], j.slot_at(16 * R, 16 * R))
                pool.wait_ge(w_in[1 - j.s], 16 * (NC // 2))
                pool.wait_ge(tid_in[1 - j.s], 16 * (NC // 2))
                pool.wait_ge(x_in[1 - j.s], 16 * R * (NC // 2))

            tiles(pool, first, body, last)

        @block.scalar
        def _(act):
            def x_high(j, k):
                act.wait_ge(xt_done, j.at(HC, k + 1))
                act.activation(xhi[:, j.s, k, :], xt[k][:, 0:TS], ACT.Copy).then_inc(xhi_done, 1)

            def w_high(j, k):
                act.activation(whi[:, j.s, k * PIECE:(k + 1) * PIECE], raw[:, j.s, k * PIECE:(k + 1) * PIECE], ACT.Copy).then_inc(whi_done, 1)

            def first():
                act.wait_ge(w_in[0], 16)
                for k in range(FC):
                    w_high(Pair(0, 0), k)
                    if k in (3, 4):
                        x_high(Pair(0, 0), k - 3)

            def gated(j):
                for r in range(R):
                    act.wait_ge(y_taken, j.at(R, r + 1))
                    act.wait_ge(marks, j.at(N_MARK, N_MARK))
                    act.wait_ge(y_sent[j.s], j.slot_at(16 * R))
                    act.activation(yout[:, j.s, r, :], ysum[:, j.s, r, :], ACT.Copy, scale=gate[:, j.s, r:r + 1]).then_inc(y_ready, 1)

            def body(j, more=True):
                n = nxt(j)
                for c in range(FC):
                    act.wait_ge(hp_done, j.at(FC, c + 1))
                    if c < 2:
                        act.wait_ge(hlo_done, j.at(FC))
                        act.wait_ge(b1_done, j.at(1, 1))
                    else:
                        act.wait_ge(hlo_done, j.at(FC, c - 1))
                    act.activation(hid[:, c % 2, :], hp[c % 2][:, 0:TS], ACT.Relu, bias=b1[:, j.s, c:c + 1]).then_inc(hid_done, 1)
                    if c == 1 and not j.first():
                        gated(prev(j))
                    if more:
                        if c == 0:
                            act.wait_ge(w_in[n.s], n.slot_at(16, 16))
                            act.wait_ge(acc_done, j.at(1))
                        w_high(n, c)
                        if c in (5, 6):
                            x_high(n, c - 5)
                if not more:
                    gated(j)

            tiles(act, first, body, lambda j: body(j, False))

        @block.tensor
        def _(pe):
            def transposes(j):
                pe.wait_ge(x_in[j.s], j.slot_at(16 * R, 16 * R))
                pe.wait_ge(xlo_done, j.at(HC))
                for k in range(HC):
                    for r in range(R):
                        last = pe.transpose(xt[k][:, r * P:(r + 1) * P], xg[:, j.s, r, k * P:(k + 1) * P], ident[:, :])
                    last.then_inc(xt_done, 1)

            def up(j, c):
                pe.wait_ge(hid_done, j.at(FC, max(0, c - 1)))
                n = 0
                for k in range(HC):
                    at = k * FF + c * P
                    for w_, x_ in ((whi, xhi), (wlo, xhi), (whi, xlo)):
                        last = pe.matmul(hp[c % 2][:, 0:TS], w_[:, j.s, at:at + P], x_[:, j.s, k, :], start=n == 0, stop=n == 3 * HC - 1)
                        n += 1
                last.then_inc(hp_done, 1)

            def down(j, c):
                pe.wait_ge(hlo_done, j.at(FC, c + 1))
                if c == 0:
                    pe.wait_ge(y_taken, j.at(R))
                at = W2AT + c * C
                for r in range(R):
                    for n, (h_, w_) in enumerate(((hhi, whi), (hhi, wlo), (hlo, whi))):
                        last = pe.matmul(acc[r][:, 0:C], h_[:, c % 4, r * P:(r + 1) * P], w_[:, j.s, at:at + C],
                                         start=c == 0 and n == 0, stop=c == FC - 1 and n == 2)
                return last

            def first_weights(c):
                w1 = ((HC - 1) * FF + (c + 1) * P - 1) // PIECE + 1
                w2 = (W2AT + (c - 1) * C - 1) // PIECE + 1
                return max(w1, w2)

            def body(j, more=True):
                if not j.first():
                    pe.wait_ge(wlo_done, j.at(FC, FC))
                pe.wait_ge(xlo_done, j.at(HC, HC))
                for c in range(FC):
                    if j.first():
                        pe.wait_ge(wlo_done, first_weights(c))
                    up(j, c)
                    if c >= 2:
                        down(j, c - 2)
                    if c == 4 and more:
                        transposes(nxt(j))
                if j.first():
                    pe.wait_ge(wlo_done, FC)
                down(j, FC - 2)
                down(j, FC - 1).then_inc(acc_done, 1)

            tiles(pe, lambda: transposes(Pair(0, 0)), body, lambda j: body(j, False))

        @block.vector
        def _(dve):
            def indices(j):
                dve.tensor_copy(idx[:, j.s, :].unsqueeze(1), table[:, bass.ds(j.at(1), 1), :]).then_inc(idx_ready, 1)

            def w_low(j, k):
                a = slice(k * PIECE, (k + 1) * PIECE)
                dve.wait_ge(whi_done, j.at(FC, k + 1))
                dve.tensor_tensor(wlo[:, j.s, a], raw[:, j.s, a], whi[:, j.s, a].bitcast(F32), ALU.subtract).then_inc(wlo_done, 1)

            def x_low(j, k):
                dve.wait_ge(xhi_done, j.at(HC, k + 1))
                dve.tensor_tensor(xlo[:, j.s, k, :], xt[k][:, 0:TS], xhi[:, j.s, k, :].bitcast(F32), ALU.subtract).then_inc(xlo_done, 1)

            def bias(j):
                dve.tensor_copy(b1[:, j.s, :], raw[:, j.s, B1AT:WROW]).then_inc(b1_done, 1)

            def mark(j):
                def after(k):
                    dve.wait_ge(marks, j.at(N_MARK, k))

                e_j = ej[:, bass.ds(j.at(1), 1)]
                dve.wait_ge(tid_in[j.s], j.slot_at(16, 16))
                dve.wait_ge(x_in[j.s], j.slot_at(16 * R, 16 * R))
                after(0)
                dve.scalar_tensor_tensor(out=tk[:, :], in0=tid[:, j.s, :], scalar=-float(NTOK), in1=part[:, 0:R],
                                         op0=ALU.add, op1=ALU.subtract).then_inc(marks, 1)
                dve.scalar_tensor_tensor(out=gA[:, :], in0=xg[:, j.s, :, C + 2], scalar=e_j, in1=xg[:, j.s, :, C],
                                         op0=ALU.is_equal, op1=ALU.mult).then_inc(marks, 1)
                dve.scalar_tensor_tensor(out=gB[:, :], in0=xg[:, j.s, :, C + 2], scalar=e_j, in1=xg[:, j.s, :, C + 1],
                                         op0=ALU.not_equal, op1=ALU.mult).then_inc(marks, 1)
                after(1)
                dve.scalar_tensor_tensor(out=tk2[:, :], in0=tid[:, j.s, :], scalar=float(NTOK), in1=tk[:, :],
                                         op0=ALU.is_lt, op1=ALU.mult).then_inc(marks, 1)
                after(3)
                dve.tensor_tensor(gate[:, j.s, :], gA[:, :], gB[:, :], ALU.add).then_inc(marks, 1)
                after(4)
                dve.scalar_tensor_tensor(out=dest[:, j.s, :], in0=tk2[:, :], scalar=float(NTOK), in1=part[:, 0:R],
                                         op0=ALU.add, op1=ALU.add).then_inc(marks, 1)

            def first():
                indices(Pair(0, 0))
                indices(Pair(0, 1))
                dve.wait_ge(w_in[0], 16)
                bias(Pair(0, 0))
                for k in range(FC):
                    w_low(Pair(0, 0), k)
                    if k in (3, 4):
                        x_low(Pair(0, 0), k - 3)
                mark(Pair(0, 0))

            def body(j, more=True):
                n = nxt(j)
                for c in range(FC):
                    dve.wait_ge(hid_done, j.at(FC, c + 1))
                    if c < 4:
                        dve.wait_ge(acc_done, j.at(1))
                    else:
                        dve.wait_ge(hp_done, j.at(FC, c - 1))
                    dve.tensor_copy(hhi[:, c % 4, :], hid[:, c % 2, :]).then_inc(hhi_done, 1)
                    dve.wait_ge(hhi_done, j.at(FC, c + 1))
                    dve.tensor_tensor(hlo[:, c % 4, :], hid[:, c % 2, :], hhi[:, c % 4, :].bitcast(F32), ALU.subtract).then_inc(hlo_done, 1)
                    if more:
                        if c == 0:
                            dve.wait_ge(w_in[n.s], n.slot_at(16, 16))
                            bias(n)
                        w_low(n, c)
                        if c == 1:
                            dve.wait_ge(w_in[j.s], j.slot_at(16, 16))
                            dve.wait_ge(tid_in[j.s], j.slot_at(16, 16))
                            dve.wait_ge(b2_in[j.s], j.slot_at(16, 16))
                            indices(Pair(j.g + 1, j.s))
                        if c in (6, 7):
                            x_low(n, c - 6)
                        if c == 7:
                            if not j.first():
                                dve.wait_ge(y_ready, j.at(R))
                                dve.wait_ge(y_sent[n.s], prev(j).slot_at(16 * R, 16 * R))
                            mark(n)
                dve.wait_ge(acc_done, j.at(1, 1))
                dve.wait_ge(b2_in[j.s], j.slot_at(16, 16))
                dve.wait_ge(y_ready, prev(j).at(R) if not j.first() else 0)
                for r in range(R):
                    dve.tensor_tensor(ysum[:, j.s, r, :], acc[r][:, 0:C], b2s[:, j.s, :], ALU.add).then_inc(y_taken, 1)

            tiles(dve, first, body, lambda j: body(j, False))


def audio_tower(nc, x, taps, taps_down, wkT, wrT, woT, decay, first, rw, rb, ew, b2, out):
    rows = nc.dram_tensor("token_rows", (NTOK + 1, ROW), F32, kind="Internal").ap()
    lists = nc.dram_tensor("expert_lists", (LIST, 1), U32, kind="Internal").ap()
    with ExitStack() as ctx:
        tables = Tables(nc, ctx)
        tokens_to_experts(nc, x, taps, taps_down, wkT, wrT, woT, decay, first, rw, rb, out, rows, lists, tables)
        experts(nc, ew, b2, out, rows, lists, tables)


def kernel(x, L0_tok_h0, L0_attn_Wk, L0_attn_Wr, L0_attn_Wo, L0_attn_time_decay, L0_attn_time_first,
           L0_ffn_router_w, L0_ffn_router_b, L0_ffn_W1, L0_ffn_b1, L0_ffn_W2, L0_ffn_b2):
    import numpy as np
    import concourse.bacc as bacc
    from concourse.bass_utils import run_bass_kernel_spmd

    def arr(a):
        return np.asarray(a)

    w1 = arr(L0_ffn_W1).reshape(E, HC, P, FF).transpose(0, 2, 1, 3).reshape(E, P, HC * FF)
    w2 = arr(L0_ffn_W2).reshape(E, FC, P, C).transpose(0, 2, 1, 3).reshape(E, P, FC * C)
    b1 = arr(L0_ffn_b1).reshape(E, FC, P).transpose(0, 2, 1)
    ins = {
        "x": arr(x),
        "taps": np.pad(arr(L0_tok_h0), (TAP0, ROW1 - TAP0 - TAPS)),
        "taps_down": np.pad(arr(L0_tok_h0)[::-1], (TAPR - TAPS + 1, ROW2 - TAPR - 1)),
        "wkT": arr(L0_attn_Wk).T, "wrT": arr(L0_attn_Wr).T, "woT": arr(L0_attn_Wo).T,
        "decay": arr(L0_attn_time_decay).reshape(HC, P).T, "first": arr(L0_attn_time_first).reshape(HC, P).T,
        "rw": arr(L0_ffn_router_w), "rb": arr(L0_ffn_router_b),
        "ew": np.concatenate([w1, w2, b1], axis=2).reshape(E * P, WROW), "b2": arr(L0_ffn_b2),
    }
    nc = bacc.Bacc("TRN2", target_bir_lowering=False, num_devices=1)
    arrays, args = {}, {}
    for name, a in ins.items():
        arrays[f"in_{name}"] = np.ascontiguousarray(a)
        args[name] = nc.dram_tensor(f"in_{name}", a.shape, mybir.dt.from_np(a.dtype), kind="ExternalInput").ap()
    out = nc.dram_tensor("out_rows", (NTOK + TS, C), F32, kind="ExternalOutput").ap()
    audio_tower(nc, **args, out=out)
    r = run_bass_kernel_spmd(nc, [arrays], core_ids=[0])
    return r.results[0]["out_rows"][0:NTOK].reshape(B, T, C)
```
